# Optimizing a Trainium2 kernel written in Bass

```python
import numpy as np
import jax
import jax.numpy as jnp

def _softmax(x, axis=-1):
    return jax.nn.softmax(x, axis=axis)

def _gelu(x):
    return jax.nn.gelu(x, approximate=True)

def _silu(x):
    return jax.nn.silu(x)

def _sigmoid(x):
    return jax.nn.sigmoid(x)

def _layernorm(x, axis=-1, eps=1e-05):
    m = jnp.mean(x, axis=axis, keepdims=True)
    v = jnp.var(x, axis=axis, keepdims=True)
    return (x - m) / jnp.sqrt(v + eps)

def _scatter_add(tgt, idx, src, axis=0):
    return tgt.at[idx].add(src)

def _segment_sum(src, seg, n):
    return jax.ops.segment_sum(src, seg, n)
kernel_name = 'mk_vit_tower_d2_tok_img1024_r4_970293'

def setup_inputs(seed: int=0):
    np.random.seed(seed)
    _w = jnp.asarray

    def _rec_inputs():
        import jax
        import jax.numpy as jnp
        _rk = jax.random.key(seed)
        x = -0.00016672 + 0.999947 * jax.random.normal(jax.random.fold_in(_rk, 1), (16, 3, 96, 96), jnp.float32)
        return x
    x = _rec_inputs()

    def _L0_tok_setup():
        import jax, jax.numpy as jnp
        import numpy as np
        B, C, H, W = (64, 3, 96, 96)
        P = 16
        HP, WP = (H // P, W // P)
        N = HP * WP
        F = C * P * P
        D = 256
        key = jax.random.key(seed)
        k1, k2, k3, k4, k5 = jax.random.split(key, 5)
        data = jax.random.normal(k1, (B, C, H, W), dtype=jnp.float32)
        lim = 1.0 / np.sqrt(F)
        W_lin = jax.random.uniform(k2, (D, F), minval=-lim, maxval=lim, dtype=jnp.float32)
        b_lin = jax.random.uniform(k3, (D,), minval=-lim, maxval=lim, dtype=jnp.float32)
        class_token = jax.random.normal(k4, (1, 1, D), dtype=jnp.float32)
        position_embeddings = jax.random.normal(k5, (1, N + 1, D), dtype=jnp.float32)
        return {'data': data, 'W_lin': W_lin, 'b_lin': b_lin, 'class_token': class_token, 'position_embeddings': position_embeddings}
    _L0_tok_all = _L0_tok_setup()
    _L0_tok_in = {k: v for k, v in _L0_tok_all.items() if k in ('W_lin', 'b_lin', 'class_token', 'position_embeddings')}
    del _L0_tok_all

    def _L0_attn_setup():
        import jax, jax.numpy as jnp
        import numpy as np
        B, S, HID, NH = (8, 1024, 256, 16)
        D = HID // NH
        LN_EPS = 1e-05

        def _l2norm(a):
            n = jnp.sqrt(jnp.sum(a * a, axis=-1, keepdims=True))
            return a / jnp.maximum(n, 1e-12)
        key = jax.random.key(seed)
        ks = jax.random.split(key, 8)
        s = 0.02
        x = jax.random.normal(ks[0], (B, S, HID), jnp.float32)
        Wq = jax.random.normal(ks[1], (HID, NH * D), jnp.float32) * s
        Wk = jax.random.normal(ks[2], (HID, NH * D), jnp.float32) * s
        Wv = jax.random.normal(ks[3], (HID, NH * D), jnp.float32) * s
        Wbeta = jax.random.normal(ks[4], (HID, NH), jnp.float32) * s
        Wg = jax.random.normal(ks[5], (HID, NH * D), jnp.float32) * s
        Wout = jax.random.normal(ks[6], (NH * D, HID), jnp.float32) * s
        ln_g = jnp.ones((NH * D,), jnp.float32)
        ln_b = jnp.zeros((NH * D,), jnp.float32)
        return {'x': x, 'Wq': Wq, 'Wk': Wk, 'Wv': Wv, 'Wbeta': Wbeta, 'Wg': Wg, 'Wout': Wout, 'ln_g': ln_g, 'ln_b': ln_b}
    _L0_attn_all = _L0_attn_setup()
    _L0_attn_in = {k: v for k, v in _L0_attn_all.items() if k in ('Wq', 'Wk', 'Wv', 'Wbeta', 'Wg', 'Wout', 'ln_g', 'ln_b')}
    del _L0_attn_all

    def _L0_ffn_setup():
        import jax, jax.numpy as jnp
        import numpy as np
        TOP_K = 2
        key = jax.random.key(seed)
        k1, k2, k3, k4, k5 = jax.random.split(key, 5)
        B, S, D, F, E = (2, 256, 256, 512, 8)
        return {'x': jax.random.normal(k1, (B, S, D), dtype=jnp.float32), 'router_kernel_DE': jax.random.normal(k2, (D, E), dtype=jnp.float32) * 0.02, 'kernel_gating_EDF': jax.random.normal(k3, (E, D, F), dtype=jnp.float32) * 0.02, 'kernel_up_EDF': jax.random.normal(k4, (E, D, F), dtype=jnp.float32) * 0.02, 'kernel_down_EFD': jax.random.normal(k5, (E, F, D), dtype=jnp.float32) * 0.02}
    _L0_ffn_all = _L0_ffn_setup()
    _L0_ffn_in = {k: v for k, v in _L0_ffn_all.items() if k in ('router_kernel_DE', 'kernel_gating_EDF', 'kernel_up_EDF', 'kernel_down_EFD')}
    del _L0_ffn_all

    def _L1_attn_setup():
        import jax, jax.numpy as jnp
        import numpy as np
        from jax import lax
        DIM = 256
        E = DIM
        K = 4
        B, T = (4, 1024)

        def _hawk_forward(x, w_in, w_conv, b_conv, w_gates, b_gates, forget_base, w_out):
            proj = jnp.einsum('btc,ec->bte', x, w_in)
            gate, xa = jnp.split(proj, 2, axis=-1)
            k = w_conv.shape[-1]
            xc = lax.conv_general_dilated(xa.transpose(0, 2, 1), w_conv, window_strides=(1,), padding=[(k - 1, 0)], feature_group_count=w_conv.shape[0], dimension_numbers=('NCH', 'OIH', 'NCH'))
            xc = (xc + b_conv[None, :, None]).transpose(0, 2, 1)
            g = jnp.einsum('bte,fe->btf', xc, w_gates) + b_gates
            forget, inp = jnp.split(g, 2, axis=-1)
            alpha = jnp.exp(-8.0 * jax.nn.softplus(forget_base) * jax.nn.sigmoid(forget))
            beta = jnp.sqrt(1.0 - alpha ** 2 + 1e-06)
            u = beta * jax.nn.sigmoid(inp) * xc

            def combine(c1, c2):
                a1, b1 = c1
                a2, b2 = c2
                return (a1 * a2, a2 * b1 + b2)
            _, h = lax.associative_scan(combine, (alpha, u), axis=1)
            y = jax.nn.gelu(gate, approximate=False) * h
            return jnp.einsum('bte,ce->btc', y, w_out)
        key = jax.random.key(seed)
        ks = jax.random.split(key, 8)
        x = jax.random.normal(ks[0], (B, T, DIM), dtype=jnp.float32)
        w_in = jax.random.normal(ks[1], (2 * E, DIM), dtype=jnp.float32) * DIM ** (-0.5)
        w_conv = jax.random.normal(ks[2], (E, 1, K), dtype=jnp.float32) * (1.0 / K) ** 0.5
        b_conv = jax.random.normal(ks[3], (E,), dtype=jnp.float32) * 0.02
        w_gates = jax.random.normal(ks[4], (2 * E, E), dtype=jnp.float32) * E ** (-0.5)
        b_gates = jnp.zeros((2 * E,), dtype=jnp.float32)
        forget_base = jnp.linspace(-4.323, -9.0, E, dtype=jnp.float32)
        w_out = jax.random.normal(ks[5], (DIM, E), dtype=jnp.float32) * E ** (-0.5)
        return {'x': x, 'w_in': w_in, 'w_conv': w_conv, 'b_conv': b_conv, 'w_gates': w_gates, 'b_gates': b_gates, 'forget_base': forget_base, 'w_out': w_out}
    _L1_attn_all = _L1_attn_setup()
    _L1_attn_in = {k: v for k, v in _L1_attn_all.items() if k in ('w_in', 'w_conv', 'b_conv', 'w_gates', 'b_gates', 'forget_base', 'w_out')}
    del _L1_attn_all

    def _L1_ffn_setup():
        import jax, jax.numpy as jnp
        import numpy as np
        EPS = 1e-05
        key = jax.random.key(seed)
        kx, kw, kb = jax.random.split(key, 3)
        B, S, K, N = (8, 2048, 256, 256)
        x = jax.random.normal(kx, (B, S, K), dtype=jnp.float32)
        W = jax.random.normal(kw, (N, K), dtype=jnp.float32) * 0.02
        weight_scale = jnp.maximum(jnp.max(jnp.abs(W), axis=1, keepdims=True) / 127.0, EPS)
        weight_int8 = jnp.clip(jnp.round(W / weight_scale), -128, 127).astype(jnp.int8)
        bias = jax.random.normal(kb, (N,), dtype=jnp.float32) * 0.01
        return {'x': x, 'weight_int8': weight_int8, 'weight_scale': weight_scale, 'bias': bias}
    _L1_ffn_all = _L1_ffn_setup()
    _L1_ffn_in = {k: v for k, v in _L1_ffn_all.items() if k in ('weight_int8', 'weight_scale', 'bias')}
    del _L1_ffn_all
    return {'x': x, 'L0_tok_W_lin': _L0_tok_in['W_lin'], 'L0_tok_b_lin': _L0_tok_in['b_lin'], 'L0_tok_class_token': _L0_tok_in['class_token'], 'L0_tok_position_embeddings': _L0_tok_in['position_embeddings'], 'L0_attn_Wq': _L0_attn_in['Wq'], 'L0_attn_Wk': _L0_attn_in['Wk'], 'L0_attn_Wv': _L0_attn_in['Wv'], 'L0_attn_Wbeta': _L0_attn_in['Wbeta'], 'L0_attn_Wg': _L0_attn_in['Wg'], 'L0_attn_Wout': _L0_attn_in['Wout'], 'L0_attn_ln_g': _L0_attn_in['ln_g'], 'L0_attn_ln_b': _L0_attn_in['ln_b'], 'L0_ffn_router_kernel_DE': _L0_ffn_in['router_kernel_DE'], 'L0_ffn_kernel_gating_EDF': _L0_ffn_in['kernel_gating_EDF'], 'L0_ffn_kernel_up_EDF': _L0_ffn_in['kernel_up_EDF'], 'L0_ffn_kernel_down_EFD': _L0_ffn_in['kernel_down_EFD'], 'L1_attn_w_in': _L1_attn_in['w_in'], 'L1_attn_w_conv': _L1_attn_in['w_conv'], 'L1_attn_b_conv': _L1_attn_in['b_conv'], 'L1_attn_w_gates': _L1_attn_in['w_gates'], 'L1_attn_b_gates': _L1_attn_in['b_gates'], 'L1_attn_forget_base': _L1_attn_in['forget_base'], 'L1_attn_w_out': _L1_attn_in['w_out'], 'L1_ffn_weight_int8': _L1_ffn_in['weight_int8'], 'L1_ffn_weight_scale': _L1_ffn_in['weight_scale'], 'L1_ffn_bias': _L1_ffn_in['bias']}

def reference(x, L0_tok_W_lin, L0_tok_b_lin, L0_tok_class_token, L0_tok_position_embeddings, L0_attn_Wq, L0_attn_Wk, L0_attn_Wv, L0_attn_Wbeta, L0_attn_Wg, L0_attn_Wout, L0_attn_ln_g, L0_attn_ln_b, L0_ffn_router_kernel_DE, L0_ffn_kernel_gating_EDF, L0_ffn_kernel_up_EDF, L0_ffn_kernel_down_EFD, L1_attn_w_in, L1_attn_w_conv, L1_attn_b_conv, L1_attn_w_gates, L1_attn_b_gates, L1_attn_forget_base, L1_attn_w_out, L1_ffn_weight_int8, L1_ffn_weight_scale, L1_ffn_bias):
    import jax
    import jax.numpy as jnp

    def _L0_tok_ref(data, W_lin, b_lin, class_token, position_embeddings):
        import jax, jax.numpy as jnp
        import numpy as np
        B, C, H, W = (64, 3, 96, 96)
        P = 16
        HP, WP = (H // P, W // P)
        N = HP * WP
        F = C * P * P
        D = 256
        b = data.shape[0]
        x = data.reshape(b, C, HP, P, WP, P)
        x = x.transpose(0, 2, 4, 1, 3, 5).reshape(b, N, F)
        x = jnp.einsum('bnf,df->bnd', x, W_lin) + b_lin
        cls = jnp.broadcast_to(class_token, (b, 1, D))
        out = jnp.concatenate([cls, x], axis=1) + position_embeddings
        return out

    def _L0_attn_ref(x, Wq, Wk, Wv, Wbeta, Wg, Wout, ln_g, ln_b):
        import jax, jax.numpy as jnp
        import numpy as np
        B, S, HID, NH = (8, 1024, 256, 16)
        D = HID // NH
        LN_EPS = 1e-05

        def _l2norm(a):
            n = jnp.sqrt(jnp.sum(a * a, axis=-1, keepdims=True))
            return a / jnp.maximum(n, 1e-12)
        b, s, _ = x.shape
        nh = Wbeta.shape[1]
        d = Wq.shape[1] // nh
        q = _l2norm((x @ Wq).reshape(b, s, nh, d))
        k = _l2norm((x @ Wk).reshape(b, s, nh, d))
        v = (x @ Wv).reshape(b, s, nh, d)
        beta = jax.nn.sigmoid(x @ Wbeta)
        qT = jnp.moveaxis(q, 1, 0)
        kT = jnp.moveaxis(k, 1, 0)
        vT = jnp.moveaxis(v, 1, 0)
        bT = jnp.moveaxis(beta, 1, 0)
        state0 = jnp.zeros((b, nh, d, d), x.dtype)

        def step(state, inp):
            qt, kt, vt, bt = inp
            kk = kt[..., :, None] * kt[..., None, :]
            bb = bt[..., None, None]
            state = state * (1.0 - bb * kk) + bb * (vt[..., :, None] * kt[..., None, :])
            out_t = jnp.einsum('bhij,bhj->bhi', state, qt)
            return (state, out_t)
        _, outs = jax.lax.scan(step, state0, (qT, kT, vT, bT))
        out = jnp.moveaxis(outs, 0, 1).reshape(b, s, nh * d)
        mu = jnp.mean(out, axis=-1, keepdims=True)
        var = jnp.mean((out - mu) ** 2, axis=-1, keepdims=True)
        out = (out - mu) / jnp.sqrt(var + LN_EPS) * ln_g + ln_b
        out = out * jax.nn.silu(x @ Wg)
        return out @ Wout

    def _L0_ffn_ref(x, router_kernel_DE, kernel_gating_EDF, kernel_up_EDF, kernel_down_EFD):
        import jax, jax.numpy as jnp
        import numpy as np
        TOP_K = 2
        E = router_kernel_DE.shape[-1]
        x = x.astype(jnp.float32)
        logits_BSE = jnp.einsum('BSD,DE->BSE', x, router_kernel_DE)
        probs_BSE = jax.nn.softmax(logits_BSE.astype(jnp.float32), axis=-1)
        weights_BSK, indices_BSK = jax.lax.top_k(probs_BSE, TOP_K)
        norm_weights_BSK = jax.nn.softmax(weights_BSK, axis=-1)
        one_hot_BSKE = jax.nn.one_hot(indices_BSK, num_classes=E, dtype=x.dtype)
        full_weights_BSE = jnp.sum(one_hot_BSKE * norm_weights_BSK[..., None], axis=2)
        gating_BSEF = jnp.einsum('BSD,EDF->BSEF', x, kernel_gating_EDF)
        act_BSEF = jax.nn.silu(gating_BSEF)
        up_BSEF = jnp.einsum('BSD,EDF->BSEF', x, kernel_up_EDF)
        fuse_BSEF = act_BSEF * up_BSEF
        down_BSED = jnp.einsum('BSEF,EFD->BSED', fuse_BSEF, kernel_down_EFD)
        out_BSD = jnp.einsum('BSED,BSE->BSD', down_BSED, full_weights_BSE)
        return out_BSD.astype(jnp.float32)

    def _L1_attn_ref(x, w_in, w_conv, b_conv, w_gates, b_gates, forget_base, w_out):
        import jax, jax.numpy as jnp
        import numpy as np
        from jax import lax
        DIM = 256
        E = DIM
        K = 4
        B, T = (4, 1024)

        def _hawk_forward(x, w_in, w_conv, b_conv, w_gates, b_gates, forget_base, w_out):
            proj = jnp.einsum('btc,ec->bte', x, w_in)
            gate, xa = jnp.split(proj, 2, axis=-1)
            k = w_conv.shape[-1]
            xc = lax.conv_general_dilated(xa.transpose(0, 2, 1), w_conv, window_strides=(1,), padding=[(k - 1, 0)], feature_group_count=w_conv.shape[0], dimension_numbers=('NCH', 'OIH', 'NCH'))
            xc = (xc + b_conv[None, :, None]).transpose(0, 2, 1)
            g = jnp.einsum('bte,fe->btf', xc, w_gates) + b_gates
            forget, inp = jnp.split(g, 2, axis=-1)
            alpha = jnp.exp(-8.0 * jax.nn.softplus(forget_base) * jax.nn.sigmoid(forget))
            beta = jnp.sqrt(1.0 - alpha ** 2 + 1e-06)
            u = beta * jax.nn.sigmoid(inp) * xc

            def combine(c1, c2):
                a1, b1 = c1
                a2, b2 = c2
                return (a1 * a2, a2 * b1 + b2)
            _, h = lax.associative_scan(combine, (alpha, u), axis=1)
            y = jax.nn.gelu(gate, approximate=False) * h
            return jnp.einsum('bte,ce->btc', y, w_out)
        return _hawk_forward(x, w_in, w_conv, b_conv, w_gates, b_gates, forget_base, w_out)

    def _L1_ffn_ref(x, weight_int8, weight_scale, bias):
        import jax, jax.numpy as jnp
        import numpy as np
        EPS = 1e-05
        B, S, K = x.shape
        x2 = x.reshape(-1, K)
        x_scale = jnp.maximum(jnp.abs(x2).max() / 127.0, EPS)
        x_int8 = jnp.clip(jnp.round(x2 / x_scale), -128, 127).astype(jnp.int8)
        acc_i32 = jax.lax.dot_general(x_int8, weight_int8.T, dimension_numbers=(((1,), (0,)), ((), ())), preferred_element_type=jnp.int32)
        out = acc_i32.astype(jnp.float32) * x_scale * weight_scale.T
        out = out + bias
        return out.reshape(B, S, -1)
    h = _L0_tok_ref(x, L0_tok_W_lin, L0_tok_b_lin, L0_tok_class_token, L0_tok_position_embeddings)
    h = h + _L0_attn_ref(_layernorm(h, axis=-1), L0_attn_Wq, L0_attn_Wk, L0_attn_Wv, L0_attn_Wbeta, L0_attn_Wg, L0_attn_Wout, L0_attn_ln_g, L0_attn_ln_b)
    h = h + _L0_ffn_ref(_layernorm(h, axis=-1), L0_ffn_router_kernel_DE, L0_ffn_kernel_gating_EDF, L0_ffn_kernel_up_EDF, L0_ffn_kernel_down_EFD)
    h = h + _L1_attn_ref(_layernorm(h, axis=-1), L1_attn_w_in, L1_attn_w_conv, L1_attn_b_conv, L1_attn_w_gates, L1_attn_b_gates, L1_attn_forget_base, L1_attn_w_out)
    h = h + _L1_ffn_ref(_layernorm(h, axis=-1), L1_ffn_weight_int8, L1_ffn_weight_scale, L1_ffn_bias)
    return h

_drawn_inputs = setup_inputs


def setup_inputs(seed=0):
    import zlib

    import numpy as np

    out = dict(_drawn_inputs(seed))
    spreads = {'L0_attn_ln_g': (1.0, 0.6), 'L0_attn_ln_b': (0.0, 0.8), 'L1_attn_b_gates': (0.0, 0.8)}
    factors = {'L0_attn_Wbeta': 7.503,
     'L0_ffn_router_kernel_DE': 4.393,
     'L0_ffn_kernel_gating_EDF': 3.819,
     'L0_ffn_kernel_up_EDF': 3.78,
     'L0_ffn_kernel_down_EFD': 3.783,
     'L1_attn_b_conv': 4.349,
     'L1_ffn_bias': 6.818}
    for name, (base, spread) in spreads.items():
        noise = np.random.default_rng([zlib.crc32(name.encode()), seed]).standard_normal(out[name].shape)
        drawn = base * np.exp(spread * noise) if base else spread * noise
        out[name] = jnp.asarray(drawn.astype(out[name].dtype))
    for name, factor in factors.items():
        out[name] = (out[name] * factor).astype(out[name].dtype)
    return out
```

```python
from contextlib import ExitStack

import concourse.bass as bass
from concourse import mybir

F32 = mybir.dt.float32
F32R = mybir.dt.float32r
BF16 = mybir.dt.bfloat16
I8 = mybir.dt.int8
I32 = mybir.dt.int32
ALU = mybir.AluOpType
ACT = mybir.ActivationFunctionType
AX_X = mybir.AxisListType.X

P = 128
B = 16
IMG = 96
PATCH = 16
CIN = 3
NPATCH = (IMG // PATCH) ** 2
T = NPATCH + 1
D = 256
M = D // P
KE = CIN * PATCH * PATCH // P
NH = 16
HD = D // NH
E = 8
FF = 512
FCH = FF // P
TOPK_STEP = 2.0
CONV = 4
HALF = 2
BH = B // HALF
NT = BH * T
NP = BH * NPATCH
RT = 2 * T
NRT = B * T // RT
IB = 4
NI = HD // IB
EPS = 1e-5
ROUND = 12582912.0
CW = 2 * M * P + D
BODY = 2 * FCH

V_BLIN = 0
V_CLS = V_BLIN + M
V_POS = V_CLS + M
V_LNG = V_POS + M * T
V_LNB = V_LNG + M
V_CONV = V_LNB + M
V_BCONV = V_CONV + M * CONV
V_BGATE = V_BCONV + M
V_FBASE = V_BGATE + 2 * M
V_WSCALE = V_FBASE + M
V_BIAS = V_WSCALE + M
V_RANK = V_BIAS + M
V_ALL = V_RANK + E


def vit_tower(nc, patches, w_lin, vecs, w_qkvg, w_beta, w_attn_out, w_router, w_experts,
              w_in, w_gates, w_hawk_out, w_int8, out):
    with ExitStack() as ctx:
        sems = {}

        def S(name):
            if name not in sems:
                sems[name] = ctx.enter_context(nc.semaphore(name))
            return sems[name]

        def sb(name, shape, dt=F32):
            return ctx.enter_context(nc.sbuf_tensor(name, shape, dt))

        bank = ctx.enter_context(nc.psum_tensor("bank", [P, 8, 512], F32))

        vec = sb("vec", [P, V_ALL])
        wl = sb("wl", [P, KE, D])
        wq = sb("wq", [P, M, 4 * D])
        wb = sb("wb", [P, M, NH])
        wo = sb("wo", [P, M, D])
        wr = sb("wr", [P, M, E])
        wi = sb("wi", [P, M, 2 * D])
        wg = sb("wg", [P, M, 2 * D])
        wh = sb("wh", [P, M, D])
        w8 = sb("w8", [P, M, D // 4], I32)
        w8b = sb("w8b", [P, M, D], BF16)
        mean_w = sb("mean_w", [P, P])
        ident = sb("ident", [P, P])
        posb = sb("posb", [P, M, T])
        h = sb("h", [P, M, B * T])
        xm = sb("xm", [P, M, B * T])
        xsq = sb("xsq", [P, M, B * T])
        std = sb("std", [P, HALF, NT])
        rstd = sb("rstd", [P, HALF, NT])
        n = sb("n", [P, M, B * T])
        sp = sb("sp", [P, 8, M])
        eps_ap = sb("eps_ap", [P, 2])
        silu_g = sb("silu_g", [P, M, B * T])

        shared = ctx.enter_context(nc.sbuf_tensor("raw_place", [P, BODY * CW], F32))
        raw = shared[:, :].rearrange("p (k w) -> p k w", w=CW)
        xp = shared[:, 0:HALF * KE * NP].rearrange("p (c k n) -> p c k n", c=HALF, k=KE)

        with ExitStack() as attn:
            def at(name, shape, dt=F32):
                return attn.enter_context(nc.sbuf_tensor(name, shape, dt))

            chan = at("chan", [P, 3, M, B * T])
            chan_b = at("chan_b", [NH, B * T])
            head = at("head", [P, HALF, 3, HD, T])
            head_b = at("head_b", [P, HALF, T])
            hsq = xsq[:, :, :].rearrange("p x (i t) -> p x i t", t=T)[:, :, 0:HD]
            ssq = at("ssq", [P, HALF, 2, T])
            nrm = at("nrm", [P, HALF, 2, T])
            rnrm = at("rnrm", [P, HALF, 2, T])
            bk = at("bk", [P, HALF, HD, T])
            bv = at("bv", [P, HALF, HD, T])
            decay = at("decay", [P, HD, HD, T])
            kk = at("kk", [P, IB, HD, T])
            write = at("write", [P, 2, IB, HD, T])
            state = at("state", [P, 2, IB, HD, T])
            att = chan[:, 1].rearrange("p c (i t) -> p c i t", t=T)
        och = chan[:, 0]

        with ExitStack() as moe:
            def mo(name, shape, dt=F32):
                return moe.enter_context(nc.sbuf_tensor(name, shape, dt))

            n_hi = mo("n_hi", [P, M, B * T], F32R)
            n_lo = mo("n_lo", [P, M, B * T], F32R)
            w_hi = mo("w_hi", [P, FCH, CW], F32R)
            w_lo = mo("w_lo", [P, FCH, CW], F32R)
            f_hi = mo("f_hi", [P, 2, HALF, NT], F32R)
            f_lo = mo("f_lo", [P, 2, HALF, NT], F32R)
            act_g = mo("act_g", [P, 2, HALF, NT])
            act_u = mo("act_u", [P, HALF, NT])
            fuse = mo("fuse", [P, 2, HALF, NT])
            wbc = mo("wbc", [P, E, HALF, NT])
            r_t = mo("r_t", [RT, 12, NRT, E])
            r_s = mo("r_s", [RT, 12, NRT])

        with ExitStack() as hawk:
            def hk(name, shape, dt=F32):
                return hawk.enter_context(nc.sbuf_tensor(name, shape, dt))

            gelu_g = hk("gelu_g", [P, HALF, M, NT])
            xc = hk("xc", [P, HALF, M, NT])
            sig_f = hk("sig_f", [P, HALF, M, NT])
            sig_i = hk("sig_i", [P, HALF, M, NT])
            alpha = hk("alpha", [P, HALF, M, NT])
            asq = hk("asq", [P, HALF, M, NT])
            beta = hk("beta", [P, HALF, M, NT])
            upd = hk("upd", [P, HALF, M, NT])
            hst = hk("hst", [P, HALF, M, NT])
            amax = hk("amax", [P, 8])
            q1 = hk("q1", [P, HALF, M, NT])
            q2 = hk("q2", [P, HALF, M, NT])
            qx = hk("qx", [P, HALF, M, NT], BF16)
            y1 = hk("y1", [P, HALF, M, NT])
            y = hk("y", [P, HALF, M, NT])

        def half(t, c):
            return t[:, :, c * NT:(c + 1) * NT]

        def V(o, w=1):
            return vec[:, o:o + w]

        def by_image(t):
            return t.rearrange("p m (b t) -> p m b t", t=T)

        def pair(b0):
            return bank[:, b0:b0 + 2, 0:NT]

        block = ctx.enter_context(nc.Block())

        @block.sync
        def _(sp_):
            def load(dst, src, name):
                sp_.dma_start(dst, src).then_inc(S(name), 16)

            load(vec[:, :], vecs, "vec_in")
            load(wl[:, :, :], w_lin, "wl_in")
            load(xp[:, 0], patches[0], "xp0_in")
            load(xp[:, 1], patches[1], "xp1_in")
            load(wq[:, :, :], w_qkvg, "wq_in")
            load(wb[:, :, :], w_beta, "wb_in")
            load(wo[:, :, :], w_attn_out, "wo_in")
            load(wr[:, :, :], w_router, "wr_in")
            load(wi[:, :, :], w_in, "wi_in")
            load(wg[:, :, :], w_gates, "wg_in")
            load(wh[:, :, :], w_hawk_out, "wh_in")
            load(w8[:, :, :], w_int8, "w8_in")
            for c in range(HALF):
                for x, name in enumerate(("k_chan", "q_chan", "v_chan")):
                    sp_.wait_ge(S(name), c + 1)
                    for b in range(BH):
                        for m in range(M):
                            src = chan[:, x, m, (c * BH + b) * T:(c * BH + b + 1) * T]
                            p0 = b * NH + m * (NH // M)
                            sp_.dma_start(head[p0:p0 + NH // M, c, x], src)\
                               .then_inc(S(f"head{c}{x}"), 16)
                sp_.wait_ge(S("b_chan"), c + 1)
                for b in range(BH):
                    sp_.dma_start(head_b[b * NH:(b + 1) * NH, c],
                                  chan_b[:, (c * BH + b) * T:(c * BH + b + 1) * T])\
                       .then_inc(S(f"headb{c}"), 16)
            sp_.wait_ge(S("emb_mm"), HALF)
            for g in range(2):
                sp_.dma_start(raw[:, g * FCH:(g + 1) * FCH], w_experts[g]).then_inc(S(f"raw{g}"), 16)
            for c in range(HALF):
                sp_.wait_ge(S("att_out"), 2 * (c + 1))
                for b in range(BH):
                    for m in range(M):
                        p0 = b * NH + m * (NH // M)
                        sp_.dma_start(och[:, m, (c * BH + b) * T:(c * BH + b + 1) * T],
                                      att[p0:p0 + NH // M, c]).then_inc(S(f"och{c}"), 16)
            with sp_.Fori(0, E // 2 - 1) as i:
                for g in range(2):
                    sp_.wait_ge(S("w_split"), i * BODY + (g + 1) * FCH)
                    sp_.dma_start(raw[:, g * FCH:(g + 1) * FCH],
                                  w_experts[bass.ds(i * 2 + (2 + g), 1)].rearrange("a p k w -> (a p) k w"))\
                       .then_inc(S(f"raw{g}"), 16)
            for c in range(HALF):
                sp_.wait_ge(S("y"), M * (c + 1))
                sp_.dma_start(out[:, :, c * NT:(c + 1) * NT], y[:, c]).then_inc(S("stored"), 16)
            sp_.wait_ge(S("stored"), 16 * HALF)

        @block.gpsimd
        def _(pool):
            pool.memset(mean_w[:, :], 1.0 / D).then_inc(S("mean_w"), 1)
            pool.memset(ident[:, :], 0.0).then_inc(S("ident0"), 1)
            pool.wait_ge(S("ident0"), 1)
            pool.affine_select(out=ident[:, :], in_=ident[:, :], compare_op=ALU.not_equal, fill=1.0,
                               base=0, pattern=[[-1, P]], channel_multiplier=1).then_inc(S("ident"), 1)
            pool.memset(decay[:, :, :, 0:1], 0.0).then_inc(S("decay0"), 1)
            pool.wait_ge(S("w8_in"), 16)
            pool.tensor_copy(w8b[:, :, :], w8[:, :, :].bitcast(I8)).then_inc(S("w8b"), 1)
            for c in range(HALF):
                pool.wait_ge(S("head_beta"), c + 1)
                pool.wait_ge(S(f"head{c}2"), 16 * BH * M)
                pool.tensor_tensor(bv[:, c], head[:, c, 2],
                                   head_b[:, c][:, None, :].to_broadcast([P, HD, T]), ALU.mult)\
                    .then_inc(S("bv"), 1)
                pool.wait_ge(S("khat"), c + 1)
                pool.wait_ge(S("bv"), c + 1)
                for I in range(NI):
                    s = c * NI + I
                    if s >= 2:
                        pool.wait_ge(S("state"), s - 1)
                    pool.tensor_tensor(
                        write[:, s % 2],
                        bv[:, c, I * IB:(I + 1) * IB][:, :, None, :].to_broadcast([P, IB, HD, T]),
                        head[:, c, 0][:, None, :, :].to_broadcast([P, IB, HD, T]),
                        ALU.mult).then_inc(S("write"), 1)

            def split_lo(k, sl):
                pool.tensor_tensor(w_lo[:, sl], raw[:, k], w_hi[:, sl].bitcast(F32), ALU.subtract)\
                    .then_inc(S("w_split"), 1)

            with pool.Fori(0, E // 2) as i:
                for k in range(BODY):
                    pool.wait_ge(S("w_hi"), i * BODY + (k + 1))
                    split_lo(k, k % FCH)
            pool.wait_ge(S("amax"), 1)
            pool.partition_all_reduce(amax[:, 3:4], amax[:, 2:3], P, bass.bass_isa.ReduceOp.max)\
                .then_inc(S("amax_all"), 1)

        @block.scalar
        def _(act):
            def ln_sq(L, c):
                act.wait_ge(S(f"ln{L}_xm"), c + 1)
                act.activation(half(xsq, c), half(xm, c), ACT.Square).then_inc(S(f"ln{L}_sq"), 1)

            def ln_std(L, c):
                act.wait_ge(S(f"ln{L}_var"), c + 1)
                act.activation(std[:, c], bank[:, 6 + c, 0:NT], ACT.Sqrt, bias=eps_ap[:, 0:1]).then_inc(S(f"ln{L}_std"), 1)

            act.wait_ge(S("sp_abs"), 1)
            act.activation(sp[:, 1], sp[:, 0], ACT.Exp, scale=-1.0).then_inc(S("sp_exp"), 1)
            act.wait_ge(S("eps"), 2)
            for c in range(HALF):
                ln_sq(0, c)
                ln_std(0, c)
            for c in range(HALF):
                for x, (name, b0) in enumerate((("k_chan", 0), ("q_chan", 2), ("v_chan", 0))):
                    act.wait_ge(S(name.replace("chan", "mm")), c + 1)
                    act.copy(half(chan[:, x], c), pair(b0)).then_inc(S(name), 1)
                act.wait_ge(S("b_mm"), c + 1)
                act.copy(chan_b[:, c * NT:(c + 1) * NT], bank[0:NH, 4 + c, 0:NT]).then_inc(S("b_chan"), 1)
                act.wait_ge(S("g_mm"), c + 1)
                act.activation(half(silu_g, c), pair(2), ACT.Silu).then_inc(S("silu_g"), 1)
            def prep(c):
                act.wait_ge(S(f"headb{c}"), 16 * BH)
                act.activation(head_b[:, c], head_b[:, c], ACT.Sigmoid).then_inc(S("head_beta"), 1)
                act.wait_ge(S("ssq"), c + 1)
                act.activation(nrm[:, c], ssq[:, c], ACT.Sqrt).then_inc(S("nrm"), 1)

            def decay_rows(c, I):
                s = c * NI + I
                nj = HD - I * IB
                act.wait_ge(S("kk"), s + 1)
                if I == 0 and c == 1:
                    act.wait_ge(S("state"), NI)
                act.activation(decay[:, I * IB:(I + 1) * IB, I * IB:HD, 1:T], kk[:, :, 0:nj, 1:T],
                               ACT.Identity, scale=-1.0, bias=1.0).then_inc(S("decay"), 1)
                if I < NI - 1:
                    act.activation(decay[:, (I + 1) * IB:HD, I * IB:(I + 1) * IB, 1:T],
                                   kk[:, :, IB:nj, 1:T].rearrange("p i j t -> p j i t"),
                                   ACT.Identity, scale=-1.0, bias=1.0).then_inc(S("decay_mirror"), 1)

            def att_evac(c, I):
                if I % 2 == 1:
                    act.wait_ge(S("att_mm"), c * 2 + I // 2 + 1)
                    act.copy(att[:, c, (I - 1) * IB:(I + 1) * IB],
                             bank[:, 2 * c + I // 2, 0:2 * IB * T].rearrange("p (i t) -> p i t", t=T))\
                       .then_inc(S("att_out"), 1)

            act.wait_ge(S("decay0"), 1)
            prep(0)
            for I in range(NI):
                decay_rows(0, I)
            prep(1)
            for c in range(HALF):
                act.wait_ge(S(f"head{c}1"), 16 * BH * M)
            for I in range(NI):
                att_evac(0, I)
            for I in range(NI):
                decay_rows(1, I)
            ln_sq(1, 0)
            ln_std(1, 0)
            for I in range(NI):
                att_evac(1, I)
            ln_sq(1, 1)
            ln_std(1, 1)
            for c in range(HALF):
                ln_sq(2, c)
                ln_std(2, c)
            act.wait_ge(S("r_diff"), 1)
            act.activation(r_t[:, 1], r_t[:, 0], ACT.Exp).then_inc(S("r_exp"), 1)
            act.wait_ge(S("r_gap"), 1)
            act.activation(r_s[:, 6], r_s[:, 5], ACT.Exp).then_inc(S("r_gexp"), 1)
            for c in range(HALF):
                act.wait_ge(S("ln2_n"), c + 1)
                act.copy(half(n_hi, c), half(n, c)).then_inc(S("n_hi"), 1)

            def w_high(k, sl, i):
                act.copy(w_hi[:, sl], raw[:, k]).then_inc(S("w_hi"), 1)

            def chunk(i, k, first=False):
                act.wait_ge(S("gate_mm"), i * BODY + (k + 1))
                act.activation(act_g[:, k % 2], bank[:, 0:2, 0:NT], ACT.Silu).then_inc(S("act_g"), 1)

            def high(i, k):
                act.wait_ge(S("fuse"), i * BODY + (k + 1))
                act.copy(f_hi[:, k % 2], fuse[:, k % 2]).then_inc(S("f_hi"), 1)

            for k in range(2):
                if k == 0:
                    act.wait_ge(S("raw0"), 16)
                w_high(k, k, 0)

            def passes(i, last):
                for k in range(BODY):
                    k2 = k + 2
                    act.wait_ge(S("slots_free"), i * BODY + (k2 + 1))
                    if not (last and k2 >= BODY):
                        if k2 == FCH:
                            act.wait_ge(S("raw1"), i * 16 + 16)
                        if k2 == BODY:
                            act.wait_ge(S("raw0"), i * 16 + 32)
                        w_high(k2 % BODY, k2 % FCH, i)
                    chunk(i, k)
                    high(i, k)

            with act.Fori(0, E // 2 - 1) as i:
                passes(i, False)
            passes(E // 2 - 1, True)

            for c in range(HALF):
                ln_sq(3, c)
                ln_std(3, c)
            for c in range(HALF):
                act.wait_ge(S("hgate_mm"), c + 1)
                act.activation(gelu_g[:, c], pair(2), ACT.Gelu).then_inc(S("gelu_g"), 1)
                for m in range(M):
                    act.wait_ge(S("forget_mm"), c + 1)
                    act.activation(sig_f[:, c, m], bank[:, m, 0:NT], ACT.Sigmoid, bias=V(V_BGATE + m))\
                       .then_inc(S("sig_f"), 1)
                for m in range(M):
                    act.wait_ge(S("input_mm"), c + 1)
                    act.activation(sig_i[:, c, m], bank[:, 2 + m, 0:NT], ACT.Sigmoid, bias=V(V_BGATE + M + m))\
                       .then_inc(S("sig_i"), 1)
                for m in range(M):
                    act.wait_ge(S("sig_f"), M * c + m + 1)
                    act.activation(alpha[:, c, m], sig_f[:, c, m], ACT.Exp, scale=sp[:, 7, m:m + 1])\
                       .then_inc(S("alpha"), 1)
                act.wait_ge(S("one_minus"), c + 1)
                act.activation(beta[:, c], asq[:, c], ACT.Sqrt, bias=eps_ap[:, 1:2]).then_inc(S("beta"), 1)
            for c in range(HALF):
                ln_sq(4, c)
                ln_std(4, c)

        @block.vector
        def _(dve):
            tt = dve.tensor_tensor
            ts = dve.tensor_scalar
            stt = dve.scalar_tensor_tensor

            def ln_xm(L, c, src):
                dve.wait_ge(S(f"ln{L}_mean"), c + 1)
                tt(half(xm, c), half(src, c),
                   bank[:, 4 + c, 0:NT][:, None, :].to_broadcast([P, M, NT]), ALU.subtract)\
                    .then_inc(S(f"ln{L}_xm"), 1)

            def ln_n(L, c):
                dve.wait_ge(S(f"ln{L}_std"), c + 1)
                dve.reciprocal(rstd[:, c], std[:, c]).then_inc(S(f"ln{L}_rstd"), 1)
                dve.wait_ge(S(f"ln{L}_rstd"), c + 1)
                tt(half(n, c), half(xm, c), rstd[:, c][:, None, :].to_broadcast([P, M, NT]), ALU.mult)\
                    .then_inc(S(f"ln{L}_n"), 1)

            dve.memset(eps_ap[:, 0:1], EPS).then_inc(S("eps"), 1)
            dve.memset(eps_ap[:, 1:2], 1e-6).then_inc(S("eps"), 1)
            dve.wait_ge(S("vec_in"), 16)
            fb = V(V_FBASE, M)
            stt(sp[:, 0], fb, -1.0, fb, ALU.mult, ALU.max).then_inc(S("sp_abs"), 1)
            pos = V(V_POS, M * T).rearrange("p (m t) -> p m t", t=T)
            tt(posb[:, :, 1:T], pos[:, :, 1:T], V(V_BLIN, M)[:, :, None].to_broadcast([P, M, NPATCH]),
               ALU.add).then_inc(S("posb"), 1)
            tt(posb[:, :, 0:1], pos[:, :, 0:1], V(V_CLS, M)[:, :, None], ALU.add).then_inc(S("posb"), 1)
            dve.wait_ge(S("posb"), 2)
            hi_ = by_image(h[:, :, :])
            dve.tensor_copy(hi_[:, :, :, 0], posb[:, :, 0:1].to_broadcast([P, M, B])).then_inc(S("cls"), 1)
            dve.wait_ge(S("sp_exp"), 1)
            ts(sp[:, 2], sp[:, 1], 2.0, None, ALU.add).then_inc(S("sp_step"), 1)
            dve.wait_ge(S("sp_step"), 1)
            dve.reciprocal(sp[:, 3], sp[:, 2]).then_inc(S("sp_step"), 1)
            dve.wait_ge(S("sp_step"), 2)
            tt(sp[:, 4], sp[:, 1], sp[:, 3], ALU.mult).then_inc(S("sp_step"), 1)
            dve.wait_ge(S("sp_step"), 3)
            tt(sp[:, 5], sp[:, 4], sp[:, 4], ALU.mult).then_inc(S("sp_step"), 1)
            dve.wait_ge(S("sp_step"), 4)
            ts(sp[:, 6], sp[:, 5], 1.0 / 17.0, None, ALU.mult).then_inc(S("sp_step"), 1)
            step = 5
            for odd in range(15, 1, -2):
                dve.wait_ge(S("sp_step"), step)
                stt(sp[:, 6], sp[:, 6], 1.0 / odd, sp[:, 5], ALU.add, ALU.mult).then_inc(S("sp_step"), 1)
                step += 1
            dve.wait_ge(S("sp_step"), step)
            stt(sp[:, 6], sp[:, 6], 1.0, sp[:, 4], ALU.add, ALU.mult).then_inc(S("sp_step"), 1)
            ts(sp[:, 2], fb, 0.0, -8.0, ALU.max, ALU.mult).then_inc(S("sp_step"), 1)
            dve.wait_ge(S("sp_step"), step + 2)
            stt(sp[:, 7], sp[:, 6], -16.0, sp[:, 2], ALU.mult, ALU.add).then_inc(S("sp"), 1)

            for c in range(HALF):
                dve.wait_ge(S("emb_mm"), c + 1)
                for m in range(M):
                    tt(hi_[:, m, c * BH:(c + 1) * BH, 1:T],
                       bank[:, 2 * c + m, 0:NP].rearrange("p (b t) -> p b t", t=NPATCH),
                       posb[:, m, 1:T][:, None, :].to_broadcast([P, BH, NPATCH]), ALU.add)\
                        .then_inc(S("emb"), 1)
            for c in range(HALF):
                ln_xm(0, c, h)
            for c in range(HALF):
                ln_n(0, c)

            def prep(c):
                dve.wait_ge(S(f"head{c}0"), 16 * BH * M)
                dve.wait_ge(S(f"head{c}1"), 16 * BH * M)
                if c:
                    dve.wait_ge(S("ssq"), c)
                tt(hsq[:, :], head[:, c, 0:2], head[:, c, 0:2], ALU.mult).then_inc(S("hsq"), 1)
                dve.wait_ge(S("hsq"), c + 1)
                dve.tensor_reduce(ssq[:, c], hsq[:, :].rearrange("p x i t -> p x t i"), AX_X, ALU.add)\
                    .then_inc(S("ssq0"), 1)
                dve.wait_ge(S("ssq0"), c + 1)
                ts(ssq[:, c], ssq[:, c], 1e-24, None, ALU.max).then_inc(S("ssq"), 1)
                dve.wait_ge(S("nrm"), c + 1)
                dve.reciprocal(rnrm[:, c], nrm[:, c]).then_inc(S("rnrm"), 1)
                dve.wait_ge(S("rnrm"), c + 1)
                tt(head[:, c, 0:2], head[:, c, 0:2],
                   rnrm[:, c][:, :, None, :].to_broadcast([P, 2, HD, T]), ALU.mult).then_inc(S("khat"), 1)
                dve.wait_ge(S("khat"), c + 1)
                dve.wait_ge(S("head_beta"), c + 1)
                tt(bk[:, c], head[:, c, 0], head_b[:, c][:, None, :].to_broadcast([P, HD, T]), ALU.mult)\
                    .then_inc(S("bk"), 1)

            def outer(c, I):
                s = c * NI + I
                nj = HD - I * IB
                dve.wait_ge(S("bk"), c + 1)
                if s >= 1:
                    dve.wait_ge(S("decay"), s)
                    dve.wait_ge(S("decay_mirror"), c * (NI - 1) + I)
                tt(kk[:, :, 0:nj],
                   bk[:, c, I * IB:(I + 1) * IB][:, :, None, :].to_broadcast([P, IB, nj, T]),
                   head[:, c, 0, I * IB:HD][:, None, :, :].to_broadcast([P, IB, nj, T]), ALU.mult)\
                    .then_inc(S("kk"), 1)

            def scan(c, I):
                s = c * NI + I
                dve.wait_ge(S("write"), s + 1)
                dve.wait_ge(S("decay"), s + 1)
                if c * (NI - 1) + I:
                    dve.wait_ge(S("decay_mirror"), c * (NI - 1) + I)
                if s >= 2:
                    dve.wait_ge(S("att_part"), s - 1)
                dve.tensor_tensor_scan(
                    state[:, s % 2].rearrange("p i j t -> p (i j t)"),
                    decay[:, I * IB:(I + 1) * IB].rearrange("p i j t -> p (i j t)"),
                    write[:, s % 2].rearrange("p i j t -> p (i j t)"),
                    0.0, ALU.mult, ALU.add).then_inc(S("state"), 1)

            def query(c, I):
                s = c * NI + I
                dve.wait_ge(S("state"), s + 1)
                tt(state[:, s % 2], state[:, s % 2],
                   head[:, c, 1][:, None, :, :].to_broadcast([P, IB, HD, T]), ALU.mult)\
                    .then_inc(S("read"), 1)

            def attn_norm(c):
                ln_n(1, c)
                for m in range(M):
                    dve.wait_ge(S("ln1_n"), c + 1)
                    ts(half(n, c)[:, m], half(n, c)[:, m], V(V_LNG + m), V(V_LNB + m), ALU.mult, ALU.add)\
                        .then_inc(S("affine"), 1)
                dve.wait_ge(S("affine"), M * (c + 1))
                dve.wait_ge(S("silu_g"), c + 1)
                tt(half(n, c), half(n, c), half(silu_g, c), ALU.mult).then_inc(S("gated"), 1)

            def residual(name, mm, c, b0):
                dve.wait_ge(S(mm), c + 1)
                tt(half(h, c), half(h, c), pair(b0), ALU.add).then_inc(S(name), 1)

            prep(0)
            for I in range(NI):
                outer(0, I)
            prep(1)
            for I in range(NI):
                scan(0, I)
                query(0, I)
            for I in range(NI):
                outer(1, I)
            ln_xm(1, 0, och)
            scan(1, 0)
            query(1, 0)
            attn_norm(0)
            scan(1, 1)
            query(1, 1)
            residual("h1", "wo_mm", 0, 0)
            for I in range(2, NI):
                scan(1, I)
                query(1, I)
            ln_xm(1, 1, och)
            ln_xm(2, 0, h)
            attn_norm(1)
            ln_n(2, 0)
            residual("h1", "wo_mm", 1, 2)
            ln_xm(2, 1, h)
            ln_n(2, 1)

            step = 0

            def last(ins):
                ins.then_inc(S("route"), 1)

            def chain():
                dve.wait_ge(S("route"), step)

            lg = bank[0:RT, 0, 0:NRT * E].rearrange("p (r e) -> p r e", e=E)
            rank = vec[0:RT, V_RANK:V_RANK + E][:, None, :].to_broadcast([RT, NRT, E])

            def bc(k):
                return r_s[:, k][:, :, None].to_broadcast([RT, NRT, E])

            dve.wait_ge(S("router_mm"), 1)
            last(dve.tensor_reduce(r_s[:, 0], lg, AX_X, ALU.max)); step += 1
            chain()
            tt(r_t[:, 0], lg, bc(0), ALU.subtract).then_inc(S("r_diff"), 1)
            dve.wait_ge(S("r_exp"), 1)
            last(dve.tensor_reduce(r_s[:, 1], r_t[:, 1], AX_X, ALU.add)); step += 1
            chain()
            last(dve.reciprocal(r_s[:, 2], r_s[:, 1])); step += 1
            chain()
            last(tt(r_t[:, 2], r_t[:, 1], bc(2), ALU.mult)); step += 1
            chain()
            last(dve.tensor_reduce(r_s[:, 3], r_t[:, 2], AX_X, ALU.max)); step += 1
            chain()
            last(tt(r_t[:, 3], r_t[:, 2], bc(3), ALU.is_equal)); step += 1
            chain()
            last(tt(r_t[:, 3], r_t[:, 3], rank, ALU.mult)); step += 1
            chain()
            last(dve.tensor_reduce(r_s[:, 8], r_t[:, 3], AX_X, ALU.max)); step += 1
            chain()
            last(tt(r_t[:, 4], rank, bc(8), ALU.is_equal)); step += 1
            chain()
            last(stt(r_t[:, 5], r_t[:, 4], -TOPK_STEP, r_t[:, 2], ALU.mult, ALU.add)); step += 1
            chain()
            last(dve.tensor_reduce(r_s[:, 4], r_t[:, 5], AX_X, ALU.max)); step += 1
            chain()
            tt(r_s[:, 5], r_s[:, 4], r_s[:, 3], ALU.subtract).then_inc(S("r_gap"), 1)
            last(tt(r_t[:, 6], r_t[:, 5], bc(4), ALU.is_equal)); step += 1
            chain()
            last(tt(r_t[:, 6], r_t[:, 6], rank, ALU.mult)); step += 1
            chain()
            last(dve.tensor_reduce(r_s[:, 9], r_t[:, 6], AX_X, ALU.max)); step += 1
            chain()
            last(tt(r_t[:, 7], rank, bc(9), ALU.is_equal)); step += 1
            dve.wait_ge(S("r_gexp"), 1)
            last(ts(r_s[:, 7], r_s[:, 6], 1.0, None, ALU.add)); step += 1
            chain()
            last(dve.reciprocal(r_s[:, 10], r_s[:, 7])); step += 1
            chain()
            last(tt(r_s[:, 11], r_s[:, 6], r_s[:, 10], ALU.mult)); step += 1
            last(tt(r_t[:, 8], r_t[:, 4], bc(10), ALU.mult)); step += 1
            chain()
            last(tt(r_t[:, 9], r_t[:, 7], bc(11), ALU.mult)); step += 1
            chain()
            tt(r_t[:, 10], r_t[:, 8], r_t[:, 9], ALU.add).then_inc(S("r_weight"), 1)
            for c in range(HALF):
                dve.wait_ge(S("n_hi"), c + 1)
                tt(half(n_lo, c), half(n, c), half(n_hi, c).bitcast(F32), ALU.subtract)\
                    .then_inc(S("n_lo"), 1)
            for e in range(E):
                dve.wait_ge(S("wbc_mm"), e + 1)
                dve.tensor_copy(wbc[:, e], pair(2 * (e % 2))).then_inc(S("wbc"), 1)
            dve.wait_ge(S("wbc"), E)

            def expert_chunk(i, k):
                e = i * 2 + k // FCH
                dve.wait_ge(S("act_g"), i * BODY + (k + 1))
                dve.wait_ge(S("up_mm"), i * BODY + (k + 1))
                tt(act_u[:, :], act_g[:, k % 2], bank[:, 2:4, 0:NT], ALU.mult).then_inc(S("act_u"), 1)
                dve.wait_ge(S("act_u"), i * BODY + (k + 1))
                w = wbc[:, e] if isinstance(e, int) else \
                    wbc[:, bass.ds(e, 1)].rearrange("p a c n -> p (a c) n")
                tt(fuse[:, k % 2], act_u[:, :], w, ALU.mult).then_inc(S("fuse"), 1)
                dve.wait_ge(S("f_hi"), i * BODY + (k + 1))
                tt(f_lo[:, k % 2], fuse[:, k % 2], f_hi[:, k % 2].bitcast(F32), ALU.subtract)\
                    .then_inc(S("f_lo"), 1)
                if k == BODY - 1:
                    dve.wait_ge(S("slots_free"), i * BODY + (FCH + BODY))
                    for m in range(M):
                        tt(h[:, m].rearrange("p (c n) -> p c n", c=HALF),
                           h[:, m].rearrange("p (c n) -> p c n", c=HALF),
                           bank[:, 4 + 2 * m:6 + 2 * m, 0:NT], ALU.add).then_inc(S("sums_added"), 1)

            with dve.Fori(0, E // 2 - 1) as i:
                for k in range(BODY):
                    expert_chunk(i, k)
            for k in range(BODY):
                expert_chunk(E // 2 - 1, k)

            dve.wait_ge(S("sums_added"), M + E // 2 * M)
            for c in range(HALF):
                ln_xm(3, c, h)
            for c in range(HALF):
                ln_n(3, c)
            def im(t):
                return t.rearrange("p (b t) -> p b t", t=T)

            for c in range(HALF):
                dve.wait_ge(S("hx_mm"), c + 1)
                for m in range(M):
                    base = V_CONV + m * CONV
                    k0 = (c * M + m) * CONV
                    ts(xc[:, c, m], bank[:, m, 0:NT], V(base + CONV - 1), V(V_BCONV + m), ALU.mult, ALU.add)\
                        .then_inc(S("conv"), 1)
                    for s in range(1, CONV):
                        dve.wait_ge(S("conv"), k0 + s)
                        stt(im(xc[:, c, m])[:, :, s:T], im(bank[:, m, 0:NT])[:, :, 0:T - s],
                            V(base + CONV - 1 - s), im(xc[:, c, m])[:, :, s:T], ALU.mult, ALU.add)\
                            .then_inc(S("conv"), 1)
                dve.wait_ge(S("alpha"), M * (c + 1))
                tt(asq[:, c], alpha[:, c], alpha[:, c], ALU.mult).then_inc(S("asq"), 1)
                dve.wait_ge(S("asq"), c + 1)
                ts(asq[:, c], asq[:, c], -1.0, 1.0, ALU.mult, ALU.add).then_inc(S("one_minus"), 1)
                dve.memset(alpha[:, c].rearrange("p m (b t) -> p (m b) t", t=T)[:, :, 0:1], 0.0)\
                    .then_inc(S("alpha0"), 1)
                dve.wait_ge(S("sig_i"), M * (c + 1))
                tt(upd[:, c], sig_i[:, c], xc[:, c], ALU.mult).then_inc(S("upd0"), 1)
                dve.wait_ge(S("upd0"), c + 1)
                dve.wait_ge(S("beta"), c + 1)
                tt(upd[:, c], upd[:, c], beta[:, c], ALU.mult).then_inc(S("upd"), 1)
                dve.wait_ge(S("upd"), c + 1)
                dve.wait_ge(S("alpha0"), c + 1)
                dve.tensor_tensor_scan(hst[:, c].rearrange("p m n -> p (m n)"),
                                       alpha[:, c].rearrange("p m n -> p (m n)"),
                                       upd[:, c].rearrange("p m n -> p (m n)"),
                                       0.0, ALU.mult, ALU.add).then_inc(S("hst"), 1)
                dve.wait_ge(S("hst"), c + 1)
                dve.wait_ge(S("gelu_g"), c + 1)
                tt(hst[:, c], hst[:, c], gelu_g[:, c], ALU.mult).then_inc(S("hawk_y"), 1)
                residual("h3", "hawk_mm", c, 0)
            for c in range(HALF):
                ln_xm(4, c, h)
            for c in range(HALF):
                ln_n(4, c)
                dve.wait_ge(S("ln4_n"), c + 1)
                dve.tensor_reduce(amax[:, c:c + 1], half(n, c), mybir.AxisListType.XY, ALU.max,
                                  apply_absolute_value=True).then_inc(S("amax_half"), 1)
            dve.wait_ge(S("amax_half"), HALF)
            tt(amax[:, 2:3], amax[:, 0:1], amax[:, 1:2], ALU.max).then_inc(S("amax"), 1)
            dve.wait_ge(S("amax_all"), 1)
            ts(amax[:, 4:5], amax[:, 3:4], 1.0 / 127.0, EPS, ALU.mult, ALU.max).then_inc(S("x_scale"), 1)
            dve.wait_ge(S("x_scale"), 1)
            dve.reciprocal(amax[:, 5:6], amax[:, 4:5]).then_inc(S("x_scale"), 1)
            dve.wait_ge(S("x_scale"), 2)
            for c in range(HALF):
                ts(q1[:, c], half(n, c), amax[:, 5:6], 127.0, ALU.mult, ALU.min).then_inc(S("q1"), 1)
                dve.wait_ge(S("q1"), c + 1)
                ts(q2[:, c], q1[:, c], -128.0, ROUND, ALU.max, ALU.add).then_inc(S("q2"), 1)
                dve.wait_ge(S("q2"), c + 1)
                ts(qx[:, c], q2[:, c], ROUND, None, ALU.subtract).then_inc(S("qx"), 1)
            for c in range(HALF):
                dve.wait_ge(S("int_mm"), c + 1)
                for m in range(M):
                    ts(y1[:, c, m], bank[:, 2 * c + m, 0:NT], amax[:, 4:5], V(V_WSCALE + m),
                       ALU.mult, ALU.mult).then_inc(S("y1"), 1)
                for m in range(M):
                    dve.wait_ge(S("y1"), M * c + m + 1)
                    stt(y[:, c, m], y1[:, c, m], V(V_BIAS + m), half(h, c)[:, m], ALU.add, ALU.add)\
                        .then_inc(S("y"), 1)

        @block.tensor
        def _(pe):
            def mm(o, w, x, start, stop):
                return pe.matmul(o, w, x, start=start, stop=stop)

            def linear(o, w, x, kt):
                for k in range(kt):
                    r = mm(o, w(k), x(k), k == 0, k == kt - 1)
                return r

            def ln_mean(L, c, src):
                linear(bank[:, 4 + c, 0:NT], lambda k: mean_w[:, :], lambda k: half(src, c)[:, k], M)\
                    .then_inc(S(f"ln{L}_mean"), 1)

            def ln_var(L, c):
                pe.wait_ge(S(f"ln{L}_sq"), c + 1)
                linear(bank[:, 6 + c, 0:NT], lambda k: mean_w[:, :], lambda k: half(xsq, c)[:, k], M)\
                    .then_inc(S(f"ln{L}_var"), 1)

            def project(w, m0, c, b0, src=n):
                for m in range(M):
                    r = linear(bank[:, b0 + m, 0:NT], lambda k: w[:, k, m0 + m * P:m0 + (m + 1) * P],
                               lambda k: half(src, c)[:, k], M)
                return r

            pe.wait_ge(S("wl_in"), 16)
            for c in range(HALF):
                pe.wait_ge(S(f"xp{c}_in"), 16)
                for m in range(M):
                    r = linear(bank[:, 2 * c + m, 0:NP], lambda k: wl[:, k, m * P:(m + 1) * P],
                               lambda k: xp[:, c, k], KE)
                r.then_inc(S("emb_mm"), 1)
            pe.wait_ge(S("mean_w"), 1)
            pe.wait_ge(S("cls"), 1)
            for c in range(HALF):
                pe.wait_ge(S("emb"), M * (c + 1))
                ln_mean(0, c, h)
            for c in range(HALF):
                ln_var(0, c)
            pe.wait_ge(S("wq_in"), 16)
            pe.wait_ge(S("wb_in"), 16)
            for c in range(HALF):
                pe.wait_ge(S("ln0_n"), c + 1)
                if c:
                    pe.wait_ge(S("v_chan"), c)
                project(wq, D, c, 0).then_inc(S("k_mm"), 1)
                if c:
                    pe.wait_ge(S("silu_g"), c)
                project(wq, 0, c, 2).then_inc(S("q_mm"), 1)
                pe.wait_ge(S("k_chan"), c + 1)
                project(wq, 2 * D, c, 0).then_inc(S("v_mm"), 1)
                linear(bank[0:NH, 4 + c, 0:NT], lambda k: wb[:, k], lambda k: half(n, c)[:, k], M)\
                    .then_inc(S("b_mm"), 1)
                pe.wait_ge(S("q_chan"), c + 1)
                project(wq, 3 * D, c, 2).then_inc(S("g_mm"), 1)

            def att_sum(c, I):
                s = c * NI + I
                pe.wait_ge(S("read"), s + 1)
                o = bank[:, 2 * c + I // 2, (I % 2) * IB * T:(I % 2 + 1) * IB * T]\
                    .rearrange("p (i t) -> p i t", t=T)
                for j in range(HD):
                    r = mm(o, ident[:, :], state[:, s % 2, :, j], j == 0, j == HD - 1)
                r.then_inc(S("att_part"), 1)
                if I % 2 == 1:
                    pe.wait_ge(S("att_part"), s + 1)
                    pe.nop().then_inc(S("att_mm"), 1)

            def out_proj(c):
                pe.wait_ge(S("gated"), c + 1)
                if c == 0:
                    pe.wait_ge(S("wo_in"), 16)
                project(wo, 0, c, 2 * c).then_inc(S("wo_mm"), 1)

            pe.wait_ge(S("ident"), 1)
            pe.wait_ge(S("v_chan"), HALF)
            for I in range(NI):
                att_sum(0, I)
            pe.wait_ge(S("silu_g"), HALF)
            pe.wait_ge(S("b_chan"), HALF)
            pe.wait_ge(S("och0"), 16 * BH * M)
            ln_mean(1, 0, och)
            ln_var(1, 0)
            att_sum(1, 0)
            out_proj(0)
            for I in range(1, NI):
                att_sum(1, I)
            pe.wait_ge(S("och1"), 16 * BH * M)
            ln_mean(1, 1, och)
            pe.wait_ge(S("h1"), 1)
            pe.wait_ge(S("ln1_xm"), 1)
            ln_mean(2, 0, h)
            ln_var(1, 1)
            ln_var(2, 0)
            out_proj(1)
            pe.wait_ge(S("h1"), 2)
            ln_mean(2, 1, h)
            ln_var(2, 1)

            pe.wait_ge(S("wr_in"), 16)
            for c in range(HALF):
                pe.wait_ge(S("ln2_n"), c + 1)
                for r_ in range(c * NRT // HALF, (c + 1) * NRT // HALF):
                    r = linear(bank[0:RT, 0, r_ * E:(r_ + 1) * E],
                               lambda k: n[:, k, r_ * RT:(r_ + 1) * RT], lambda k: wr[:, k], M)
            r.then_inc(S("router_mm"), 1)
            pe.wait_ge(S("r_weight"), 1)
            for e in range(E):
                if e >= 2:
                    pe.wait_ge(S("wbc"), e - 1)
                for r_ in range(NRT):
                    c, q = divmod(r_, NRT // HALF)
                    r = mm(bank[:, 2 * (e % 2) + c, q * RT:(q + 1) * RT],
                           r_t[:, 10, r_, e:e + 1].to_broadcast([RT, P]), ident[0:RT, 0:RT], True, True)
                r.then_inc(S("wbc_mm"), 1)

            def three(o, w, x, start, stop):
                mm(o, w[0], x[0], start, False)
                mm(o, w[0], x[1], False, False)
                return mm(o, w[1], x[0], False, stop)

            def gate_up(i, k):
                sl = k % FCH
                pe.wait_ge(S("w_split"), i * BODY + (k + 1))
                for what, b0, done, name in ((0, 0, "act_g", "gate_mm"), (1, 2, "act_u", "up_mm")):
                    if not (isinstance(i, int) and i * BODY + k == 0):
                        pe.wait_ge(S(done), i * BODY + k)
                    for kt in range(M):
                        o = (what * M + kt) * P
                        for c in range(HALF):
                            r = three(bank[:, b0 + c, 0:NT],
                                      (w_hi[:, sl, o:o + P], w_lo[:, sl, o:o + P]),
                                      (half(n_hi, c)[:, kt], half(n_lo, c)[:, kt]), kt == 0, kt == M - 1)
                    r.then_inc(S(name), 1)

            def down(i, k):
                sl = k % FCH
                pe.wait_ge(S("f_lo"), i * BODY + (k + 1))
                if k == 0:
                    pe.wait_ge(S("sums_added"), i * M + M)
                for m in range(M):
                    o = 2 * M * P + m * P
                    for c in range(HALF):
                        r = three(bank[:, 4 + 2 * m + c, 0:NT],
                                  (w_hi[:, sl, o:o + P], w_lo[:, sl, o:o + P]),
                                  (f_hi[:, k % 2, c], f_lo[:, k % 2, c]), k == 0, k == BODY - 1)
                r.then_inc(S("slots_free"), 1)

            for c in range(HALF):
                pe.wait_ge(S("n_lo"), c + 1)
            pe.nop().then_inc(S("slots_free"), FCH)
            pe.nop().then_inc(S("sums_added"), M)
            pe.wait_ge(S("wbc"), E)
            gate_up(0, 0)
            with pe.Fori(0, E // 2 - 1) as i:
                for k in range(BODY):
                    if k < BODY - 1:
                        gate_up(i, k + 1)
                    else:
                        gate_up(i + 1, 0)
                    down(i, k)
            for k in range(BODY):
                if k < BODY - 1:
                    gate_up(E // 2 - 1, k + 1)
                down(E // 2 - 1, k)

            pe.wait_ge(S("sums_added"), M + E // 2 * M)
            for c in range(HALF):
                ln_mean(3, c, h)
            for c in range(HALF):
                ln_var(3, c)
            pe.wait_ge(S("wi_in"), 16)
            pe.wait_ge(S("wg_in"), 16)
            pe.wait_ge(S("wh_in"), 16)
            for c in range(HALF):
                pe.wait_ge(S("ln3_n"), c + 1)
                if c:
                    pe.wait_ge(S("h3"), c)
                project(wi, D, c, 0).then_inc(S("hx_mm"), 1)
                project(wi, 0, c, 2).then_inc(S("hgate_mm"), 1)
                pe.wait_ge(S("conv"), CONV * M * (c + 1))
                for m in range(M):
                    r = linear(bank[:, m, 0:NT], lambda k: wg[:, k, m * P:(m + 1) * P],
                               lambda k: xc[:, c, k], M)
                r.then_inc(S("forget_mm"), 1)
                pe.wait_ge(S("gelu_g"), c + 1)
                for m in range(M):
                    r = linear(bank[:, 2 + m, 0:NT], lambda k: wg[:, k, D + m * P:D + (m + 1) * P],
                               lambda k: xc[:, c, k], M)
                r.then_inc(S("input_mm"), 1)
                pe.wait_ge(S("hawk_y"), c + 1)
                for m in range(M):
                    r = linear(bank[:, m, 0:NT], lambda k: wh[:, k, m * P:(m + 1) * P],
                               lambda k: hst[:, c, k], M)
                r.then_inc(S("hawk_mm"), 1)
            pe.wait_ge(S("h3"), HALF)
            for c in range(HALF):
                ln_mean(4, c, h)
            for c in range(HALF):
                ln_var(4, c)
            pe.wait_ge(S("w8b"), 1)
            for c in range(HALF):
                pe.wait_ge(S("qx"), c + 1)
                for m in range(M):
                    r = linear(bank[:, 2 * c + m, 0:NT], lambda k: w8b[:, k, m * P:(m + 1) * P],
                               lambda k: qx[:, c, k], M)
                r.then_inc(S("int_mm"), 1)


def _tiles(a):
    k, n = a.shape
    return a.reshape(k // 128, 128, n).transpose(1, 0, 2)


def kernel(**inputs):
    import numpy as np
    import concourse.bacc as bacc
    from concourse.bass_utils import run_bass_kernel_spmd

    a = {k: np.asarray(v) for k, v in inputs.items()}
    g = IMG // PATCH
    x = a["x"].reshape(HALF, BH, CIN, g, PATCH, g, PATCH).transpose(0, 2, 4, 6, 1, 3, 5)
    x = x.reshape(HALF, KE, P, NP).transpose(0, 2, 1, 3)

    def cols(v):
        return v.reshape(-1, P).T

    pos = a["L0_tok_position_embeddings"][0].reshape(T, M, P).transpose(2, 1, 0).reshape(P, M * T)
    conv = a["L1_attn_w_conv"].reshape(M, P, CONV).transpose(1, 0, 2).reshape(P, M * CONV)
    rank = np.broadcast_to(np.arange(E, 0, -1, dtype=np.float32), (P, E))
    vecs = np.concatenate([
        cols(a["L0_tok_b_lin"]), cols(a["L0_tok_class_token"].reshape(D)), pos,
        cols(a["L0_attn_ln_g"]), cols(a["L0_attn_ln_b"]), conv, cols(a["L1_attn_b_conv"]),
        cols(a["L1_attn_b_gates"]), cols(a["L1_attn_forget_base"]),
        cols(a["L1_ffn_weight_scale"].reshape(D)), cols(a["L1_ffn_bias"]), rank], axis=1)

    def up(w):
        return w.reshape(E, M, P, FCH, P).transpose(0, 2, 3, 1, 4).reshape(E, P, FCH, M * P)

    dn = a["L0_ffn_kernel_down_EFD"].reshape(E, FCH, P, D).transpose(0, 2, 1, 3)
    experts = np.concatenate([up(a["L0_ffn_kernel_gating_EDF"]), up(a["L0_ffn_kernel_up_EDF"]), dn], axis=3)
    arrays = {
        "patches": x,
        "w_lin": _tiles(a["L0_tok_W_lin"].T),
        "vecs": vecs,
        "w_qkvg": _tiles(np.concatenate([a["L0_attn_Wq"], a["L0_attn_Wk"], a["L0_attn_Wv"],
                                         a["L0_attn_Wg"]], axis=1)),
        "w_beta": _tiles(a["L0_attn_Wbeta"]),
        "w_attn_out": _tiles(a["L0_attn_Wout"]),
        "w_router": _tiles(a["L0_ffn_router_kernel_DE"]),
        "w_experts": experts,
        "w_in": _tiles(a["L1_attn_w_in"].T),
        "w_gates": _tiles(a["L1_attn_w_gates"].T),
        "w_hawk_out": _tiles(a["L1_attn_w_out"].T),
        "w_int8": np.ascontiguousarray(_tiles(a["L1_ffn_weight_int8"].T)).view(np.int32),
    }
    nc = bacc.Bacc("TRN2", target_bir_lowering=False, num_devices=1)
    args = []
    for name in arrays:
        arrays[name] = np.ascontiguousarray(arrays[name])
        args.append(nc.dram_tensor(name, arrays[name].shape, mybir.dt.from_np(arrays[name].dtype),
                                   kind="ExternalInput").ap())
    args.append(nc.dram_tensor("out", (P, M, B * T), F32, kind="ExternalOutput").ap())
    vit_tower(nc, *args)
    r = run_bass_kernel_spmd(nc, [arrays], core_ids=[0])
    o = r.results[0]["out"]
    return o.transpose(2, 1, 0).reshape(B, T, D)
```

```python
from contextlib import ExitStack

import concourse.bass as bass
from concourse import mybir

F32 = mybir.dt.float32
F32R = mybir.dt.float32r
BF16 = mybir.dt.bfloat16
I8 = mybir.dt.int8
I32 = mybir.dt.int32
U32 = mybir.dt.uint32
ALU = mybir.AluOpType
ACT = mybir.ActivationFunctionType
AX_X = mybir.AxisListType.X

P = 128
B = 16
IMG = 96
PATCH = 16
CIN = 3
NPATCH = (IMG // PATCH) ** 2
T = NPATCH + 1
D = 256
M = D // P
KE = CIN * PATCH * PATCH // P
NH = 16
HD = D // NH
E = 8
FF = 512
FCH = FF // P
TOPK_STEP = 2.0
CONV = 4
HALF = 2
BH = B // HALF
NT = BH * T
NP = BH * NPATCH
RT = 2 * T
NRT = B * T // RT
NRH = NRT // HALF
IB = 4
NI = HD // IB
EPS = 1e-5
ROUND = 12582912.0
SPREAD = 16
SLOTS = 208
GR = SLOTS // 2
TP = 640
NR = TP // P
NRT0 = (B * T // 2 + P - 1) // P
OV = (2 * B * T - 1) // SLOTS
OVE = (B * T + SLOTS - 1) // SLOTS - 1
ZREP = 4
ZCOLS = OV * SLOTS * D // P // ZREP
PW = 512
PIECES = 6
GU = FCH

V_BLIN = 0
V_CLS = V_BLIN + M
V_POS = V_CLS + M
V_LNG = V_POS + M * T
V_LNB = V_LNG + M
V_CONV = V_LNB + M
V_BCONV = V_CONV + M * CONV
V_BGATE = V_BCONV + M
V_FBASE = V_BGATE + 2 * M
V_WSCALE = V_FBASE + M
V_BIAS = V_WSCALE + M
V_RANK = V_BIAS + M
V_VALID = V_RANK + E
V_RESET = V_VALID + NR
V_BASE = V_RESET + E * NR
V_OVER = V_BASE + E
V_IOTA = V_OVER + E
V_ALL = V_IOTA + SLOTS


def vit_tower(nc, patches, w_lin, vecs, w_qkvg, w_beta, w_attn_out, w_router, w_experts,
              w_in, w_gates, w_hawk_out, w_int8, out):
    with ExitStack() as ctx:
        sems = {}

        def S(name):
            if name not in sems:
                sems[name] = ctx.enter_context(nc.semaphore(name))
            return sems[name]

        def sb(name, shape, dt=F32):
            return ctx.enter_context(nc.sbuf_tensor(name, shape, dt))

        by_head = nc.dram_tensor("by_head", (HALF, 3, BH, D, T), F32, kind="Internal").ap()
        beta_by_head = nc.dram_tensor("beta_by_head", (HALF, BH, NH, T), F32, kind="Internal").ap()
        sum_by_head = nc.dram_tensor("sum_by_head", (HALF, BH, D, T), F32, kind="Internal").ap()
        y_rows = nc.dram_tensor("y_rows", ((E + OV) * SLOTS, D), F32, kind="Internal").ap()
        bank = ctx.enter_context(nc.psum_tensor("bank", [P, 8, 512], F32))

        vec = sb("vec", [P, V_ALL])
        wl = sb("wl", [P, KE, D])
        wq = sb("wq", [P, M, 4 * D])
        wb = sb("wb", [P, M, NH])
        wo = sb("wo", [P, M, D])
        wr = sb("wr", [P, M, E])
        wi = sb("wi", [P, M, 2 * D])
        wg = sb("wg", [P, M, 2 * D])
        wh = sb("wh", [P, M, D])
        w8 = sb("w8", [P, M, D // 4], I32)
        w8b = sb("w8b", [P, M, D], BF16)
        mean_w = sb("mean_w", [P, P])
        ident = sb("ident", [P, P])
        posb = sb("posb", [P, M, T])
        h = sb("h", [P, M, B * T])
        xm = sb("xm", [P, M, B * T])
        xsq = sb("xsq", [P, M, TP])
        var = sb("var", [RT, HALF, NRH])
        rstd = sb("rstd", [RT, HALF, NRH])
        neg_half = sb("neg_half", [RT, NRH])
        n = sb("n", [P, M, TP])
        before = sb("before", [P, P])
        ones = sb("ones", [P, P])
        e_tab = sb("e_tab", [1, OV + 1], I32)
        sp = sb("sp", [P, 8, M])
        eps_ap = sb("eps_ap", [P, 1])
        silu_g = sb("silu_g", [P, M, TP])

        shared = ctx.enter_context(nc.sbuf_tensor("raw_place", [P, 2 * PIECES * PW], F32))
        raw = shared[:, :].rearrange("p (s k w) -> p s k w", s=2, w=PW)
        xp = shared[:, 0:HALF * KE * NP].rearrange("p (c k n) -> p c k n", c=HALF, k=KE)

        with ExitStack() as attn:
            def at(name, shape, dt=F32):
                return attn.enter_context(nc.sbuf_tensor(name, shape, dt))

            chan = at("chan", [P, 3, M, B * T])
            chan_b = at("chan_b", [NH, B * T])
            head = at("head", [P, HALF, 3, HD, T])
            head_b = at("head_b", [P, HALF, T])
            hsq = xsq[:, :, 0:HD * T].rearrange("p x (i t) -> p x i t", t=T)
            ssq = at("ssq", [P, HALF, 2, T])
            rnrm = at("rnrm", [P, HALF, 2, T])
            nrm = at("nrm", [P, HALF, 2, T])
            bk = at("bk", [P, HALF, HD, T])
            bv = at("bv", [P, HALF, HD, T])
            decay = at("decay", [P, HD, HD, T])
            kk = at("kk", [P, IB, HD, T])
            write = at("write", [P, 2, IB, HD, T])
            state = at("state", [P, 2, IB, HD, T])
            att = chan[:, 1].rearrange("p c (i t) -> p c i t", t=T)
        och = chan[:, 0]

        with ExitStack() as moe:
            def mo(name, shape, dt=F32):
                return moe.enter_context(nc.sbuf_tensor(name, shape, dt))

            w_hi = mo("w_hi", [P, 2, PIECES, PW], F32R)
            w_lo = mo("w_lo", [P, 2, PIECES, PW], F32R)
            tok_hi = mo("tok_hi", [P, NR, D], F32R)
            tok_lo = mo("tok_lo", [P, NR, D], F32R)
            pick = mo("pick", [P, 2, NR, SLOTS], F32R)
            pick_a = mo("pick_a", [P, NR, SLOTS])
            pick_b = mo("pick_b", [P, NR, SLOTS])
            x_hi = mo("x_hi", [P, 2, M, SLOTS], F32R)
            x_lo = mo("x_lo", [P, 2, M, SLOTS], F32R)
            act_g = mo("act_g", [P, 2, FCH, SLOTS])
            fuse = mo("fuse", [P, 2, FCH, SLOTS])
            f_hi = mo("f_hi", [P, 2, FCH, SLOTS], F32R)
            f_lo = mo("f_lo", [P, 2, FCH, SLOTS], F32R)
            y_sb = mo("y_sb", [GR, 2, 2, D])
            y_tok = mo("y_tok", [P, NR, 2, D])
            y_w = silu_g[:, :, :].rearrange("p m n -> p (m n)").rearrange("p (r c) -> p r c", c=D)
            y_sum = xsq[:, :, :].rearrange("p m n -> p (m n)").rearrange("p (r c) -> p r c", c=D)
            r_t = mo("r_t", [P, 12, NR, E])
            r_s = mo("r_s", [P, 12, NR])
            c_t = mo("c_t", [P, 8, E, NR])
            c_s = mo("c_s", [P, 6, E])
            rows = mo("rows", [P, 4, NR])
            row_i = mo("row_i", [P, 2, NR], U32)
            e_f = mo("e_f", [1, OV, E])
            e_s = mo("e_s", [1, OV + 1])

        with ExitStack() as hawk:
            def hk(name, shape, dt=F32):
                return hawk.enter_context(nc.sbuf_tensor(name, shape, dt))

            gelu_g = hk("gelu_g", [P, HALF, M, NT])
            xc = hk("xc", [P, HALF, M, NT])
            sig_f = hk("sig_f", [P, HALF, M, NT])
            sig_i = hk("sig_i", [P, HALF, M, NT])
            alpha = hk("alpha", [P, HALF, M, NT])
            asq = hk("asq", [P, HALF, M, NT])
            beta = hk("beta", [P, HALF, M, NT])
            upd = hk("upd", [P, HALF, M, NT])
            hst = hk("hst", [P, HALF, M, NT])
            amax = hk("amax", [P, 8])
            q1 = hk("q1", [P, HALF, M, NT])
            q2 = hk("q2", [P, HALF, M, NT])
            qx = hk("qx", [P, HALF, M, NT], BF16)
            y1 = hk("y1", [P, HALF, M, NT])
            y = hk("y", [P, HALF, M, NT])

        def half(t, c):
            return t[:, :, c * NT:(c + 1) * NT]

        def V(o, w=1):
            return vec[:, o:o + w]

        def by_image(t):
            return t.rearrange("p m (b t) -> p m b t", t=T)

        def pair(b0):
            return bank[:, b0:b0 + 2, 0:NT]

        def expert(e):
            return w_experts[bass.ds(e, 1)].rearrange("a p k w -> (a p) k w")

        def tile_rows(t):
            return y_rows[bass.ds(t * SLOTS, SLOTS)].rearrange("(g p) c -> p g c", g=2)

        block = ctx.enter_context(nc.Block())

        @block.sync
        def _(sp_):
            def load(dst, src, name):
                sp_.dma_start(dst, src).then_inc(S(name), 16)

            load(vec[:, :], vecs, "vec_in")
            load(wl[:, :, :], w_lin, "wl_in")
            load(xp[:, 0], patches[0], "xp0_in")
            load(xp[:, 1], patches[1], "xp1_in")
            load(wq[:, :, :], w_qkvg, "wq_in")
            load(wb[:, :, :], w_beta, "wb_in")
            load(wo[:, :, :], w_attn_out, "wo_in")
            load(wr[:, :, :], w_router, "wr_in")
            load(wi[:, :, :], w_in, "hawk_w_in")
            load(wg[:, :, :], w_gates, "hawk_w_in")
            load(wh[:, :, :], w_hawk_out, "hawk_w_in")
            load(w8[:, :, :], w_int8, "w8_in")
            sp_.wait_ge(S("zeros"), 1)
            sp_.dma_start(y_rows[E * SLOTS:, :].rearrange("r c -> (r c)").rearrange("(p z w) -> p z w", p=P, z=ZREP),
                          silu_g[:, 0, 0:ZCOLS][:, None, :].to_broadcast([P, ZREP, ZCOLS]))\
               .then_inc(S("y_zeroed"), 16)
            for c in range(HALF):
                for x, name in enumerate(("k_chan", "q_chan", "v_chan")):
                    sp_.wait_ge(S(name), c + 1)
                    for m in range(M):
                        sp_.dma_start(by_head[c, x, :, m * P:(m + 1) * P].rearrange("b p t -> p b t"),
                                      chan[:, x, m, c * NT:(c + 1) * NT].rearrange("p (b t) -> p b t", t=T))\
                           .then_inc(S(f"spill{c}{x}"), 16)
                    sp_.wait_ge(S(f"spill{c}{x}"), 16 * M)
                    sp_.dma_start(head[:, c, x].rearrange("p i t -> p (i t)"),
                                  by_head[c, x].rearrange("b (h i) t -> (b h) (i t)", i=HD))\
                       .then_inc(S(f"head{c}{x}"), 16)
                    if x == 0:
                        sp_.wait_ge(S("b_chan"), c + 1)
                        sp_.dma_start(beta_by_head[c].rearrange("b h t -> h b t"),
                                      chan_b[:, c * NT:(c + 1) * NT].rearrange("p (b t) -> p b t", t=T))\
                           .then_inc(S(f"spillb{c}"), 16)
                        sp_.wait_ge(S(f"spillb{c}"), 16)
                        sp_.dma_start(head_b[:, c], beta_by_head[c].rearrange("b h t -> (b h) t"))\
                           .then_inc(S(f"headb{c}"), 16)
            sp_.wait_ge(S("emb_mm"), HALF)
            for g in range(2):
                sp_.dma_start(raw[:, g], w_experts[g]).then_inc(S(f"raw{g}"), 16)
            for c in range(HALF):
                sp_.wait_ge(S("att_out"), 2 * (c + 1))
                sp_.dma_start(sum_by_head[c].rearrange("b (h i) t -> (b h) (i t)", i=HD),
                              att[:, c].rearrange("p i t -> p (i t)")).then_inc(S(f"spillo{c}"), 16)
                sp_.wait_ge(S(f"spillo{c}"), 16)
                for m in range(M):
                    sp_.dma_start(och[:, m, c * NT:(c + 1) * NT].rearrange("p (b t) -> p b t", t=T),
                                  sum_by_head[c, :, m * P:(m + 1) * P].rearrange("b p t -> p b t"))\
                       .then_inc(S(f"och{c}"), 16)
            for g in range(2):
                sp_.nop().then_inc(S(f"y_stored{g}"), 16)

            def store(t, slot):
                sp_.wait_ge(S("y_out"), t + 3)
                sp_.dma_start(tile_rows(t), y_sb[:, slot]).then_inc(S(f"y_stored{slot}"), 16)

            def reload(t, slot):
                sp_.wait_ge(S("w_split"), (t + 1) * PIECES)
                sp_.dma_start(raw[:, slot], expert(t + 2)).then_inc(S(f"raw{slot}"), 16)

            reload(0, 0)
            with sp_.Fori(0, E // 2 - 2) as i:
                for slot in range(2):
                    reload(i * 2 + slot + 1, 1 - slot)
                    store(i * 2 + slot, slot)
            reload(E - 3, 1)
            for t in range(E - 4, E):
                store(t, t % 2)
            sp_.wait_ge(S("e_tab"), 1)
            n_over = sp_.value_load(e_tab[0:1, OV:OV + 1], min_val=0, max_val=OV)
            with sp_.If(n_over > 0):
                with sp_.Fori(0, n_over) as o:
                    sp_.wait_ge(S("w_split"), o * PIECES + E * PIECES)
                    e = sp_.value_load(e_tab[0:1, bass.ds(o, 1)], min_val=0, max_val=E - 1)
                    sp_.dma_start(raw[:, 0], expert(e)).then_inc(S("raw0"), 16)
                    store(o + E, 0)
            for c in range(HALF):
                sp_.wait_ge(S("y"), M * (c + 1))
                sp_.dma_start(out[:, :, c * NT:(c + 1) * NT], y[:, c]).then_inc(S("stored"), 16)
            sp_.wait_ge(S("stored"), 16 * HALF)

        @block.gpsimd
        def _(pool):
            pool.memset(mean_w[:, :], 1.0 / D).then_inc(S("mean_w"), 1)
            pool.memset(ident[:, :], 0.0).then_inc(S("ident0"), 1)
            pool.wait_ge(S("ident0"), 1)
            pool.affine_select(out=ident[:, :], in_=ident[:, :], compare_op=ALU.not_equal, fill=1.0,
                               base=0, pattern=[[-1, P]], channel_multiplier=1).then_inc(S("ident"), 1)
            pool.memset(decay[:, :, :, 0:1], 0.0).then_inc(S("decay0"), 1)
            pool.memset(silu_g[:, 0, 0:ZCOLS], 0.0).then_inc(S("zeros"), 1)
            pool.memset(ones[:, :], 1.0).then_inc(S("ones"), 1)
            pool.wait_ge(S("ones"), 1)
            pool.affine_select(out=before[:, :], in_=ones[:, :], compare_op=ALU.is_gt, fill=0.0,
                               base=0, pattern=[[1, P]], channel_multiplier=-1).then_inc(S("before"), 1)
            pool.memset(n[:, :, B * T:TP], 0.0).then_inc(S("n_pad"), 1)
            pool.memset(neg_half[:, :], -0.5).then_inc(S("neg_half"), 1)
            pool.wait_ge(S("neg_half"), 1)

            def ln_rstd(L, c):
                pool.wait_ge(S(f"ln_eps{c}"), L + 1)
                pool.tensor_tensor(rstd[:, c], var[:, c], neg_half[:, :], ALU.pow)\
                    .then_inc(S(f"ln_rstd{c}"), 1)

            for c in range(HALF):
                ln_rstd(0, c)
            pool.wait_ge(S("w8_in"), 16)
            pool.tensor_copy(w8b[:, :, :], w8[:, :, :].bitcast(I8)).then_inc(S("w8b"), 1)
            def head_scales(c):
                pool.wait_ge(S("head_beta"), c + 1)
                pool.wait_ge(S(f"head{c}2"), 16)
                pool.tensor_tensor(bv[:, c], head[:, c, 2],
                                   head_b[:, c][:, None, :].to_broadcast([P, HD, T]), ALU.mult)\
                    .then_inc(S("bv"), 1)

            head_scales(0)
            for c in range(HALF):
                pool.wait_ge(S("khat"), c + 1)
                pool.wait_ge(S("bv"), c + 1)
                for I in range(NI):
                    s = c * NI + I
                    if s >= 2:
                        pool.wait_ge(S("state"), s - 1)
                    pool.tensor_tensor(
                        write[:, s % 2],
                        bv[:, c, I * IB:(I + 1) * IB][:, :, None, :].to_broadcast([P, IB, HD, T]),
                        head[:, c, 0][:, None, :, :].to_broadcast([P, IB, HD, T]),
                        ALU.mult).then_inc(S("write"), 1)
                    if s == 1:
                        head_scales(1)
                    if s == NI + 2:
                        ln_rstd(1, 0)
            ln_rstd(2, 0)
            ln_rstd(1, 1)
            ln_rstd(2, 1)

            def split(t, slot):
                for p in range(PIECES):
                    pool.wait_ge(S("w_hi"), t * PIECES + (p + 1))
                    pool.tensor_tensor(w_lo[:, slot, p], raw[:, slot, p], w_hi[:, slot, p].bitcast(F32),
                                       ALU.subtract).then_inc(S("w_split"), 1)

            with pool.Fori(0, E // 2) as i:
                for slot in range(2):
                    split(i * 2 + slot, slot)
            pool.wait_ge(S("e_tab"), 1)
            n_over = pool.value_load(e_tab[0:1, OV:OV + 1], min_val=0, max_val=OV)
            with pool.If(n_over > 0):
                with pool.Fori(0, n_over) as o:
                    split(o + E, 0)
                    pool.wait_ge(S("y_stored0"), o * 16 + 16 * (E // 2 + 2))
            for slot in range(2):
                pool.wait_ge(S(f"y_stored{slot}"), 16 * (E // 2 + 1))
            pool.wait_ge(S("y_zeroed"), 16)
            pool.wait_ge(S("row_i"), 1)
            for r in range(NR):
                for j in range(2):
                    pool.indirect_dma_start(
                        out=y_tok[:, r, j], out_offset=None, in_=y_rows,
                        in_offset=bass.IndirectOffsetOnAxis(ap=row_i[:, j, r:r + 1], axis=0))\
                        .then_inc(S(f"y_tok{r}"), 16)
            for L in (3, 4):
                for c in range(HALF):
                    ln_rstd(L, c)
            pool.wait_ge(S("amax"), 1)
            pool.partition_all_reduce(amax[:, 3:4], amax[:, 2:3], P, bass.bass_isa.ReduceOp.max)\
                .then_inc(S("amax_all"), 1)

        @block.scalar
        def _(act):
            def ln_sq(L, c):
                act.wait_ge(S(f"ln_xm{c}"), L + 1)
                act.activation(half(xsq, c), half(xm, c), ACT.Square).then_inc(S(f"ln_sq{c}"), 1)

            act.wait_ge(S("sp_abs"), 1)
            act.activation(sp[:, 1], sp[:, 0], ACT.Exp, scale=-1.0).then_inc(S("sp_exp"), 1)
            act.wait_ge(S("eps"), 1)
            for c in range(HALF):
                ln_sq(0, c)
            for c in range(HALF):
                for x, (name, b0) in enumerate((("k_chan", 0), ("q_chan", 2), ("v_chan", 0))):
                    act.wait_ge(S(name.replace("chan", "mm")), c + 1)
                    act.copy(half(chan[:, x], c), pair(b0)).then_inc(S(name), 1)
                act.wait_ge(S("b_mm"), c + 1)
                act.copy(chan_b[:, c * NT:(c + 1) * NT], bank[0:NH, 4 + c, 0:NT]).then_inc(S("b_chan"), 1)
                act.wait_ge(S("g_mm"), c + 1)
                if c == 0:
                    act.wait_ge(S("y_zeroed"), 16)
                act.activation(half(silu_g, c), pair(2), ACT.Silu).then_inc(S("silu_g"), 1)
            def prep(c):
                act.wait_ge(S(f"headb{c}"), 16)
                act.activation(head_b[:, c], head_b[:, c], ACT.Sigmoid).then_inc(S("head_beta"), 1)
                act.wait_ge(S("ssq"), c + 1)
                act.activation(nrm[:, c], ssq[:, c], ACT.Sqrt).then_inc(S("nrm"), 1)

            def decay_rows(c, I):
                s = c * NI + I
                nj = HD - I * IB
                act.wait_ge(S("kk"), s + 1)
                if I == 0 and c == 1:
                    act.wait_ge(S("state"), NI)
                act.activation(decay[:, I * IB:(I + 1) * IB, I * IB:HD, 1:T], kk[:, :, 0:nj, 1:T],
                               ACT.Identity, scale=-1.0, bias=1.0).then_inc(S("decay"), 1)
                if I < NI - 1:
                    act.activation(decay[:, (I + 1) * IB:HD, I * IB:(I + 1) * IB, 1:T],
                                   kk[:, :, IB:nj, 1:T].rearrange("p i j t -> p j i t"),
                                   ACT.Identity, scale=-1.0, bias=1.0).then_inc(S("decay_mirror"), 1)

            def att_evac(c, I):
                if I % 2 == 1:
                    act.wait_ge(S("att_mm"), c * 2 + I // 2 + 1)
                    act.copy(att[:, c, (I - 1) * IB:(I + 1) * IB],
                             bank[:, 2 * c + I // 2, 0:2 * IB * T].rearrange("p (i t) -> p i t", t=T))\
                       .then_inc(S("att_out"), 1)

            act.wait_ge(S("decay0"), 1)
            prep(0)
            for I in range(NI):
                decay_rows(0, I)
            prep(1)
            for c in range(HALF):
                act.wait_ge(S(f"head{c}1"), 16)
            for I in range(NI):
                att_evac(0, I)
            for I in range(NI):
                decay_rows(1, I)
            ln_sq(1, 0)
            for I in range(NI):
                att_evac(1, I)
            ln_sq(2, 0)
            ln_sq(1, 1)
            ln_sq(2, 1)

            def w_high(t, slot, pieces):
                for p in pieces:
                    act.copy(w_hi[:, slot, p], raw[:, slot, p]).then_inc(S("w_hi"), 1)

            act.wait_ge(S("ln_xm1"), 2)
            act.wait_ge(S("raw0"), 16)
            w_high(0, 0, range(PIECES))
            act.wait_ge(S("r_diff"), 1)
            act.activation(r_t[:, 1], r_t[:, 0], ACT.Exp).then_inc(S("r_exp"), 1)
            act.wait_ge(S("r_gap"), 1)
            act.activation(r_s[:, 6], r_s[:, 5], ACT.Exp).then_inc(S("r_gexp"), 1)
            act.wait_ge(S("tok_mm"), 1)
            act.copy(tok_hi[:, 0:4].rearrange("p (b r) c -> p b (r c)", b=2), bank[:, 0:2, :])\
               .then_inc(S("tok_hi"), 1)
            act.copy(tok_hi[:, 4], bank[:, 2, 0:D]).then_inc(S("tok_hi"), 1)
            act.wait_ge(S("raw1"), 16)
            w_high(1, 1, range(PIECES))

            def x_high(t, slot):
                act.wait_ge(S("x_hi_mm"), t + 1)
                act.copy(x_hi[:, slot], bank[:, 0, 0:M * SLOTS].rearrange("p (m s) -> p m s", m=M))\
                   .then_inc(S("x_hi"), 1)

            def silu(t, slot):
                act.wait_ge(S("gate_mm"), t + 1)
                act.activation(act_g[:, slot].rearrange("p (b f) s -> p b (f s)", b=2),
                               bank[:, 2:4, 0:2 * SLOTS], ACT.Silu).then_inc(S("act_g"), 1)

            def f_high(t, slot):
                act.wait_ge(S("fuse"), t + 1)
                act.copy(f_hi[:, slot], fuse[:, slot]).then_inc(S("f_hi"), 1)

            x_high(0, 0)
            silu(0, 0)
            f_high(0, 0)
            x_high(1, 1)
            with act.Fori(0, E // 2 - 1) as i:
                for slot in range(2):
                    t = i * 2 + slot
                    act.wait_ge(S(f"raw{slot}"), i * 16 + 32)
                    act.wait_ge(S("front"), t + 1)
                    w_high(t + 2, slot, range(GU))
                    silu(t + 1, 1 - slot)
                    f_high(t + 1, 1 - slot)
                    x_high(t + 2, slot)
                    act.wait_ge(S("back"), t + 1)
                    w_high(t + 2, slot, range(GU, PIECES))
            silu(E - 1, 1)
            f_high(E - 1, 1)
            act.wait_ge(S("e_tab"), 1)
            n_over = act.value_load(e_tab[0:1, OV:OV + 1], min_val=0, max_val=OV)
            with act.If(n_over > 0):
                with act.Fori(0, n_over) as o:
                    act.wait_ge(S("raw0"), o * 16 + 16 * (E // 2 + 1))
                    act.wait_ge(S("back"), o + E)
                    w_high(o + E, 0, range(PIECES))
                    x_high(o + E, 0)
                    silu(o + E, 0)
                    f_high(o + E, 0)

            for c in range(HALF):
                ln_sq(3, c)
            for c in range(HALF):
                act.wait_ge(S("hgate_mm"), c + 1)
                act.activation(gelu_g[:, c], pair(4 * c + 2), ACT.Gelu).then_inc(S("gelu_g"), 1)
            for c in range(HALF):
                for m in range(M):
                    act.wait_ge(S("forget_mm"), c + 1)
                    act.activation(sig_f[:, c, m], bank[:, 4 * c + m, 0:NT], ACT.Sigmoid, bias=V(V_BGATE + m))\
                       .then_inc(S("sig_f"), 1)
                for m in range(M):
                    act.wait_ge(S("input_mm"), c + 1)
                    act.activation(sig_i[:, c, m], bank[:, 4 * c + 2 + m, 0:NT], ACT.Sigmoid,
                                   bias=V(V_BGATE + M + m)).then_inc(S("sig_i"), 1)
            for c in range(HALF):
                for m in range(M):
                    act.wait_ge(S("sig_f"), M * c + m + 1)
                    act.activation(alpha[:, c, m], sig_f[:, c, m], ACT.Exp, scale=sp[:, 7, m:m + 1])\
                       .then_inc(S("alpha"), 1)
            for c in range(HALF):
                act.wait_ge(S("one_minus"), c + 1)
                act.activation(beta[:, c], asq[:, c], ACT.Sqrt, bias=eps_ap[:, :]).then_inc(S("beta"), 1)
            for c in range(HALF):
                ln_sq(4, c)

        @block.vector
        def _(dve):
            tt = dve.tensor_tensor
            ts = dve.tensor_scalar
            stt = dve.scalar_tensor_tensor
            steps = [0]

            def step(ins):
                ins.then_inc(S("dve_step"), 1)
                steps[0] += 1
                dve.wait_ge(S("dve_step"), steps[0])

            def ln_xm(L, c, src, mb):
                dve.wait_ge(S(f"ln_mean{c}"), L + 1)
                tt(half(xm, c), half(src, c),
                   bank[:, mb, 0:NT][:, None, :].to_broadcast([P, M, NT]), ALU.subtract)\
                    .then_inc(S(f"ln_xm{c}"), 1)

            def ln_eps(L, c, vb):
                dve.wait_ge(S(f"ln_var{c}"), L + 1)
                ts(var[:, c], bank[0:RT, vb, 0:NRH], EPS, None, ALU.add).then_inc(S(f"ln_eps{c}"), 1)

            def ln_n(L, c, vb):
                dve.wait_ge(S(f"ln_bc{c}"), L + 1)
                tt(half(n, c), half(xm, c),
                   bank[:, vb, SPREAD:SPREAD + NT][:, None, :].to_broadcast([P, M, NT]), ALU.mult)\
                    .then_inc(S(f"ln_n{c}"), 1)

            dve.memset(eps_ap[:, :], 1e-6).then_inc(S("eps"), 1)
            dve.wait_ge(S("vec_in"), 16)
            fb = V(V_FBASE, M)
            stt(sp[:, 0], fb, -1.0, fb, ALU.mult, ALU.max).then_inc(S("sp_abs"), 1)
            pos = V(V_POS, M * T).rearrange("p (m t) -> p m t", t=T)
            step(tt(posb[:, :, 1:T], pos[:, :, 1:T], V(V_BLIN, M)[:, :, None].to_broadcast([P, M, NPATCH]),
                    ALU.add))
            step(tt(posb[:, :, 0:1], pos[:, :, 0:1], V(V_CLS, M)[:, :, None], ALU.add))
            hi_ = by_image(h[:, :, :])
            dve.tensor_copy(hi_[:, :, :, 0], posb[:, :, 0:1].to_broadcast([P, M, B])).then_inc(S("cls"), 1)
            dve.wait_ge(S("sp_exp"), 1)
            step(ts(sp[:, 2], sp[:, 1], 2.0, None, ALU.add))
            step(dve.reciprocal(sp[:, 3], sp[:, 2]))
            step(tt(sp[:, 4], sp[:, 1], sp[:, 3], ALU.mult))
            step(tt(sp[:, 5], sp[:, 4], sp[:, 4], ALU.mult))
            step(ts(sp[:, 6], sp[:, 5], 1.0 / 17.0, None, ALU.mult))
            for odd in range(15, 1, -2):
                step(stt(sp[:, 6], sp[:, 6], 1.0 / odd, sp[:, 5], ALU.add, ALU.mult))
            step(stt(sp[:, 6], sp[:, 6], 1.0, sp[:, 4], ALU.add, ALU.mult))
            step(ts(sp[:, 2], fb, 0.0, -8.0, ALU.max, ALU.mult))
            stt(sp[:, 7], sp[:, 6], -16.0, sp[:, 2], ALU.mult, ALU.add).then_inc(S("sp"), 1)

            for c in range(HALF):
                dve.wait_ge(S("emb_mm"), c + 1)
                for m in range(M):
                    tt(hi_[:, m, c * BH:(c + 1) * BH, 1:T],
                       bank[:, 2 * c + m, 0:NP].rearrange("p (b t) -> p b t", t=NPATCH),
                       posb[:, m, 1:T][:, None, :].to_broadcast([P, BH, NPATCH]), ALU.add)\
                        .then_inc(S("emb"), 1)
            for c in range(HALF):
                ln_xm(0, c, h, 4 + c)
            for c in range(HALF):
                ln_eps(0, c, 6 + c)
            for c in range(HALF):
                ln_n(0, c, 6 + c)

            def prep(c):
                dve.wait_ge(S(f"head{c}0"), 16)
                dve.wait_ge(S(f"head{c}1"), 16)
                if c:
                    dve.wait_ge(S("ssq"), c)
                step(tt(hsq[:, :], head[:, c, 0:2], head[:, c, 0:2], ALU.mult))
                step(dve.tensor_reduce(ssq[:, c], hsq[:, :].rearrange("p x i t -> p x t i"), AX_X, ALU.add))
                ts(ssq[:, c], ssq[:, c], 1e-24, None, ALU.max).then_inc(S("ssq"), 1)

            def prep_b(c):
                dve.wait_ge(S("nrm"), c + 1)
                step(dve.reciprocal(rnrm[:, c], nrm[:, c]))
                tt(head[:, c, 0:2], head[:, c, 0:2],
                   rnrm[:, c][:, :, None, :].to_broadcast([P, 2, HD, T]), ALU.mult).then_inc(S("khat"), 1)
                dve.wait_ge(S("khat"), c + 1)
                dve.wait_ge(S("head_beta"), c + 1)
                tt(bk[:, c], head[:, c, 0], head_b[:, c][:, None, :].to_broadcast([P, HD, T]), ALU.mult)\
                    .then_inc(S("bk"), 1)

            def outer(c, I):
                s = c * NI + I
                nj = HD - I * IB
                dve.wait_ge(S("bk"), c + 1)
                if s >= 1:
                    dve.wait_ge(S("decay"), s)
                    dve.wait_ge(S("decay_mirror"), c * (NI - 1) + I)
                tt(kk[:, :, 0:nj],
                   bk[:, c, I * IB:(I + 1) * IB][:, :, None, :].to_broadcast([P, IB, nj, T]),
                   head[:, c, 0, I * IB:HD][:, None, :, :].to_broadcast([P, IB, nj, T]), ALU.mult)\
                    .then_inc(S("kk"), 1)

            def scan(c, I):
                s = c * NI + I
                dve.wait_ge(S("write"), s + 1)
                dve.wait_ge(S("decay"), s + 1)
                if c * (NI - 1) + I:
                    dve.wait_ge(S("decay_mirror"), c * (NI - 1) + I)
                if s >= 2:
                    dve.wait_ge(S("att_part"), s - 1)
                dve.tensor_tensor_scan(
                    state[:, s % 2].rearrange("p i j t -> p (i j t)"),
                    decay[:, I * IB:(I + 1) * IB].rearrange("p i j t -> p (i j t)"),
                    write[:, s % 2].rearrange("p i j t -> p (i j t)"),
                    0.0, ALU.mult, ALU.add).then_inc(S("state"), 1)

            def query(c, I):
                s = c * NI + I
                dve.wait_ge(S("state"), s + 1)
                tt(state[:, s % 2], state[:, s % 2],
                   head[:, c, 1][:, None, :, :].to_broadcast([P, IB, HD, T]), ALU.mult)\
                    .then_inc(S("read"), 1)

            def attn_norm(c):
                ln_n(1, c, 6 + c)
                for m in range(M):
                    dve.wait_ge(S(f"ln_n{c}"), 2)
                    step(ts(half(n, c)[:, m], half(n, c)[:, m], V(V_LNG + m), V(V_LNB + m),
                            ALU.mult, ALU.add))
                dve.wait_ge(S("silu_g"), c + 1)
                tt(half(n, c), half(n, c), half(silu_g, c), ALU.mult).then_inc(S("gated"), 1)

            def residual(name, mm, c, b0):
                dve.wait_ge(S(mm), c + 1)
                tt(half(h, c), half(h, c), pair(b0), ALU.add).then_inc(S(name), 1)

            prep(0)
            prep_b(0)
            for I in range(NI):
                outer(0, I)
            prep(1)
            for I in range(NI - 1):
                scan(0, I)
                query(0, I)
            prep_b(1)
            outer(1, 0)
            scan(0, NI - 1)
            query(0, NI - 1)
            for I in range(1, NI):
                outer(1, I)
            scan(1, 0)
            query(1, 0)
            ln_xm(1, 0, och, 4)
            scan(1, 1)
            query(1, 1)
            ln_eps(1, 0, 6)
            scan(1, 2)
            attn_norm(0)
            query(1, 2)
            scan(1, 3)
            query(1, 3)
            residual("h1", "wo_mm", 0, 0)
            ln_xm(2, 0, h, 4)
            ln_eps(2, 0, 6)
            ln_n(2, 0, 6)
            ln_xm(1, 1, och, 5)
            ln_eps(1, 1, 7)
            attn_norm(1)
            residual("h1", "wo_mm", 1, 2)
            ln_xm(2, 1, h, 5)
            ln_eps(2, 1, 7)
            ln_n(2, 1, 7)

            lg = bank[:, 3, 0:NR * E].rearrange("p (r e) -> p r e", e=E)
            rank = vec[:, V_RANK:V_RANK + E][:, None, :].to_broadcast([P, NR, E])
            valid = vec[:, V_VALID:V_VALID + NR]

            def bc(k):
                return r_s[:, k][:, :, None].to_broadcast([P, NR, E])

            def by_tile(x):
                return x.rearrange("p e r -> p r e")

            dve.wait_ge(S("router_mm"), 1)
            step(dve.tensor_reduce(r_s[:, 0], lg, AX_X, ALU.max))
            tt(r_t[:, 0], lg, bc(0), ALU.subtract).then_inc(S("r_diff"), 1)
            dve.wait_ge(S("r_exp"), 1)
            step(dve.tensor_reduce(r_s[:, 1], r_t[:, 1], AX_X, ALU.add))
            step(dve.reciprocal(r_s[:, 2], r_s[:, 1]))
            step(tt(r_t[:, 2], r_t[:, 1], bc(2), ALU.mult))
            step(dve.tensor_reduce(r_s[:, 3], r_t[:, 2], AX_X, ALU.max))
            step(tt(r_t[:, 3], r_t[:, 2], bc(3), ALU.is_equal))
            step(tt(r_t[:, 3], r_t[:, 3], rank, ALU.mult))
            step(dve.tensor_reduce(r_s[:, 8], r_t[:, 3], AX_X, ALU.max))
            step(tt(r_t[:, 4], rank, bc(8), ALU.is_equal))
            step(stt(r_t[:, 5], r_t[:, 4], -TOPK_STEP, r_t[:, 2], ALU.mult, ALU.add))
            step(dve.tensor_reduce(r_s[:, 4], r_t[:, 5], AX_X, ALU.max))
            tt(r_s[:, 5], r_s[:, 4], r_s[:, 3], ALU.subtract).then_inc(S("r_gap"), 1)
            step(tt(r_t[:, 6], r_t[:, 5], bc(4), ALU.is_equal))
            step(tt(r_t[:, 6], r_t[:, 6], rank, ALU.mult))
            step(dve.tensor_reduce(r_s[:, 9], r_t[:, 6], AX_X, ALU.max))
            step(tt(r_t[:, 7], rank, bc(9), ALU.is_equal))
            step(tt(r_t[:, 8], r_t[:, 4], r_t[:, 7], ALU.add))
            tt(by_tile(c_t[:, 0]), r_t[:, 8], valid[:, :, None].to_broadcast([P, NR, E]), ALU.mult)\
                .then_inc(S("chosen"), 1)
            for j in range(2):
                dve.wait_ge(S("tok_hi"), j + 1)
                if j == 0:
                    tt(tok_lo[:, 0:4].rearrange("p (b r) c -> p b (r c)", b=2), bank[:, 0:2, :],
                       tok_hi[:, 0:4].bitcast(F32).rearrange("p (b r) c -> p b (r c)", b=2), ALU.subtract)\
                        .then_inc(S("tok_lo"), 1)
                else:
                    tt(tok_lo[:, 4], bank[:, 2, 0:D], tok_hi[:, 4].bitcast(F32), ALU.subtract)\
                        .then_inc(S("tok_lo"), 1)
            dve.wait_ge(S("count_mm"), 1)
            in_tile = bank[:, 3, 64:64 + E * NR].rearrange("p (e r) -> p e r", r=NR)
            of_tile = bank[:, 3, 128:128 + E * NR]
            reset = vec[:, V_RESET:V_RESET + E * NR]

            def flat(x):
                return x.rearrange("p e r -> p (e r)")

            step(dve.tensor_tensor_scan(flat(c_t[:, 1]), reset, of_tile, 0.0, ALU.mult, ALU.add))
            step(tt(flat(c_t[:, 2]), flat(c_t[:, 1]), of_tile, ALU.subtract))
            step(tt(c_t[:, 3], c_t[:, 2], in_tile, ALU.add))
            step(stt(flat(c_t[:, 4]), flat(c_t[:, 3]), 1.0, flat(c_t[:, 0]), ALU.add, ALU.mult))
            step(ts(flat(c_t[:, 5]), flat(c_t[:, 4]), 1.0, None, ALU.subtract))

            iota = vec[:, V_IOTA:V_IOTA + SLOTS][:, None, :].to_broadcast([P, NR, SLOTS])

            def choose(t, slot):
                if not isinstance(t, int) or t >= 2:
                    dve.wait_ge(S("x_lo_mm"), t - 1)
                at_e = c_t[:, 5, t] if isinstance(t, int) else \
                    c_t[:, 5, bass.ds(t, 1)].rearrange("p a r -> p (a r)")
                tt(pick[:, slot], iota, at_e[:, :, None].to_broadcast([P, NR, SLOTS]), ALU.is_equal)\
                    .then_inc(S("pick"), 1)

            choose(0, 0)
            choose(1, 1)
            step(ts(c_s[:, 0], c_t[:, 1, :, NR - 1], float(SLOTS), None, ALU.is_gt))
            for k in range(2, OVE + 1):
                step(stt(c_s[:, 0], c_t[:, 1, :, NR - 1], float(k * SLOTS), c_s[:, 0], ALU.is_gt, ALU.add))
            step(dve.tensor_tensor_scan(c_s[:, 1], ones[:, 0:E], c_s[:, 0], 0.0, ALU.mult, ALU.add))
            step(tt(c_s[:, 2], c_s[:, 1], c_s[:, 0], ALU.subtract))
            step(stt(c_s[:, 3], c_s[:, 2], float(SLOTS), V(V_OVER, E), ALU.mult, ALU.add))
            step(stt(c_t[:, 6], c_t[:, 3], float(SLOTS), c_s[:, 3][:, :, None].to_broadcast([P, E, NR]),
                     ALU.is_ge, ALU.mult))
            step(tt(c_t[:, 7], c_t[:, 3], V(V_BASE, E)[:, :, None].to_broadcast([P, E, NR]), ALU.add))
            step(tt(c_t[:, 7], c_t[:, 7], c_t[:, 6], ALU.add))
            for j, hot in ((0, 4), (1, 7)):
                step(tt(r_t[:, 9 + j], r_t[:, hot], by_tile(c_t[:, 7]), ALU.mult))
                step(dve.tensor_reduce(rows[:, 2 + j], r_t[:, 9 + j], AX_X, ALU.add))
                step(tt(rows[:, j], rows[:, 2 + j], valid, ALU.mult))
            dve.tensor_copy(row_i[:, :], rows[:, 0:2]).then_inc(S("row_i"), 1)
            step(tt(e_f[:, :], c_s[0:1, 1][:, None, :].to_broadcast([1, OV, E]),
                    vec[0:1, V_IOTA:V_IOTA + OV][:, :, None].to_broadcast([1, OV, E]), ALU.is_le))
            step(dve.tensor_reduce(e_s[:, 0:OV], e_f[:, :], AX_X, ALU.add))
            step(ts(e_s[:, 0:OV], e_s[:, 0:OV], float(E - 1), None, ALU.min))
            step(dve.tensor_copy(e_s[:, OV:OV + 1], c_s[0:1, 1, E - 1:E]))
            dve.tensor_copy(e_tab[:, :], e_s[:, :]).then_inc(S("e_tab"), 1)
            dve.wait_ge(S("r_gexp"), 1)
            step(ts(r_s[:, 7], r_s[:, 6], 1.0, None, ALU.add))
            step(dve.reciprocal(r_s[:, 10], r_s[:, 7]))
            step(tt(r_s[:, 11], r_s[:, 6], r_s[:, 10], ALU.mult))
            step(ts(rows[:, 2:4], rows[:, 0:2], float(E * SLOTS), None, ALU.subtract))

            def x_low(t, slot):
                dve.wait_ge(S("x_lo_mm"), t + 1)
                dve.tensor_copy(x_lo[:, slot], bank[:, 1, 0:M * SLOTS].rearrange("p (m s) -> p m s", m=M))\
                   .then_inc(S("x_lo"), 1)

            def gate_up(t, slot):
                dve.wait_ge(S("act_g"), t + 1)
                dve.wait_ge(S("front"), t + 1)
                tt(fuse[:, slot].rearrange("p (b f) s -> p b (f s)", b=2),
                   act_g[:, slot].rearrange("p (b f) s -> p b (f s)", b=2),
                   bank[:, 4:6, 0:2 * SLOTS], ALU.mult).then_inc(S("fuse"), 1)
                dve.wait_ge(S("f_hi"), t + 1)
                tt(f_lo[:, slot], fuse[:, slot], f_hi[:, slot].bitcast(F32), ALU.subtract)\
                    .then_inc(S("f_lo"), 1)

            def results(t, slot, stored):
                dve.wait_ge(S("back"), t + 1)
                dve.wait_ge(S(f"y_stored{slot}"), stored)
                dve.tensor_copy(y_sb[:, slot],
                                bank[0:GR, 6 + slot, :].rearrange("p (g c) -> p g c", g=2))\
                   .then_inc(S("y_out"), 1)

            x_low(0, 0)
            gate_up(0, 0)
            x_low(1, 1)
            with dve.Fori(0, E // 2 - 1) as i:
                for slot in range(2):
                    t = i * 2 + slot
                    choose(t + 2, slot)
                    gate_up(t + 1, 1 - slot)
                    x_low(t + 2, slot)
                    results(t, slot, i * 16 + 16)
            gate_up(E - 1, 1)
            for slot in range(2):
                results(E - 2 + slot, slot, 16 * (E // 2))
            n_over = dve.value_load(e_tab[0:1, OV:OV + 1], min_val=0, max_val=OV)
            with dve.If(n_over > 0):
                with dve.Fori(0, n_over) as o:
                    dve.wait_ge(S("back"), o + E)
                    for j in range(2):
                        dst = (pick_a, pick_b)[j]
                        tt(dst[:, :], iota, rows[:, 2 + j][:, :, None].to_broadcast([P, NR, SLOTS]),
                           ALU.is_equal).then_inc(S("pick_ab"), 1)
                    dve.wait_ge(S("pick_ab"), o * 2 + 2)
                    tt(pick[:, 0], pick_a[:, :], pick_b[:, :], ALU.add).then_inc(S("pick"), 1)
                    ts(rows[:, 2:4], rows[:, 2:4], float(SLOTS), None, ALU.subtract).then_inc(S("rows"), 1)
                    dve.wait_ge(S("rows"), o + 1)
                    x_low(o + E, 0)
                    gate_up(o + E, 0)
                    results(o + E, 0, o * 16 + 16 * (E // 2 + 1))
            for r in range(NR):
                dve.wait_ge(S(f"y_tok{r}"), 32)
                step(ts(y_w[:, r], y_tok[:, r, 0], r_s[:, 10, r:r + 1], None, ALU.mult))
                stt(y_sum[:, r], y_tok[:, r, 1], r_s[:, 11, r:r + 1], y_w[:, r], ALU.mult, ALU.add)\
                    .then_inc(S("y_sum"), 1)
            for b, lo, hi, tiles in ((0, 0, NRT0 * P, NRT0), (M, NRT0 * P, B * T, NR)):
                dve.wait_ge(S("y_turned"), tiles)
                tt(h[:, :, lo:hi], h[:, :, lo:hi], bank[:, b:b + M, 0:hi - lo], ALU.add).then_inc(S("h2"), 1)

            for c in range(HALF):
                ln_xm(3, c, h, 4 + c)
            for c in range(HALF):
                ln_eps(3, c, 6 + c)
            for c in range(HALF):
                ln_n(3, c, 6 + c)

            def im(t):
                return t.rearrange("p (b t) -> p b t", t=T)

            for c in range(HALF):
                dve.wait_ge(S("hx_mm"), c + 1)
                for s in range(CONV):
                    for m in range(M):
                        base = V_CONV + m * CONV
                        if s == 0:
                            ts(xc[:, c, m], bank[:, 4 * c + m, 0:NT], V(base + CONV - 1), V(V_BCONV + m),
                               ALU.mult, ALU.add).then_inc(S("conv"), 1)
                            continue
                        dve.wait_ge(S("conv"), (c * CONV + s - 1) * M + m + 1)
                        stt(im(xc[:, c, m])[:, :, s:T], im(bank[:, 4 * c + m, 0:NT])[:, :, 0:T - s],
                            V(base + CONV - 1 - s), im(xc[:, c, m])[:, :, s:T], ALU.mult, ALU.add)\
                            .then_inc(S("conv"), 1)
            for c in range(HALF):
                dve.wait_ge(S("sig_i"), M * (c + 1))
                tt(upd[:, c], sig_i[:, c], xc[:, c], ALU.mult).then_inc(S("upd0"), 1)
            for c in range(HALF):
                dve.wait_ge(S("alpha"), M * (c + 1))
                step(tt(asq[:, c], alpha[:, c], alpha[:, c], ALU.mult))
                ts(asq[:, c], asq[:, c], -1.0, 1.0, ALU.mult, ALU.add).then_inc(S("one_minus"), 1)
                dve.memset(alpha[:, c].rearrange("p m (b t) -> p (m b) t", t=T)[:, :, 0:1], 0.0)\
                    .then_inc(S("alpha0"), 1)
            for c in range(HALF):
                dve.wait_ge(S("beta"), c + 1)
                step(tt(upd[:, c], upd[:, c], beta[:, c], ALU.mult))
                dve.wait_ge(S("alpha0"), c + 1)
                step(dve.tensor_tensor_scan(hst[:, c].rearrange("p m n -> p (m n)"),
                                            alpha[:, c].rearrange("p m n -> p (m n)"),
                                            upd[:, c].rearrange("p m n -> p (m n)"),
                                            0.0, ALU.mult, ALU.add))
                dve.wait_ge(S("gelu_g"), c + 1)
                tt(hst[:, c], hst[:, c], gelu_g[:, c], ALU.mult).then_inc(S("hawk_y"), 1)
            for c in range(HALF):
                residual("h3", "hawk_mm", c, 4 * c)
            for c in range(HALF):
                ln_xm(4, c, h, 4 * c + 2)
            for c in range(HALF):
                ln_eps(4, c, 4 * c + 3)
            for c in range(HALF):
                ln_n(4, c, 4 * c + 3)
                dve.wait_ge(S(f"ln_n{c}"), 5)
                step(dve.tensor_reduce(amax[:, c:c + 1], half(n, c), mybir.AxisListType.XY, ALU.max,
                                       apply_absolute_value=True))
            tt(amax[:, 2:3], amax[:, 0:1], amax[:, 1:2], ALU.max).then_inc(S("amax"), 1)
            dve.wait_ge(S("amax_all"), 1)
            step(ts(amax[:, 4:5], amax[:, 3:4], 1.0 / 127.0, EPS, ALU.mult, ALU.max))
            step(dve.reciprocal(amax[:, 5:6], amax[:, 4:5]))
            for c in range(HALF):
                step(ts(q1[:, c], half(n, c), amax[:, 5:6], 127.0, ALU.mult, ALU.min))
                step(ts(q2[:, c], q1[:, c], -128.0, ROUND, ALU.max, ALU.add))
                ts(qx[:, c], q2[:, c], ROUND, None, ALU.subtract).then_inc(S("qx"), 1)
            for c in range(HALF):
                dve.wait_ge(S("int_mm"), c + 1)
                for m in range(M):
                    step(ts(y1[:, c, m], bank[:, 2 * c + m, 0:NT], amax[:, 4:5], V(V_WSCALE + m),
                            ALU.mult, ALU.mult))
                    stt(y[:, c, m], y1[:, c, m], V(V_BIAS + m), half(h, c)[:, m], ALU.add, ALU.add)\
                        .then_inc(S("y"), 1)

        @block.tensor
        def _(pe):
            def mm(o, w, x, start, stop):
                return pe.matmul(o, w, x, start=start, stop=stop)

            def linear(o, w, x, kt):
                for k in range(kt):
                    r = mm(o, w(k), x(k), k == 0, k == kt - 1)
                return r

            def ln_mean(L, c, src, mb):
                linear(bank[:, mb, 0:NT], lambda k: mean_w[:, :], lambda k: half(src, c)[:, k], M)\
                    .then_inc(S(f"ln_mean{c}"), 1)

            def ln_var(L, c, vb):
                pe.wait_ge(S(f"ln_sq{c}"), L + 1)
                for q in range(NRH):
                    o = c * NT + q * RT
                    r = linear(bank[0:RT, vb, q:q + 1], lambda k: xsq[:, k, o:o + RT],
                               lambda k: mean_w[:, 0:1], M)
                r.then_inc(S(f"ln_var{c}"), 1)

            def ln_spread(L, c, vb):
                pe.wait_ge(S(f"ln_rstd{c}"), L + 1)
                for q in range(NRH):
                    r = mm(bank[:, vb, SPREAD + q * RT:SPREAD + (q + 1) * RT],
                           rstd[:, c, q:q + 1].to_broadcast([RT, P]), ident[0:RT, 0:RT], True, True)
                r.then_inc(S(f"ln_bc{c}"), 1)

            def project(w, m0, c, b0, src=n):
                for m in range(M):
                    r = linear(bank[:, b0 + m, 0:NT], lambda k: w[:, k, m0 + m * P:m0 + (m + 1) * P],
                               lambda k: half(src, c)[:, k], M)
                return r

            pe.wait_ge(S("wl_in"), 16)
            for c in range(HALF):
                pe.wait_ge(S(f"xp{c}_in"), 16)
                for m in range(M):
                    r = linear(bank[:, 2 * c + m, 0:NP], lambda k: wl[:, k, m * P:(m + 1) * P],
                               lambda k: xp[:, c, k], KE)
                r.then_inc(S("emb_mm"), 1)
            pe.wait_ge(S("mean_w"), 1)
            pe.wait_ge(S("cls"), 1)
            for c in range(HALF):
                pe.wait_ge(S("emb"), M * (c + 1))
                ln_mean(0, c, h, 4 + c)
            pe.wait_ge(S("ident"), 1)
            for c in range(HALF):
                ln_var(0, c, 6 + c)
            for c in range(HALF):
                ln_spread(0, c, 6 + c)
            pe.wait_ge(S("wq_in"), 16)
            pe.wait_ge(S("wb_in"), 16)
            for c in range(HALF):
                pe.wait_ge(S(f"ln_n{c}"), 1)
                if c:
                    pe.wait_ge(S("v_chan"), c)
                project(wq, D, c, 0).then_inc(S("k_mm"), 1)
                if c:
                    pe.wait_ge(S("silu_g"), c)
                project(wq, 0, c, 2).then_inc(S("q_mm"), 1)
                pe.wait_ge(S("k_chan"), c + 1)
                project(wq, 2 * D, c, 0).then_inc(S("v_mm"), 1)
                linear(bank[0:NH, 4 + c, 0:NT], lambda k: wb[:, k], lambda k: half(n, c)[:, k], M)\
                    .then_inc(S("b_mm"), 1)
                pe.wait_ge(S("q_chan"), c + 1)
                project(wq, 3 * D, c, 2).then_inc(S("g_mm"), 1)

            def att_sum(c, I):
                s = c * NI + I
                pe.wait_ge(S("read"), s + 1)
                o = bank[:, 2 * c + I // 2, (I % 2) * IB * T:(I % 2 + 1) * IB * T]\
                    .rearrange("p (i t) -> p i t", t=T)
                for j in range(HD):
                    r = mm(o, ident[:, :], state[:, s % 2, :, j], j == 0, j == HD - 1)
                r.then_inc(S("att_part"), 1)
                if I % 2 == 1:
                    pe.wait_ge(S("att_part"), s + 1)
                    pe.nop().then_inc(S("att_mm"), 1)

            def out_proj(c):
                pe.wait_ge(S("gated"), c + 1)
                if c == 0:
                    pe.wait_ge(S("wo_in"), 16)
                project(wo, 0, c, 2 * c).then_inc(S("wo_mm"), 1)

            pe.wait_ge(S("ident"), 1)
            pe.wait_ge(S("v_chan"), HALF)
            for I in range(NI):
                att_sum(0, I)
            pe.wait_ge(S("silu_g"), HALF)
            pe.wait_ge(S("b_chan"), HALF)
            att_sum(1, 0)
            pe.wait_ge(S("och0"), 16 * M)
            ln_mean(1, 0, och, 4)
            ln_var(1, 0, 6)
            att_sum(1, 1)
            ln_spread(1, 0, 6)
            out_proj(0)
            att_sum(1, 2)
            att_sum(1, 3)
            pe.wait_ge(S("h1"), 1)
            ln_mean(2, 0, h, 4)
            ln_var(2, 0, 6)
            ln_spread(2, 0, 6)
            pe.wait_ge(S("och1"), 16 * M)
            ln_mean(1, 1, och, 5)
            ln_var(1, 1, 7)
            ln_spread(1, 1, 7)
            out_proj(1)
            pe.wait_ge(S("h1"), 2)
            ln_mean(2, 1, h, 5)
            ln_var(2, 1, 7)
            ln_spread(2, 1, 7)

            pe.wait_ge(S("wr_in"), 16)
            pe.wait_ge(S("n_pad"), 1)
            for c in range(HALF):
                pe.wait_ge(S(f"ln_n{c}"), 3)
            for r_ in range(NR):
                r = linear(bank[:, 3, r_ * E:(r_ + 1) * E],
                           lambda k: n[:, k, r_ * P:(r_ + 1) * P], lambda k: wr[:, k], M)
            r.then_inc(S("router_mm"), 1)
            for r_ in range(NR):
                for m in range(M):
                    o = (r_ % 2) * D + m * P
                    r = pe.transpose(bank[:, r_ // 2, o:o + P], n[:, m, r_ * P:(r_ + 1) * P], ident[:, :])
            r.then_inc(S("tok_mm"), 1)
            pe.wait_ge(S("before"), 1)
            pe.wait_ge(S("chosen"), 1)
            chosen = c_t[:, 0].rearrange("p e r -> p (e r)")
            mm(bank[:, 3, 64:64 + E * NR], before[:, :], chosen, True, True)
            mm(bank[:, 3, 128:128 + E * NR], ones[:, :], chosen, True, True).then_inc(S("count_mm"), 1)
            pe.nop().then_inc(S("y_out"), 2)

            def gather(t, slot):
                pe.wait_ge(S("pick"), t + 1)
                for part, src, b in (("x_hi", tok_hi, 0), ("x_lo", tok_lo, 1)):
                    if not (isinstance(t, int) and t == 0):
                        pe.wait_ge(S(part), t)
                    for m in range(M):
                        for r_ in range(NR):
                            r = mm(bank[:, b, m * SLOTS:(m + 1) * SLOTS], src[:, r_, m * P:(m + 1) * P],
                                   pick[:, slot, r_], r_ == 0, r_ == NR - 1)
                    r.then_inc(S(part + "_mm"), 1)

            def three(o, w, x, start, stop):
                mm(o, w[0], x[0], start, False)
                mm(o, w[0], x[1], False, False)
                return mm(o, w[1], x[0], False, stop)

            def front(t, slot):
                pe.wait_ge(S("x_hi"), t + 1)
                pe.wait_ge(S("x_lo"), t + 1)
                first = isinstance(t, int) and t == 0
                for what, b0, done in ((0, 2, "act_g"), (1, 4, "fuse")):
                    if not first:
                        pe.wait_ge(S(done), t)
                    for f in range(FCH):
                        if what == 0:
                            pe.wait_ge(S("w_split"), t * PIECES + (f + 1))
                        for k in range(M):
                            o = (what * M + k) * P
                            r = three(bank[:, b0 + f // 2, (f % 2) * SLOTS:(f % 2 + 1) * SLOTS],
                                      (w_hi[:, slot, f, o:o + P], w_lo[:, slot, f, o:o + P]),
                                      (x_hi[:, slot, k], x_lo[:, slot, k]), k == 0, k == M - 1)
                    r.then_inc(S("front" if what else "gate_mm"), 1)

            def back(t, slot, left):
                pe.wait_ge(S("f_lo"), t + 1)
                pe.wait_ge(S("w_split"), t * PIECES + PIECES)
                pe.wait_ge(S("y_out"), left)
                for g in range(2):
                    for f in range(FCH):
                        p, o = GU + f // 2, (f % 2) * D
                        r = three(bank[0:GR, 6 + slot, g * D:(g + 1) * D],
                                  (f_hi[:, slot, f, g * GR:(g + 1) * GR], f_lo[:, slot, f, g * GR:(g + 1) * GR]),
                                  (w_hi[:, slot, p, o:o + D], w_lo[:, slot, p, o:o + D]), f == 0, f == FCH - 1)
                r.then_inc(S("back"), 1)

            pe.wait_ge(S("tok_lo"), 2)
            gather(0, 0)
            front(0, 0)
            gather(1, 1)
            with pe.Fori(0, E // 2 - 1) as i:
                for slot in range(2):
                    t = i * 2 + slot
                    front(t + 1, 1 - slot)
                    gather(t + 2, slot)
                    back(t, slot, t + 1)
            front(E - 1, 1)
            back(E - 2, 0, E - 1)
            back(E - 1, 1, E)
            pe.wait_ge(S("e_tab"), 1)
            n_over = pe.value_load(e_tab[0:1, OV:OV + 1], min_val=0, max_val=OV)
            with pe.If(n_over > 0):
                with pe.Fori(0, n_over) as o:
                    gather(o + E, 0)
                    front(o + E, 0)
                    back(o + E, 0, o + E + 2)
            for r_ in range(NR):
                pe.wait_ge(S("y_sum"), r_ + 1)
                rows_ = min(P, B * T - r_ * P)
                for m in range(M):
                    b, o = m + M * (r_ // NRT0), (r_ % NRT0) * P
                    r = pe.transpose(bank[:, b, o:o + rows_],
                                     y_sum[0:rows_, r_, m * P:(m + 1) * P], ident[0:rows_, 0:rows_])
                r.then_inc(S("y_turned"), 1)

            for c in range(HALF):
                pe.wait_ge(S("h2"), c + 1)
                ln_mean(3, c, h, 4 + c)
            for c in range(HALF):
                ln_var(3, c, 6 + c)
            for c in range(HALF):
                ln_spread(3, c, 6 + c)
            pe.wait_ge(S("hawk_w_in"), 16 * 3)
            for c in range(HALF):
                pe.wait_ge(S(f"ln_n{c}"), 4)
                project(wi, D, c, 4 * c).then_inc(S("hx_mm"), 1)
                project(wi, 0, c, 4 * c + 2).then_inc(S("hgate_mm"), 1)
            for c in range(HALF):
                pe.wait_ge(S("conv"), CONV * M * (c + 1))
                for m in range(M):
                    r = linear(bank[:, 4 * c + m, 0:NT], lambda k: wg[:, k, m * P:(m + 1) * P],
                               lambda k: xc[:, c, k], M)
                r.then_inc(S("forget_mm"), 1)
                pe.wait_ge(S("gelu_g"), c + 1)
                for m in range(M):
                    r = linear(bank[:, 4 * c + 2 + m, 0:NT], lambda k: wg[:, k, D + m * P:D + (m + 1) * P],
                               lambda k: xc[:, c, k], M)
                r.then_inc(S("input_mm"), 1)
            for c in range(HALF):
                pe.wait_ge(S("hawk_y"), c + 1)
                for m in range(M):
                    r = linear(bank[:, 4 * c + m, 0:NT], lambda k: wh[:, k, m * P:(m + 1) * P],
                               lambda k: hst[:, c, k], M)
                r.then_inc(S("hawk_mm"), 1)
            for c in range(HALF):
                pe.wait_ge(S("h3"), c + 1)
                ln_mean(4, c, h, 4 * c + 2)
            for c in range(HALF):
                ln_var(4, c, 4 * c + 3)
            for c in range(HALF):
                ln_spread(4, c, 4 * c + 3)
            pe.wait_ge(S("w8b"), 1)
            for c in range(HALF):
                pe.wait_ge(S("qx"), c + 1)
                for m in range(M):
                    r = linear(bank[:, 2 * c + m, 0:NT], lambda k: w8b[:, k, m * P:(m + 1) * P],
                               lambda k: qx[:, c, k], M)
                r.then_inc(S("int_mm"), 1)


def _tiles(a):
    k, n = a.shape
    return a.reshape(k // 128, 128, n).transpose(1, 0, 2)


def kernel(**inputs):
    import numpy as np
    import concourse.bacc as bacc
    from concourse.bass_utils import run_bass_kernel_spmd

    a = {k: np.asarray(v) for k, v in inputs.items()}
    g = IMG // PATCH
    x = a["x"].reshape(HALF, BH, CIN, g, PATCH, g, PATCH).transpose(0, 2, 4, 6, 1, 3, 5)
    x = x.reshape(HALF, KE, P, NP).transpose(0, 2, 1, 3)

    def cols(v):
        return v.reshape(-1, P).T

    pos = a["L0_tok_position_embeddings"][0].reshape(T, M, P).transpose(2, 1, 0).reshape(P, M * T)
    conv = a["L1_attn_w_conv"].reshape(M, P, CONV).transpose(1, 0, 2).reshape(P, M * CONV)
    def every(v):
        return np.broadcast_to(np.asarray(v, np.float32), (P, len(v)))

    rank = every(np.arange(E, 0, -1))
    valid = (np.arange(TP) < B * T).astype(np.float32).reshape(NR, P).T
    reset = every(np.arange(E * NR) % NR != 0)
    base = every(np.arange(E) * SLOTS)
    over = every((E - 1 - np.arange(E)) * SLOTS)
    iota = every(np.arange(SLOTS))
    vecs = np.concatenate([
        cols(a["L0_tok_b_lin"]), cols(a["L0_tok_class_token"].reshape(D)), pos,
        cols(a["L0_attn_ln_g"]), cols(a["L0_attn_ln_b"]), conv, cols(a["L1_attn_b_conv"]),
        cols(a["L1_attn_b_gates"]), cols(a["L1_attn_forget_base"]),
        cols(a["L1_ffn_weight_scale"].reshape(D)), cols(a["L1_ffn_bias"]), rank, valid,
        reset, base, over, iota], axis=1)

    def up(w):
        return w.reshape(E, M, P, FCH, P).transpose(0, 2, 3, 1, 4).reshape(E, P, FCH, M * P)

    dn = a["L0_ffn_kernel_down_EFD"].reshape(E, FCH, P, D).transpose(0, 2, 1, 3)
    experts = np.concatenate([
        np.concatenate([up(a["L0_ffn_kernel_gating_EDF"]), up(a["L0_ffn_kernel_up_EDF"])], axis=3),
        dn.reshape(E, P, PIECES - GU, PW)], axis=2)
    arrays = {
        "patches": x,
        "w_lin": _tiles(a["L0_tok_W_lin"].T),
        "vecs": vecs,
        "w_qkvg": _tiles(np.concatenate([a["L0_attn_Wq"], a["L0_attn_Wk"], a["L0_attn_Wv"],
                                         a["L0_attn_Wg"]], axis=1)),
        "w_beta": _tiles(a["L0_attn_Wbeta"]),
        "w_attn_out": _tiles(a["L0_attn_Wout"]),
        "w_router": _tiles(a["L0_ffn_router_kernel_DE"]),
        "w_experts": experts,
        "w_in": _tiles(a["L1_attn_w_in"].T),
        "w_gates": _tiles(a["L1_attn_w_gates"].T),
        "w_hawk_out": _tiles(a["L1_attn_w_out"].T),
        "w_int8": np.ascontiguousarray(_tiles(a["L1_ffn_weight_int8"].T)).view(np.int32),
    }
    nc = bacc.Bacc("TRN2", target_bir_lowering=False, num_devices=1)
    args = []
    for name in arrays:
        arrays[name] = np.ascontiguousarray(arrays[name])
        args.append(nc.dram_tensor(name, arrays[name].shape, mybir.dt.from_np(arrays[name].dtype),
                                   kind="ExternalInput").ap())
    args.append(nc.dram_tensor("out", (P, M, B * T), F32, kind="ExternalOutput").ap())
    vit_tower(nc, *args)
    r = run_bass_kernel_spmd(nc, [arrays], core_ids=[0])
    o = r.results[0]["out"]
    return o.transpose(2, 1, 0).reshape(B, T, D)
```

```python
from contextlib import ExitStack

import concourse.bass as bass
from concourse import mybir

F32 = mybir.dt.float32
F32R = mybir.dt.float32r
BF16 = mybir.dt.bfloat16
I8 = mybir.dt.int8
I32 = mybir.dt.int32
U32 = mybir.dt.uint32
ALU = mybir.AluOpType
ACT = mybir.ActivationFunctionType
AX_X = mybir.AxisListType.X

P = 128
B = 16
IMG = 96
PATCH = 16
CIN = 3
NPATCH = (IMG // PATCH) ** 2
T = NPATCH + 1
D = 256
M = D // P
KE = CIN * PATCH * PATCH // P
NH = 16
HD = D // NH
E = 8
FF = 512
FCH = FF // P
TOPK_STEP = 2.0
CONV = 4
HALF = 2
BH = B // HALF
NT = BH * T
NP = BH * NPATCH
RT = 2 * T
NRT = B * T // RT
NRH = NRT // HALF
WARM_START, WARM_ATT, WARM_ATT_LAST, WARM_OUT = 11, 4, 6, 4
WARM_ROUTE, WARM_PLACE, WARM_RESULT, WARM_NORM, WARM_HAWK, WARM_INT = 14, 8, 8, 2, 8, 16
FOLD = 6
IB = 4
NI = HD // IB
EPS = 1e-5
ROUND = 12582912.0
SPREAD = 16
SLOTS = 208
GR = SLOTS // 2
TP = 640
NR = TP // P
NRT0 = (B * T // 2 + P - 1) // P
OV = (2 * B * T - 1) // SLOTS
OVE = (B * T + SLOTS - 1) // SLOTS - 1
ZREP = 4
ZCOLS = OV * SLOTS * D // P // ZREP
PW = 512
PIECES = 6
GU = FCH

V_BLIN = 0
V_CLS = V_BLIN + M
V_POS = V_CLS + M
V_LNG = V_POS + M * T
V_LNB = V_LNG + M
V_CONV = V_LNB + M
V_BCONV = V_CONV + M * CONV
V_BGATE = V_BCONV + M
V_FBASE = V_BGATE + 2 * M
V_WSCALE = V_FBASE + M
V_BIAS = V_WSCALE + M
V_RANK = V_BIAS + M
V_VALID = V_RANK + E
V_RESET = V_VALID + NR
V_BASE = V_RESET + E * NR
V_OVER = V_BASE + E
V_IOTA = V_OVER + E
V_ALL = V_IOTA + SLOTS


def vit_tower(nc, patches, w_lin, vecs, w_qkvg, w_beta, w_attn_out, w_router, w_experts,
              w_in, w_gates, w_hawk_out, w_int8, out):
    with ExitStack() as ctx:
        sems = {}

        def S(name):
            if name not in sems:
                sems[name] = ctx.enter_context(nc.semaphore(name))
            return sems[name]

        def sb(name, shape, dt=F32):
            return ctx.enter_context(nc.sbuf_tensor(name, shape, dt))

        by_head = nc.dram_tensor("by_head", (HALF, 3, BH, D, T), F32, kind="Internal").ap()
        beta_by_head = nc.dram_tensor("beta_by_head", (HALF, BH, NH, T), F32, kind="Internal").ap()
        sum_by_head = nc.dram_tensor("sum_by_head", (HALF, BH, D, T), F32, kind="Internal").ap()
        y_rows = nc.dram_tensor("y_rows", ((E + OV) * SLOTS, D), F32, kind="Internal").ap()
        bank = ctx.enter_context(nc.psum_tensor("bank", [P, 8, 512], F32))

        vec = sb("vec", [P, V_ALL])
        wl = sb("wl", [P, KE, D])
        wq = sb("wq", [P, M, 4 * D])
        wb = sb("wb", [P, M, NH])
        wo = sb("wo", [P, M, D])
        wr = sb("wr", [P, M, E])
        wi = sb("wi", [P, M, 2 * D])
        wg = sb("wg", [P, M, 2 * D])
        wh = sb("wh", [P, M, D])
        w8 = sb("w8", [P, M, D // 4], I32)
        w8b = sb("w8b", [P, M, D], BF16)
        mean_w = sb("mean_w", [P, P])
        ident = sb("ident", [P, P])
        posb = sb("posb", [P, M, T])
        h = sb("h", [P, M, B * T])
        xm = sb("xm", [P, M, B * T])
        xsq = sb("xsq", [P, M, TP])
        var = sb("var", [RT, HALF, NRH])
        rstd = sb("rstd", [RT, HALF, NRH])
        neg_half = sb("neg_half", [RT, NRH])
        n = sb("n", [P, M, TP])
        before = sb("before", [P, P])
        ones = sb("ones", [P, P])
        e_tab = sb("e_tab", [1, OV + 1], I32)
        sp = sb("sp", [P, 8, M])
        eps_ap = sb("eps_ap", [P, 1])
        silu_g = sb("silu_g", [P, M, TP])

        shared = ctx.enter_context(nc.sbuf_tensor("raw_place", [P, 2 * PIECES * PW], F32))
        raw = shared[:, :].rearrange("p (s k w) -> p s k w", s=2, w=PW)
        xp = shared[:, 0:HALF * KE * NP].rearrange("p (c k n) -> p c k n", c=HALF, k=KE)

        with ExitStack() as attn:
            def at(name, shape, dt=F32):
                return attn.enter_context(nc.sbuf_tensor(name, shape, dt))

            chan = at("chan", [P, 3, M, B * T])
            chan_b = at("chan_b", [NH, B * T])
            head = at("head", [P, HALF, 3, HD, T])
            head_b = at("head_b", [P, HALF, T])
            hsq = xsq[:, :, 0:HD * T].rearrange("p x (i t) -> p x i t", t=T)
            ssq = at("ssq", [P, HALF, 2, T])
            rnrm = at("rnrm", [P, HALF, 2, T])
            nrm = at("nrm", [P, HALF, 2, T])
            bk = at("bk", [P, HALF, HD, T])
            bv = at("bv", [P, HALF, HD, T])
            decay = at("decay", [P, HD, HD, T])
            write = at("write", [P, 3, IB, HD, T])
            state = at("state", [P, 2, IB, HD, T])
            att = chan[:, 1].rearrange("p c (i t) -> p c i t", t=T)
        och = chan[:, 0]
        gate_b = chan[:, 2]

        with ExitStack() as moe:
            def mo(name, shape, dt=F32):
                return moe.enter_context(nc.sbuf_tensor(name, shape, dt))

            w_hi = mo("w_hi", [P, 2, PIECES, PW], F32R)
            w_lo = mo("w_lo", [P, 2, PIECES, PW], F32R)
            tok_hi = mo("tok_hi", [P, NR, D], F32R)
            tok_lo = mo("tok_lo", [P, NR, D], F32R)
            pick = mo("pick", [P, 2, NR, SLOTS], F32R)
            pick_a = mo("pick_a", [P, NR, SLOTS])
            pick_b = mo("pick_b", [P, NR, SLOTS])
            x_hi = mo("x_hi", [P, 2, M, SLOTS], F32R)
            x_lo = mo("x_lo", [P, 2, M, SLOTS], F32R)
            act_g = mo("act_g", [P, 2, FCH, SLOTS])
            fuse = mo("fuse", [P, 2, FCH, SLOTS])
            f_hi = mo("f_hi", [P, 2, FCH, SLOTS], F32R)
            f_lo = mo("f_lo", [P, 2, FCH, SLOTS], F32R)
            y_sb = mo("y_sb", [GR, 2, 2, D])
            y_tok = mo("y_tok", [P, NR, 2, D])
            y_w = silu_g[:, :, :].rearrange("p m n -> p (m n)").rearrange("p (r c) -> p r c", c=D)
            y_sum = xsq[:, :, :].rearrange("p m n -> p (m n)").rearrange("p (r c) -> p r c", c=D)
            r_t = mo("r_t", [P, 12, NR, E])
            r_s = mo("r_s", [P, 12, NR])
            c_t = mo("c_t", [P, 8, E, NR])
            c_s = mo("c_s", [P, 6, E])
            rows = mo("rows", [P, 4, NR])
            row_i = mo("row_i", [P, 2, NR], U32)
            e_f = mo("e_f", [1, OV, E])
            e_s = mo("e_s", [1, OV + 1])

        with ExitStack() as hawk:
            def hk(name, shape, dt=F32):
                return hawk.enter_context(nc.sbuf_tensor(name, shape, dt))

            gelu_g = hk("gelu_g", [P, HALF, M, NT])
            xc = hk("xc", [P, HALF, M, NT])
            sig_f = hk("sig_f", [P, HALF, M, NT])
            sig_i = hk("sig_i", [P, HALF, M, NT])
            alpha = hk("alpha", [P, HALF, M, NT])
            asq = hk("asq", [P, HALF, M, NT])
            beta = hk("beta", [P, HALF, M, NT])
            upd = hk("upd", [P, HALF, M, NT])
            hst = hk("hst", [P, HALF, M, NT])
            amax = hk("amax", [P, 8])
            q1 = hk("q1", [P, HALF, M, NT])
            q2 = hk("q2", [P, HALF, M, NT])
            qx = hk("qx", [P, HALF, M, NT], BF16)
            y1 = hk("y1", [P, HALF, M, NT])
            y = hk("y", [P, HALF, M, NT])

        def half(t, c):
            return t[:, :, c * NT:(c + 1) * NT]

        def V(o, w=1):
            return vec[:, o:o + w]

        def by_image(t):
            return t.rearrange("p m (b t) -> p m b t", t=T)

        def pair(b0):
            return bank[:, b0:b0 + 2, 0:NT]

        def expert(e):
            return w_experts[bass.ds(e, 1)].rearrange("a p k w -> (a p) k w")

        def tile_rows(t):
            return y_rows[bass.ds(t * SLOTS, SLOTS)].rearrange("(g p) c -> p g c", g=2)

        block = ctx.enter_context(nc.Block())

        @block.sync
        def _(sp_):
            def load(dst, src, name):
                sp_.dma_start(dst, src).then_inc(S(name), 16)

            for k in range(2):
                ks = slice(k * KE // 2, (k + 1) * KE // 2)
                load(wl[:, ks], w_lin[:, ks], f"emb_in{k}")
                load(xp[:, 0, ks], patches[0, :, ks], f"emb_in{k}")
                if k == 0:
                    load(vec[:, :], vecs, "vec_in")
            load(xp[:, 1], patches[1], "xp1_in")
            load(wq[:, :, :], w_qkvg, "wq_in")
            load(wb[:, :, :], w_beta, "wb_in")
            load(wo[:, :, :], w_attn_out, "wo_in")
            load(wr[:, :, :], w_router, "wr_in")
            load(wi[:, :, :], w_in, "hawk_w_in")
            load(wg[:, :, :], w_gates, "hawk_w_in")
            load(wh[:, :, :], w_hawk_out, "hawk_w_in")
            load(w8[:, :, :], w_int8, "w8_in")
            sp_.wait_ge(S("zeros"), 1)
            sp_.dma_start(y_rows[E * SLOTS:, :].rearrange("r c -> (r c)").rearrange("(p z w) -> p z w", p=P, z=ZREP),
                          silu_g[:, 0, 0:ZCOLS][:, None, :].to_broadcast([P, ZREP, ZCOLS]))\
               .then_inc(S("y_zeroed"), 16)
            def spill(c, x, name):
                sp_.wait_ge(S(name), c + 1)
                for m in range(M):
                    sp_.dma_start(by_head[c, x, :, m * P:(m + 1) * P].rearrange("b p t -> p b t"),
                                  chan[:, x, m, c * NT:(c + 1) * NT].rearrange("p (b t) -> p b t", t=T))\
                       .then_inc(S(f"spill{c}{x}"), 16)

            def unspill(c, x):
                sp_.wait_ge(S(f"spill{c}{x}"), 16 * M)
                sp_.dma_start(head[:, c, x].rearrange("p i t -> p (i t)"),
                              by_head[c, x].rearrange("b (h i) t -> (b h) (i t)", i=HD))\
                   .then_inc(S(f"head{c}{x}"), 16)

            for c in range(HALF):
                spill(c, 0, "k_chan")
                spill(c, 1, "q_chan")
                unspill(c, 0)
                sp_.wait_ge(S("b_chan"), c + 1)
                sp_.dma_start(beta_by_head[c].rearrange("b h t -> h b t"),
                              chan_b[:, c * NT:(c + 1) * NT].rearrange("p (b t) -> p b t", t=T))\
                   .then_inc(S("spillb"), 16)
                unspill(c, 1)
                spill(c, 2, "v_chan")
                sp_.wait_ge(S("spillb"), 16 * (c + 1))
                sp_.dma_start(head_b[:, c], beta_by_head[c].rearrange("b h t -> (b h) t"))\
                   .then_inc(S(f"headb{c}"), 16)
                unspill(c, 2)
            sp_.wait_ge(S("emb_mm"), HALF)
            for g in range(2):
                sp_.dma_start(raw[:, g], w_experts[g]).then_inc(S(f"raw{g}"), 16)
            for c in range(HALF):
                sp_.wait_ge(S("att_out"), 2 * (c + 1))
                sp_.dma_start(sum_by_head[c].rearrange("b (h i) t -> (b h) (i t)", i=HD),
                              att[:, c].rearrange("p i t -> p (i t)")).then_inc(S("spillo"), 16)
                sp_.wait_ge(S("spillo"), 16 * (c + 1))
                for m in range(M):
                    sp_.dma_start(och[:, m, c * NT:(c + 1) * NT].rearrange("p (b t) -> p b t", t=T),
                                  sum_by_head[c, :, m * P:(m + 1) * P].rearrange("b p t -> p b t"))\
                       .then_inc(S(f"och{c}"), 16)
            for g in range(2):
                sp_.nop().then_inc(S(f"y_stored{g}"), 16)

            def store(t, slot):
                sp_.wait_ge(S("y_out"), t + 3)
                sp_.dma_start(tile_rows(t), y_sb[:, slot]).then_inc(S(f"y_stored{slot}"), 16)

            def reload(t, slot):
                sp_.wait_ge(S("w_split"), (t + 1) * PIECES)
                sp_.dma_start(raw[:, slot], expert(t + 2)).then_inc(S(f"raw{slot}"), 16)

            reload(0, 0)
            with sp_.Fori(0, E // 2 - 2) as i:
                for slot in range(2):
                    reload(i * 2 + slot + 1, 1 - slot)
                    store(i * 2 + slot, slot)
            reload(E - 3, 1)
            for t in range(E - 4, E):
                store(t, t % 2)
            sp_.wait_ge(S("e_tab"), 1)
            n_over = sp_.value_load(e_tab[0:1, OV:OV + 1], min_val=0, max_val=OV)
            with sp_.If(n_over > 0):
                with sp_.Fori(0, n_over) as o:
                    sp_.wait_ge(S("w_split"), o * PIECES + E * PIECES)
                    e = sp_.value_load(e_tab[0:1, bass.ds(o, 1)], min_val=0, max_val=E - 1)
                    sp_.dma_start(raw[:, 0], expert(e)).then_inc(S("raw0"), 16)
                    store(o + E, 0)
            for c in range(HALF):
                sp_.wait_ge(S("y"), M * (c + 1))
                sp_.dma_start(out[:, :, c * NT:(c + 1) * NT], y[:, c]).then_inc(S("stored"), 16)
            sp_.wait_ge(S("stored"), 16 * HALF)

        @block.gpsimd
        def _(pool):
            pool.memset(mean_w[:, :], 1.0 / D).then_inc(S("mean_w"), 1)
            pool.memset(ident[:, :], 0.0).then_inc(S("ident0"), 1)
            pool.wait_ge(S("ident0"), 1)
            pool.affine_select(out=ident[:, :], in_=ident[:, :], compare_op=ALU.not_equal, fill=1.0,
                               base=0, pattern=[[-1, P]], channel_multiplier=1).then_inc(S("ident"), 1)
            pool.memset(decay[:, :, :, 0:1], 0.0).then_inc(S("decay0"), 1)
            pool.memset(silu_g[:, 0, 0:ZCOLS], 0.0).then_inc(S("zeros"), 1)
            pool.memset(ones[:, :], 1.0).then_inc(S("ones"), 1)
            pool.wait_ge(S("ones"), 1)
            pool.affine_select(out=before[:, :], in_=ones[:, :], compare_op=ALU.is_gt, fill=0.0,
                               base=0, pattern=[[1, P]], channel_multiplier=-1).then_inc(S("before"), 1)
            pool.memset(n[:, :, B * T:TP], 0.0).then_inc(S("n_pad"), 1)
            pool.memset(neg_half[:, :], -0.5).then_inc(S("neg_half"), 1)
            pool.wait_ge(S("neg_half"), 1)

            def ln_rstd(L, c):
                pool.wait_ge(S(f"ln_eps{c}"), L + 1)
                pool.tensor_tensor(rstd[:, c], var[:, c], neg_half[:, :], ALU.pow)\
                    .then_inc(S(f"ln_rstd{c}"), 1)

            for c in range(HALF):
                ln_rstd(0, c)
            pool.wait_ge(S("w8_in"), 16)
            pool.tensor_copy(w8b[:, :, :], w8[:, :, :].bitcast(I8)).then_inc(S("w8b"), 1)
            def head_scales(c):
                pool.wait_ge(S("head_beta"), c + 1)
                pool.wait_ge(S(f"head{c}2"), 16)
                pool.tensor_tensor(bv[:, c], head[:, c, 2],
                                   head_b[:, c][:, None, :].to_broadcast([P, HD, T]), ALU.mult)\
                    .then_inc(S("bv"), 1)

            def writes(s):
                c, I = s // NI, s % NI
                pool.wait_ge(S("khat"), c + 1)
                pool.wait_ge(S("bv"), c + 1)
                if s >= 3:
                    pool.wait_ge(S("state"), s - 2)
                pool.tensor_tensor(
                    write[:, s % 3],
                    bv[:, c, I * IB:(I + 1) * IB][:, :, None, :].to_broadcast([P, IB, HD, T]),
                    head[:, c, 0][:, None, :, :].to_broadcast([P, IB, HD, T]),
                    ALU.mult).then_inc(S("write"), 1)

            def fold(s):
                pool.wait_ge(S("read"), s + 1)
                o = state[:, s % 2, :, 0:FOLD]
                pool.tensor_tensor(o, o, state[:, s % 2, :, HD - FOLD:HD], ALU.add).then_inc(S("fold"), 1)

            head_scales(0)
            for s in range(3):
                writes(s)
            head_scales(1)
            for s in range(4):
                fold(s)
                writes(s + 3)
            fold(4)
            fold(5)
            writes(7)
            fold(6)
            ln_rstd(1, 0)
            ln_rstd(2, 0)
            ln_rstd(1, 1)
            ln_rstd(2, 1)

            def split(t, slot):
                for p in range(PIECES):
                    pool.wait_ge(S("w_hi"), t * PIECES + (p + 1))
                    pool.tensor_tensor(w_lo[:, slot, p], raw[:, slot, p], w_hi[:, slot, p].bitcast(F32),
                                       ALU.subtract).then_inc(S("w_split"), 1)

            with pool.Fori(0, E // 2) as i:
                for slot in range(2):
                    split(i * 2 + slot, slot)
            pool.wait_ge(S("e_tab"), 1)
            n_over = pool.value_load(e_tab[0:1, OV:OV + 1], min_val=0, max_val=OV)
            with pool.If(n_over > 0):
                with pool.Fori(0, n_over) as o:
                    split(o + E, 0)
                    pool.wait_ge(S("y_stored0"), o * 16 + 16 * (E // 2 + 2))
            for slot in range(2):
                pool.wait_ge(S(f"y_stored{slot}"), 16 * (E // 2 + 1))
            pool.wait_ge(S("y_zeroed"), 16)
            pool.wait_ge(S("row_i"), 1)
            for r in range(NR):
                for j in range(2):
                    pool.indirect_dma_start(
                        out=y_tok[:, r, j], out_offset=None, in_=y_rows,
                        in_offset=bass.IndirectOffsetOnAxis(ap=row_i[:, j, r:r + 1], axis=0))\
                        .then_inc(S(f"y_tok{r}"), 16)
            for L in (3, 4):
                for c in range(HALF):
                    ln_rstd(L, c)
            pool.wait_ge(S("amax"), 1)
            pool.partition_all_reduce(amax[:, 3:4], amax[:, 2:3], P, bass.bass_isa.ReduceOp.max)\
                .then_inc(S("amax_all"), 1)

        @block.scalar
        def _(act):
            def ln_sq(L, c):
                act.wait_ge(S(f"ln_xm{c}"), L + 1)
                act.activation(half(xsq, c), half(xm, c), ACT.Square).then_inc(S(f"ln_sq{c}"), 1)

            act.wait_ge(S("sp_abs"), 1)
            act.activation(sp[:, 1], sp[:, 0], ACT.Exp, scale=-1.0).then_inc(S("sp_exp"), 1)
            act.wait_ge(S("eps"), 1)
            for c in range(HALF):
                ln_sq(0, c)

            def prep(c):
                act.wait_ge(S(f"headb{c}"), 16)
                act.activation(head_b[:, c], head_b[:, c], ACT.Sigmoid).then_inc(S("head_beta"), 1)
                act.wait_ge(S("ssq"), c + 1)
                act.activation(nrm[:, c], ssq[:, c], ACT.Sqrt).then_inc(S("nrm"), 1)

            for c in range(HALF):
                for x, (name, b0) in enumerate((("k_chan", 0), ("q_chan", 2), ("v_chan", 0))):
                    act.wait_ge(S(name.replace("chan", "mm")), c + 1)
                    act.copy(half(chan[:, x], c), pair(b0)).then_inc(S(name), 1)
                    if c == 1 and x == 1:
                        prep(0)
                act.wait_ge(S("b_mm"), c + 1)
                act.copy(chan_b[:, c * NT:(c + 1) * NT], bank[0:NH, 4 + c, 0:NT]).then_inc(S("b_chan"), 1)


            def decay_rows(c, I):
                act.wait_ge(S("kk"), c * NI + I + 1)
                rows_ = slice(I * IB, (I + 1) * IB)
                act.activation(decay[:, rows_, I * IB:HD, 1:T], decay[:, rows_, I * IB:HD, 1:T],
                               ACT.Identity, scale=-1.0, bias=1.0).then_inc(S("decay"), 1)
                if I:
                    act.wait_ge(S("decay"), c * NI + I)
                    act.copy(decay[:, rows_, 0:I * IB, 1:T],
                             decay[:, 0:I * IB, rows_, 1:T].rearrange("p j i t -> p i j t"))\
                       .then_inc(S("decay_mirror"), 1)

            def att_evac(c, I):
                act.wait_ge(S("att_part"), c * NI + I + 1)
                act.copy(att[:, c, (I - 1) * IB:(I + 1) * IB],
                         bank[:, 2 * c + I // 2, 0:2 * IB * T].rearrange("p (i t) -> p i t", t=T))\
                   .then_inc(S("att_out"), 1)

            act.wait_ge(S("decay0"), 1)
            for I in range(NI):
                decay_rows(0, I)
            prep(1)
            decay_rows(1, 0)
            for c in range(HALF):
                act.wait_ge(S("g_chan"), c + 1)
                act.activation(half(silu_g, c), half(silu_g, c), ACT.Silu).then_inc(S("silu_g"), 1)
            for c in range(HALF):
                act.wait_ge(S("silu_g"), c + 1)
                act.wait_ge(S(f"head{c}2"), 16)
                for m in range(M):
                    act.activation(half(gate_b, c)[:, m], half(silu_g, c)[:, m], ACT.Copy, scale=V(V_LNB + m))\
                       .then_inc(S("gate_ln"), 1)
                for m in range(M):
                    act.activation(half(silu_g, c)[:, m], half(silu_g, c)[:, m], ACT.Copy, scale=V(V_LNG + m))\
                       .then_inc(S("gate_ln"), 1)
            for c in range(HALF):
                act.wait_ge(S(f"head{c}1"), 16)
            att_evac(0, 1)
            for I in range(1, NI):
                decay_rows(1, I)
            att_evac(0, 3)
            ln_sq(1, 0)
            att_evac(1, 1)
            att_evac(1, 3)
            ln_sq(2, 0)
            ln_sq(1, 1)
            ln_sq(2, 1)

            def w_high(t, slot, pieces):
                for p in pieces:
                    act.copy(w_hi[:, slot, p], raw[:, slot, p]).then_inc(S("w_hi"), 1)

            act.wait_ge(S("gated"), HALF)
            act.wait_ge(S("raw0"), 16)
            w_high(0, 0, range(PIECES))
            act.wait_ge(S("r_diff"), 1)
            act.activation(r_t[:, 1], r_t[:, 0], ACT.Exp).then_inc(S("r_exp"), 1)
            act.wait_ge(S("tok_mm"), 1)
            act.copy(tok_hi[:, 0:4].rearrange("p (b r) c -> p b (r c)", b=2), bank[:, 0:2, :])\
               .then_inc(S("tok_hi"), 1)
            act.copy(tok_hi[:, 4], bank[:, 2, 0:D]).then_inc(S("tok_hi"), 1)
            act.wait_ge(S("r_gap"), 1)
            act.activation(r_s[:, 6], r_s[:, 5], ACT.Exp).then_inc(S("r_gexp"), 1)
            act.wait_ge(S("raw1"), 16)
            w_high(1, 1, range(PIECES))

            def x_high(t, slot):
                act.wait_ge(S("x_hi_mm"), t + 1)
                act.copy(x_hi[:, slot], bank[:, 0, 0:M * SLOTS].rearrange("p (m s) -> p m s", m=M))\
                   .then_inc(S("x_hi"), 1)

            def silu(t, slot):
                act.wait_ge(S("gate_mm"), t + 1)
                act.activation(act_g[:, slot].rearrange("p (b f) s -> p b (f s)", b=2),
                               bank[:, 2:4, 0:2 * SLOTS], ACT.Silu).then_inc(S("act_g"), 1)

            def f_high(t, slot):
                act.wait_ge(S("fuse"), t + 1)
                act.copy(f_hi[:, slot], fuse[:, slot]).then_inc(S("f_hi"), 1)

            x_high(0, 0)
            silu(0, 0)
            f_high(0, 0)
            x_high(1, 1)
            with act.Fori(0, E // 2 - 1) as i:
                for slot in range(2):
                    t = i * 2 + slot
                    act.wait_ge(S(f"raw{slot}"), i * 16 + 32)
                    act.wait_ge(S("front"), t + 1)
                    w_high(t + 2, slot, range(GU))
                    silu(t + 1, 1 - slot)
                    f_high(t + 1, 1 - slot)
                    x_high(t + 2, slot)
                    act.wait_ge(S("back"), t + 1)
                    w_high(t + 2, slot, range(GU, PIECES))
            silu(E - 1, 1)
            f_high(E - 1, 1)
            act.wait_ge(S("e_tab"), 1)
            n_over = act.value_load(e_tab[0:1, OV:OV + 1], min_val=0, max_val=OV)
            with act.If(n_over > 0):
                with act.Fori(0, n_over) as o:
                    act.wait_ge(S("raw0"), o * 16 + 16 * (E // 2 + 1))
                    act.wait_ge(S("back"), o + E)
                    w_high(o + E, 0, range(PIECES))
                    x_high(o + E, 0)
                    silu(o + E, 0)
                    f_high(o + E, 0)

            for c in range(HALF):
                ln_sq(3, c)
            for c in range(HALF):
                act.wait_ge(S("hx_mm"), c + 1)
                for m in range(M):
                    act.activation(xc[:, c, m], bank[:, 4 * c + m, 0:NT], ACT.Identity,
                                   scale=V(V_CONV + m * CONV + CONV - 1), bias=V(V_BCONV + m))\
                       .then_inc(S("conv0"), 1)
                act.wait_ge(S("hgate_mm"), c + 1)
                act.activation(gelu_g[:, c], pair(4 * c + 2), ACT.Gelu).then_inc(S("gelu_g"), 1)
            for c in range(HALF):
                for m in range(M):
                    act.wait_ge(S("forget_mm"), c + 1)
                    act.activation(sig_f[:, c, m], bank[:, 4 * c + m, 0:NT], ACT.Tanh, scale=0.5,
                                   bias=sp[:, 1, m:m + 1]).then_inc(S("sig_f"), 1)
                for m in range(M):
                    act.wait_ge(S("sig_f"), M * c + m + 1)
                    act.activation(alpha[:, c, m], sig_f[:, c, m], ACT.Exp, scale=sp[:, 7, m:m + 1],
                                   bias=sp[:, 7, m:m + 1]).then_inc(S("alpha"), 1)
                for m in range(M):
                    act.wait_ge(S("input_mm"), c + 1)
                    act.activation(sig_i[:, c, m], bank[:, 4 * c + 2 + m, 0:NT], ACT.Tanh, scale=0.5,
                                   bias=sp[:, 3, m:m + 1]).then_inc(S("sig_i"), 1)
            for c in range(HALF):
                act.wait_ge(S("one_minus"), c + 1)
                act.activation(beta[:, c], asq[:, c], ACT.Sqrt, bias=eps_ap[:, :]).then_inc(S("beta"), 1)
            for c in range(HALF):
                ln_sq(4, c)
            act.wait_ge(S("out_scale"), 1)
            for c in range(HALF):
                act.wait_ge(S("int_mm"), c + 1)
                for m in range(M):
                    act.activation(y1[:, c, m], bank[:, 2 * c + m, 0:NT], ACT.Identity,
                                   scale=amax[:, 6 + m:7 + m], bias=V(V_BIAS + m)).then_inc(S("y1"), 1)

        @block.vector
        def _(dve):
            tt = dve.tensor_tensor
            ts = dve.tensor_scalar
            stt = dve.scalar_tensor_tensor
            steps = [0]

            def step(ins):
                ins.then_inc(S("dve_step"), 1)
                steps[0] += 1
                dve.wait_ge(S("dve_step"), steps[0])

            def ln_xm(L, c, src, mb):
                dve.wait_ge(S(f"ln_mean{c}"), L + 1)
                tt(half(xm, c), half(src, c),
                   bank[:, mb, 0:NT][:, None, :].to_broadcast([P, M, NT]), ALU.subtract)\
                    .then_inc(S(f"ln_xm{c}"), 1)

            def ln_eps(L, c, vb):
                dve.wait_ge(S(f"ln_var{c}"), L + 1)
                ts(var[:, c], bank[0:RT, vb, 0:NRH], EPS, None, ALU.add).then_inc(S(f"ln_eps{c}"), 1)

            def ln_n(L, c, vb):
                dve.wait_ge(S(f"ln_bc{c}"), L + 1)
                tt(half(n, c), half(xm, c),
                   bank[:, vb, SPREAD:SPREAD + NT][:, None, :].to_broadcast([P, M, NT]), ALU.mult)\
                    .then_inc(S(f"ln_n{c}"), 1)

            dve.memset(eps_ap[:, :], 1e-6).then_inc(S("eps"), 1)
            dve.wait_ge(S("vec_in"), 16)
            fb = V(V_FBASE, M)
            stt(sp[:, 0], fb, -1.0, fb, ALU.mult, ALU.max).then_inc(S("sp_abs"), 1)
            pos = V(V_POS, M * T).rearrange("p (m t) -> p m t", t=T)
            step(tt(posb[:, :, 1:T], pos[:, :, 1:T], V(V_BLIN, M)[:, :, None].to_broadcast([P, M, NPATCH]),
                    ALU.add))
            step(tt(posb[:, :, 0:1], pos[:, :, 0:1], V(V_CLS, M)[:, :, None], ALU.add))
            hi_ = by_image(h[:, :, :])
            dve.tensor_copy(hi_[:, :, :, 0], posb[:, :, 0:1].to_broadcast([P, M, B])).then_inc(S("cls"), 1)
            dve.wait_ge(S("sp_exp"), 1)
            step(ts(sp[:, 2], sp[:, 1], 2.0, None, ALU.add))
            step(dve.reciprocal(sp[:, 3], sp[:, 2]))
            step(tt(sp[:, 4], sp[:, 1], sp[:, 3], ALU.mult))
            step(tt(sp[:, 5], sp[:, 4], sp[:, 4], ALU.mult))
            step(ts(sp[:, 6], sp[:, 5], 1.0 / 17.0, None, ALU.mult))
            for odd in range(15, 1, -2):
                step(stt(sp[:, 6], sp[:, 6], 1.0 / odd, sp[:, 5], ALU.add, ALU.mult))
            step(stt(sp[:, 6], sp[:, 6], 1.0, sp[:, 4], ALU.add, ALU.mult))
            step(ts(sp[:, 2], fb, 0.0, -4.0, ALU.max, ALU.mult))
            step(stt(sp[:, 7], sp[:, 6], -8.0, sp[:, 2], ALU.mult, ALU.add))
            step(ts(sp[:, 1], V(V_BGATE, M), 0.5, None, ALU.mult))
            step(ts(sp[:, 3], V(V_BGATE + M, M), 0.5, None, ALU.mult))

            def emb(c):
                dve.wait_ge(S("emb_mm"), c + 1)
                for m in range(M):
                    tt(hi_[:, m, c * BH:(c + 1) * BH, 1:T],
                       bank[:, 2 * c + m, 0:NP].rearrange("p (b t) -> p b t", t=NPATCH),
                       posb[:, m, 1:T][:, None, :].to_broadcast([P, BH, NPATCH]), ALU.add)\
                        .then_inc(S("emb"), 1)

            emb(0)
            ln_xm(0, 0, h, 4)
            emb(1)
            ln_eps(0, 0, 6)
            ln_xm(0, 1, h, 5)
            ln_n(0, 0, 6)
            ln_eps(0, 1, 7)
            ln_n(0, 1, 7)

            def gate(c):
                dve.wait_ge(S("g_mm"), c + 1)
                dve.tensor_copy(half(silu_g, c), pair(2)).then_inc(S("g_chan"), 1)

            def prep(c):
                dve.wait_ge(S(f"head{c}0"), 16)
                dve.wait_ge(S(f"head{c}1"), 16)
                if c:
                    dve.wait_ge(S("ssq"), c)
                step(tt(hsq[:, :], head[:, c, 0:2], head[:, c, 0:2], ALU.mult))
                step(dve.tensor_reduce(ssq[:, c], hsq[:, :].rearrange("p x i t -> p x t i"), AX_X, ALU.add))
                ts(ssq[:, c], ssq[:, c], 1e-24, None, ALU.max).then_inc(S("ssq"), 1)

            def prep_b(c):
                dve.wait_ge(S("nrm"), c + 1)
                step(dve.reciprocal(rnrm[:, c], nrm[:, c]))
                tt(head[:, c, 0:2], head[:, c, 0:2],
                   rnrm[:, c][:, :, None, :].to_broadcast([P, 2, HD, T]), ALU.mult).then_inc(S("khat"), 1)
                dve.wait_ge(S("khat"), c + 1)
                dve.wait_ge(S("head_beta"), c + 1)
                tt(bk[:, c], head[:, c, 0], head_b[:, c][:, None, :].to_broadcast([P, HD, T]), ALU.mult)\
                    .then_inc(S("bk"), 1)

            def outer(c, I):
                dve.wait_ge(S("bk"), c + 1)
                if c:
                    dve.wait_ge(S("decay_mirror"), NI - 1)
                nj = HD - I * IB
                tt(decay[:, I * IB:(I + 1) * IB, I * IB:HD, 1:T],
                   bk[:, c, I * IB:(I + 1) * IB, 1:T][:, :, None, :].to_broadcast([P, IB, nj, T - 1]),
                   head[:, c, 0, I * IB:HD, 1:T][:, None, :, :].to_broadcast([P, IB, nj, T - 1]), ALU.mult)\
                    .then_inc(S("kk"), 1)

            def scan(c, I):
                s = c * NI + I
                dve.wait_ge(S("write"), s + 1)
                dve.wait_ge(S("decay"), s + 1)
                if c * (NI - 1) + I:
                    dve.wait_ge(S("decay_mirror"), c * (NI - 1) + I)
                if s >= 2:
                    dve.wait_ge(S("att_part"), s - 1)
                dve.tensor_tensor_scan(
                    state[:, s % 2].rearrange("p i j t -> p (i j t)"),
                    decay[:, I * IB:(I + 1) * IB].rearrange("p i j t -> p (i j t)"),
                    write[:, s % 3].rearrange("p i j t -> p (i j t)"),
                    0.0, ALU.mult, ALU.add).then_inc(S("state"), 1)

            def query(c, I):
                s = c * NI + I
                dve.wait_ge(S("state"), s + 1)
                tt(state[:, s % 2], state[:, s % 2],
                   head[:, c, 1][:, None, :, :].to_broadcast([P, IB, HD, T]), ALU.mult)\
                    .then_inc(S("read"), 1)

            def attn_norm(c):
                ln_n(1, c, 6 + c)
                dve.wait_ge(S(f"ln_n{c}"), 2)
                tt(half(n, c), half(n, c), half(gate_b, c), ALU.add).then_inc(S("gated"), 1)

            def attn_scale(c):
                dve.wait_ge(S("gate_ln"), 2 * M * (c + 1))
                dve.wait_ge(S(f"ln_sq{c}"), 2)
                step(tt(half(xm, c), half(xm, c), half(silu_g, c), ALU.mult))

            def residual(name, mm, c, b0):
                dve.wait_ge(S(mm), c + 1)
                tt(half(h, c), half(h, c), pair(b0), ALU.add).then_inc(S(name), 1)

            dve.wait_ge(S("y_zeroed"), 16)
            gate(0)
            prep(0)
            prep_b(0)
            gate(1)
            for I in range(NI):
                outer(0, I)
            prep(1)
            scan(0, 0)
            query(0, 0)
            prep_b(1)
            outer(1, 0)
            for I in range(1, NI):
                scan(0, I)
                query(0, I)
                outer(1, I)
            for I in range(2):
                scan(1, I)
                query(1, I)
            scan(1, 2)
            query(1, 2)
            ln_xm(1, 0, och, 4)
            scan(1, 3)
            query(1, 3)
            dve.wait_ge(S("read"), 2 * NI)
            o = state[:, 1, :, 0:FOLD]
            tt(o, o, state[:, 1, :, HD - FOLD:HD], ALU.add).then_inc(S("last_fold"), 1)
            ln_eps(1, 0, 6)
            attn_scale(0)
            attn_norm(0)
            residual("h1", "wo_mm", 0, 0)
            ln_xm(2, 0, h, 4)
            ln_xm(1, 1, och, 5)
            ln_eps(2, 0, 6)
            ln_eps(1, 1, 7)
            ln_n(2, 0, 6)
            attn_scale(1)
            attn_norm(1)
            residual("h1", "wo_mm", 1, 2)
            ln_xm(2, 1, h, 5)
            ln_eps(2, 1, 7)
            ln_n(2, 1, 7)

            lg = bank[:, 6, 0:NR * E].rearrange("p (r e) -> p r e", e=E)
            rank = vec[:, V_RANK:V_RANK + E][:, None, :].to_broadcast([P, NR, E])
            valid = vec[:, V_VALID:V_VALID + NR]

            def bc(k):
                return r_s[:, k][:, :, None].to_broadcast([P, NR, E])

            def by_tile(x):
                return x.rearrange("p e r -> p r e")

            dve.wait_ge(S("router_mm"), 1)
            step(dve.tensor_reduce(r_s[:, 0], lg, AX_X, ALU.max))
            tt(r_t[:, 0], lg, bc(0), ALU.subtract).then_inc(S("r_diff"), 1)
            dve.wait_ge(S("r_exp"), 1)
            step(dve.tensor_reduce(r_s[:, 1], r_t[:, 1], AX_X, ALU.add))
            step(dve.reciprocal(r_s[:, 2], r_s[:, 1]))
            step(tt(r_t[:, 2], r_t[:, 1], bc(2), ALU.mult))
            step(dve.tensor_reduce(r_s[:, 3], r_t[:, 2], AX_X, ALU.max))
            step(tt(r_t[:, 3], r_t[:, 2], bc(3), ALU.is_equal))
            step(tt(r_t[:, 3], r_t[:, 3], rank, ALU.mult))
            step(dve.tensor_reduce(r_s[:, 8], r_t[:, 3], AX_X, ALU.max))
            step(tt(r_t[:, 4], rank, bc(8), ALU.is_equal))
            step(stt(r_t[:, 5], r_t[:, 4], -TOPK_STEP, r_t[:, 2], ALU.mult, ALU.add))
            step(dve.tensor_reduce(r_s[:, 4], r_t[:, 5], AX_X, ALU.max))
            tt(r_s[:, 5], r_s[:, 4], r_s[:, 3], ALU.subtract).then_inc(S("r_gap"), 1)
            step(tt(r_t[:, 6], r_t[:, 5], bc(4), ALU.is_equal))
            step(tt(r_t[:, 6], r_t[:, 6], rank, ALU.mult))
            step(dve.tensor_reduce(r_s[:, 9], r_t[:, 6], AX_X, ALU.max))
            step(tt(r_t[:, 7], rank, bc(9), ALU.is_equal))
            step(tt(r_t[:, 8], r_t[:, 4], r_t[:, 7], ALU.add))
            tt(by_tile(c_t[:, 0]), r_t[:, 8], valid[:, :, None].to_broadcast([P, NR, E]), ALU.mult)\
                .then_inc(S("chosen"), 1)
            for j in range(2):
                dve.wait_ge(S("tok_hi"), j + 1)
                if j == 0:
                    tt(tok_lo[:, 0:4].rearrange("p (b r) c -> p b (r c)", b=2), bank[:, 0:2, :],
                       tok_hi[:, 0:4].bitcast(F32).rearrange("p (b r) c -> p b (r c)", b=2), ALU.subtract)\
                        .then_inc(S("tok_lo"), 1)
                else:
                    tt(tok_lo[:, 4], bank[:, 2, 0:D], tok_hi[:, 4].bitcast(F32), ALU.subtract)\
                        .then_inc(S("tok_lo"), 1)
            dve.wait_ge(S("count_mm"), 1)
            in_tile = bank[:, 6, 64:64 + E * NR].rearrange("p (e r) -> p e r", r=NR)
            of_tile = bank[:, 6, 128:128 + E * NR]
            reset = vec[:, V_RESET:V_RESET + E * NR]

            def flat(x):
                return x.rearrange("p e r -> p (e r)")

            step(dve.tensor_tensor_scan(flat(c_t[:, 1]), reset, of_tile, 0.0, ALU.mult, ALU.add))
            step(tt(flat(c_t[:, 2]), flat(c_t[:, 1]), of_tile, ALU.subtract))
            step(tt(c_t[:, 3], c_t[:, 2], in_tile, ALU.add))
            step(stt(flat(c_t[:, 4]), flat(c_t[:, 3]), 1.0, flat(c_t[:, 0]), ALU.add, ALU.mult))
            step(ts(flat(c_t[:, 5]), flat(c_t[:, 4]), 1.0, None, ALU.subtract))

            iota = vec[:, V_IOTA:V_IOTA + SLOTS][:, None, :].to_broadcast([P, NR, SLOTS])

            def choose(t, slot):
                if not isinstance(t, int) or t >= 2:
                    dve.wait_ge(S("x_lo_mm"), t - 1)
                at_e = c_t[:, 5, t] if isinstance(t, int) else \
                    c_t[:, 5, bass.ds(t, 1)].rearrange("p a r -> p (a r)")
                tt(pick[:, slot], iota, at_e[:, :, None].to_broadcast([P, NR, SLOTS]), ALU.is_equal)\
                    .then_inc(S("pick"), 1)

            def x_low(t, slot):
                dve.wait_ge(S("x_lo_mm"), t + 1)
                dve.tensor_copy(x_lo[:, slot], bank[:, 1, 0:M * SLOTS].rearrange("p (m s) -> p m s", m=M))\
                   .then_inc(S("x_lo"), 1)

            choose(0, 0)
            choose(1, 1)
            x_low(0, 0)
            step(ts(c_s[:, 0], c_t[:, 1, :, NR - 1], float(SLOTS), None, ALU.is_gt))
            for k in range(2, OVE + 1):
                step(stt(c_s[:, 0], c_t[:, 1, :, NR - 1], float(k * SLOTS), c_s[:, 0], ALU.is_gt, ALU.add))
            step(dve.tensor_tensor_scan(c_s[:, 1], ones[:, 0:E], c_s[:, 0], 0.0, ALU.mult, ALU.add))
            step(tt(c_s[:, 2], c_s[:, 1], c_s[:, 0], ALU.subtract))
            step(stt(c_s[:, 3], c_s[:, 2], float(SLOTS), V(V_OVER, E), ALU.mult, ALU.add))
            step(stt(c_t[:, 6], c_t[:, 3], float(SLOTS), c_s[:, 3][:, :, None].to_broadcast([P, E, NR]),
                     ALU.is_ge, ALU.mult))
            step(tt(c_t[:, 7], c_t[:, 3], V(V_BASE, E)[:, :, None].to_broadcast([P, E, NR]), ALU.add))
            step(tt(c_t[:, 7], c_t[:, 7], c_t[:, 6], ALU.add))
            for j, hot in ((0, 4), (1, 7)):
                step(tt(r_t[:, 9 + j], r_t[:, hot], by_tile(c_t[:, 7]), ALU.mult))
                step(dve.tensor_reduce(rows[:, 2 + j], r_t[:, 9 + j], AX_X, ALU.add))
                step(tt(rows[:, j], rows[:, 2 + j], valid, ALU.mult))
            dve.tensor_copy(row_i[:, :], rows[:, 0:2]).then_inc(S("row_i"), 1)
            step(tt(e_f[:, :], c_s[0:1, 1][:, None, :].to_broadcast([1, OV, E]),
                    vec[0:1, V_IOTA:V_IOTA + OV][:, :, None].to_broadcast([1, OV, E]), ALU.is_le))
            step(dve.tensor_reduce(e_s[:, 0:OV], e_f[:, :], AX_X, ALU.add))
            step(ts(e_s[:, 0:OV], e_s[:, 0:OV], float(E - 1), None, ALU.min))
            step(dve.tensor_copy(e_s[:, OV:OV + 1], c_s[0:1, 1, E - 1:E]))
            dve.tensor_copy(e_tab[:, :], e_s[:, :]).then_inc(S("e_tab"), 1)
            dve.wait_ge(S("r_gexp"), 1)
            step(ts(r_s[:, 7], r_s[:, 6], 1.0, None, ALU.add))
            step(dve.reciprocal(r_s[:, 10], r_s[:, 7]))
            step(tt(r_s[:, 11], r_s[:, 6], r_s[:, 10], ALU.mult))
            step(ts(rows[:, 2:4], rows[:, 0:2], float(E * SLOTS), None, ALU.subtract))

            def gate_up(t, slot):
                dve.wait_ge(S("act_g"), t + 1)
                dve.wait_ge(S("front"), t + 1)
                tt(fuse[:, slot].rearrange("p (b f) s -> p b (f s)", b=2),
                   act_g[:, slot].rearrange("p (b f) s -> p b (f s)", b=2),
                   bank[:, 4:6, 0:2 * SLOTS], ALU.mult).then_inc(S("fuse"), 1)
                dve.wait_ge(S("f_hi"), t + 1)
                tt(f_lo[:, slot], fuse[:, slot], f_hi[:, slot].bitcast(F32), ALU.subtract)\
                    .then_inc(S("f_lo"), 1)

            def results(t, slot, stored):
                dve.wait_ge(S("back"), t + 1)
                dve.wait_ge(S(f"y_stored{slot}"), stored)
                dve.tensor_copy(y_sb[:, slot],
                                bank[0:GR, 6 + slot, :].rearrange("p (g c) -> p g c", g=2))\
                   .then_inc(S("y_out"), 1)

            gate_up(0, 0)
            x_low(1, 1)
            with dve.Fori(0, E // 2 - 1) as i:
                for slot in range(2):
                    t = i * 2 + slot
                    choose(t + 2, slot)
                    gate_up(t + 1, 1 - slot)
                    x_low(t + 2, slot)
                    results(t, slot, i * 16 + 16)
            gate_up(E - 1, 1)
            for slot in range(2):
                results(E - 2 + slot, slot, 16 * (E // 2))
            n_over = dve.value_load(e_tab[0:1, OV:OV + 1], min_val=0, max_val=OV)
            with dve.If(n_over > 0):
                with dve.Fori(0, n_over) as o:
                    dve.wait_ge(S("back"), o + E)
                    for j in range(2):
                        dst = (pick_a, pick_b)[j]
                        tt(dst[:, :], iota, rows[:, 2 + j][:, :, None].to_broadcast([P, NR, SLOTS]),
                           ALU.is_equal).then_inc(S("pick_ab"), 1)
                    dve.wait_ge(S("pick_ab"), o * 2 + 2)
                    tt(pick[:, 0], pick_a[:, :], pick_b[:, :], ALU.add).then_inc(S("pick"), 1)
                    ts(rows[:, 2:4], rows[:, 2:4], float(SLOTS), None, ALU.subtract).then_inc(S("rows"), 1)
                    dve.wait_ge(S("rows"), o + 1)
                    x_low(o + E, 0)
                    gate_up(o + E, 0)
                    results(o + E, 0, o * 16 + 16 * (E // 2 + 1))
            for r in range(NR):
                dve.wait_ge(S(f"y_tok{r}"), 32)
                step(ts(y_w[:, r], y_tok[:, r, 0], r_s[:, 10, r:r + 1], None, ALU.mult))
                stt(y_sum[:, r], y_tok[:, r, 1], r_s[:, 11, r:r + 1], y_w[:, r], ALU.mult, ALU.add)\
                    .then_inc(S("y_sum"), 1)
            for b, lo, hi, tiles in ((0, 0, NRT0 * P, NRT0), (M, NRT0 * P, B * T, NR)):
                dve.wait_ge(S("y_turned"), tiles)
                tt(h[:, :, lo:hi], h[:, :, lo:hi], bank[:, b:b + M, 0:hi - lo], ALU.add).then_inc(S("h2"), 1)

            for c in range(HALF):
                ln_xm(3, c, h, 4 + c)
            for c in range(HALF):
                ln_eps(3, c, 6 + c)
            for c in range(HALF):
                ln_n(3, c, 6 + c)

            def im(t):
                return t.rearrange("p (b t) -> p b t", t=T)

            for c in range(HALF):
                for s in range(CONV):
                    for m in range(M):
                        base = V_CONV + m * CONV
                        if s == 0:
                            dve.wait_ge(S("conv0"), c * M + m + 1)
                            continue
                        if s > 1:
                            dve.wait_ge(S("conv"), (c * (CONV - 1) + s - 2) * M + m + 1)
                        stt(im(xc[:, c, m])[:, :, s:T], im(bank[:, 4 * c + m, 0:NT])[:, :, 0:T - s],
                            V(base + CONV - 1 - s), im(xc[:, c, m])[:, :, s:T], ALU.mult, ALU.add)\
                            .then_inc(S("conv"), 1)
            for c in range(HALF):
                dve.wait_ge(S("alpha"), M * (c + 1))
                step(tt(asq[:, c], alpha[:, c], alpha[:, c], ALU.mult))
                ts(asq[:, c], asq[:, c], -1.0, 1.0, ALU.mult, ALU.add).then_inc(S("one_minus"), 1)
                step(dve.memset(alpha[:, c].rearrange("p m (b t) -> p (m b) t", t=T)[:, :, 0:1], 0.0))
                dve.wait_ge(S("sig_i"), M * (c + 1))
                step(stt(upd[:, c], sig_i[:, c], 1.0, xc[:, c], ALU.add, ALU.mult))
            for c in range(HALF):
                dve.wait_ge(S("beta"), c + 1)
                step(stt(upd[:, c], upd[:, c], 0.5, beta[:, c], ALU.mult, ALU.mult))
                step(dve.tensor_tensor_scan(hst[:, c].rearrange("p m n -> p (m n)"),
                                            alpha[:, c].rearrange("p m n -> p (m n)"),
                                            upd[:, c].rearrange("p m n -> p (m n)"),
                                            0.0, ALU.mult, ALU.add))
                dve.wait_ge(S("gelu_g"), c + 1)
                tt(hst[:, c], hst[:, c], gelu_g[:, c], ALU.mult).then_inc(S("hawk_y"), 1)
            for c in range(HALF):
                residual("h3", "hawk_mm", c, 4 * c)
            for c in range(HALF):
                ln_xm(4, c, h, 4 * c + 2)
            for c in range(HALF):
                ln_eps(4, c, 4 * c + 3)
            for c in range(HALF):
                ln_n(4, c, 4 * c + 3)
                dve.wait_ge(S(f"ln_n{c}"), 5)
                step(dve.tensor_reduce(amax[:, c:c + 1], half(n, c), mybir.AxisListType.XY, ALU.max,
                                       apply_absolute_value=True))
            tt(amax[:, 2:3], amax[:, 0:1], amax[:, 1:2], ALU.max).then_inc(S("amax"), 1)
            dve.wait_ge(S("amax_all"), 1)
            step(ts(amax[:, 4:5], amax[:, 3:4], 1.0 / 127.0, EPS, ALU.mult, ALU.max))
            step(dve.reciprocal(amax[:, 5:6], amax[:, 4:5]))
            ts(amax[:, 6:6 + M], V(V_WSCALE, M), amax[:, 4:5], None, ALU.mult).then_inc(S("out_scale"), 1)
            for c in range(HALF):
                step(ts(q1[:, c], half(n, c), amax[:, 5:6], 127.0, ALU.mult, ALU.min))
                step(ts(q2[:, c], q1[:, c], -128.0, ROUND, ALU.max, ALU.add))
                ts(qx[:, c], q2[:, c], ROUND, None, ALU.subtract).then_inc(S("qx"), 1)
            for c in range(HALF):
                for m in range(M):
                    dve.wait_ge(S("y1"), M * c + m + 1)
                    tt(y[:, c, m], y1[:, c, m], half(h, c)[:, m], ALU.add).then_inc(S("y"), 1)

        @block.tensor
        def _(pe):
            def mm(o, w, x, start, stop):
                return pe.matmul(o, w, x, start=start, stop=stop)

            def keep_warm(b, count):
                for _ in range(count):
                    mm(bank[:, b, 0:P], ident[:, :], ident[:, :], True, True)

            def linear(o, w, x, kt):
                for k in range(kt):
                    r = mm(o, w(k), x(k), k == 0, k == kt - 1)
                return r

            def ln_mean(L, c, src, mb):
                linear(bank[:, mb, 0:NT], lambda k: mean_w[:, :], lambda k: half(src, c)[:, k], M)\
                    .then_inc(S(f"ln_mean{c}"), 1)

            def ln_var(L, c, vb):
                pe.wait_ge(S(f"ln_sq{c}"), L + 1)
                for q in range(NRH):
                    o = c * NT + q * RT
                    r = linear(bank[0:RT, vb, q:q + 1], lambda k: xsq[:, k, o:o + RT],
                               lambda k: mean_w[:, 0:1], M)
                r.then_inc(S(f"ln_var{c}"), 1)

            def ln_spread(L, c, vb):
                pe.wait_ge(S(f"ln_rstd{c}"), L + 1)
                for q in range(NRH):
                    r = mm(bank[:, vb, SPREAD + q * RT:SPREAD + (q + 1) * RT],
                           rstd[:, c, q:q + 1].to_broadcast([RT, P]), ident[0:RT, 0:RT], True, True)
                r.then_inc(S(f"ln_bc{c}"), 1)

            def project(w, m0, c, b0, src=n):
                for m in range(M):
                    r = linear(bank[:, b0 + m, 0:NT], lambda k: w[:, k, m0 + m * P:m0 + (m + 1) * P],
                               lambda k: half(src, c)[:, k], M)
                return r

            def embed(c, m):
                if m == 0 and c:
                    pe.wait_ge(S("xp1_in"), 16)
                for k in range(KE):
                    if c == 0 and m == 0 and k % (KE // 2) == 0:
                        pe.wait_ge(S(f"emb_in{k // (KE // 2)}"), 32)
                    r = mm(bank[:, 2 * c + m, 0:NP], wl[:, k, m * P:(m + 1) * P], xp[:, c, k],
                           k == 0, k == KE - 1)
                return r

            pe.wait_ge(S("ident"), 1)
            keep_warm(7, WARM_START)
            embed(0, 0)
            embed(0, 1).then_inc(S("emb_mm"), 1)
            embed(1, 0)
            pe.wait_ge(S("mean_w"), 1)
            pe.wait_ge(S("cls"), 1)
            pe.wait_ge(S("emb"), M)
            ln_mean(0, 0, h, 4)
            embed(1, 1).then_inc(S("emb_mm"), 1)
            ln_var(0, 0, 6)
            pe.wait_ge(S("emb"), M * HALF)
            ln_mean(0, 1, h, 5)
            pe.wait_ge(S("ident"), 1)
            ln_spread(0, 0, 6)
            pe.wait_ge(S("wq_in"), 16)
            pe.wait_ge(S("wb_in"), 16)
            ln_var(0, 1, 7)
            for c in range(HALF):
                pe.wait_ge(S(f"ln_n{c}"), 1)
                if c:
                    pe.wait_ge(S("v_chan"), c)
                project(wq, D, c, 0).then_inc(S("k_mm"), 1)
                if c == 0:
                    ln_spread(0, 1, 7)
                if c:
                    pe.wait_ge(S("g_chan"), c)
                project(wq, 0, c, 2).then_inc(S("q_mm"), 1)
                pe.wait_ge(S("k_chan"), c + 1)
                project(wq, 2 * D, c, 0).then_inc(S("v_mm"), 1)
                if c == 0:
                    pe.wait_ge(S("ln_n1"), 1)
                linear(bank[0:NH, 4 + c, 0:NT], lambda k: wb[:, k], lambda k: half(n, c)[:, k], M)\
                    .then_inc(S("b_mm"), 1)
                pe.wait_ge(S("q_chan"), c + 1)
                project(wq, 3 * D, c, 2).then_inc(S("g_mm"), 1)

            def att_sum(c, I):
                s = c * NI + I
                pe.wait_ge(S("state"), s + 1)
                keep_warm(7, WARM_ATT if s < 2 * NI - 1 else WARM_ATT_LAST)
                pe.wait_ge(S("read"), s + 1)
                o = bank[:, 2 * c + I // 2, (I % 2) * IB * T:(I % 2 + 1) * IB * T]\
                    .rearrange("p (i t) -> p i t", t=T)
                for j in range(FOLD, HD - FOLD):
                    mm(o, ident[:, :], state[:, s % 2, :, j], j == FOLD, False)
                if s < 2 * NI - 1:
                    pe.wait_ge(S("fold"), s + 1)
                else:
                    pe.wait_ge(S("last_fold"), 1)
                for j in range(FOLD):
                    r = mm(o, ident[:, :], state[:, s % 2, :, j], False, j == FOLD - 1)
                r.then_inc(S("att_part"), 1)

            def router(r_):
                return linear(bank[:, 6, r_ * E:(r_ + 1) * E],
                              lambda k: n[:, k, r_ * P:(r_ + 1) * P], lambda k: wr[:, k], M)

            def turn(r_):
                for m in range(M):
                    o = (r_ % 2) * D + m * P
                    r = pe.transpose(bank[:, r_ // 2, o:o + P], n[:, m, r_ * P:(r_ + 1) * P], ident[:, :])
                return r

            def out_proj(c):
                pe.wait_ge(S("gated"), c + 1)
                if c == 0:
                    pe.wait_ge(S("wo_in"), 16)
                project(wo, 0, c, 2 * c).then_inc(S("wo_mm"), 1)

            pe.wait_ge(S("ident"), 1)
            pe.wait_ge(S("v_chan"), HALF)
            for I in range(NI):
                att_sum(0, I)
            pe.wait_ge(S("g_chan"), HALF)
            pe.wait_ge(S("b_chan"), HALF)
            att_sum(1, 0)
            att_sum(1, 1)
            pe.wait_ge(S("och0"), 16 * M)
            ln_mean(1, 0, och, 4)
            att_sum(1, 2)
            ln_var(1, 0, 6)
            att_sum(1, 3)
            ln_spread(1, 0, 6)
            keep_warm(7, 5)
            out_proj(0)
            keep_warm(7, 3)
            pe.wait_ge(S("h1"), 1)
            ln_mean(2, 0, h, 4)
            pe.wait_ge(S("och1"), 16 * M)
            ln_mean(1, 1, och, 5)
            ln_var(2, 0, 6)
            ln_var(1, 1, 7)
            ln_spread(2, 0, 6)
            ln_spread(1, 1, 7)
            pe.wait_ge(S("wr_in"), 16)
            pe.wait_ge(S("n_pad"), 1)
            pe.wait_ge(S("ln_n0"), 3)
            router(0)
            router(1)
            keep_warm(4, WARM_OUT)
            out_proj(1)
            turn(0)
            pe.wait_ge(S("h1"), 2)
            ln_mean(2, 1, h, 5)
            turn(1)
            keep_warm(4, 3)
            ln_var(2, 1, 7)
            keep_warm(4, 6)
            ln_spread(2, 1, 7)
            keep_warm(4, 3)
            pe.wait_ge(S("ln_n1"), 3)
            for r_ in range(2, NR):
                r = router(r_)
            r.then_inc(S("router_mm"), 1)
            for r_ in range(2, NR):
                r = turn(r_)
            r.then_inc(S("tok_mm"), 1)
            keep_warm(4, WARM_ROUTE)
            pe.wait_ge(S("before"), 1)
            pe.wait_ge(S("chosen"), 1)
            chosen = c_t[:, 0].rearrange("p e r -> p (e r)")
            mm(bank[:, 6, 64:64 + E * NR], before[:, :], chosen, True, True)
            mm(bank[:, 6, 128:128 + E * NR], ones[:, :], chosen, True, True).then_inc(S("count_mm"), 1)
            keep_warm(5, WARM_PLACE)
            pe.nop().then_inc(S("y_out"), 2)

            def gather(t, slot):
                pe.wait_ge(S("pick"), t + 1)
                for part, src, b in (("x_hi", tok_hi, 0), ("x_lo", tok_lo, 1)):
                    if not (isinstance(t, int) and t == 0):
                        pe.wait_ge(S(part), t)
                    for m in range(M):
                        for r_ in range(NR):
                            r = mm(bank[:, b, m * SLOTS:(m + 1) * SLOTS], src[:, r_, m * P:(m + 1) * P],
                                   pick[:, slot, r_], r_ == 0, r_ == NR - 1)
                    r.then_inc(S(part + "_mm"), 1)

            def three(o, w, x, start, stop):
                mm(o, w[0], x[0], start, False)
                mm(o, w[0], x[1], False, False)
                return mm(o, w[1], x[0], False, stop)

            def front(t, slot):
                pe.wait_ge(S("x_hi"), t + 1)
                pe.wait_ge(S("x_lo"), t + 1)
                first = isinstance(t, int) and t == 0
                for what, b0, done in ((0, 2, "act_g"), (1, 4, "fuse")):
                    if not first:
                        pe.wait_ge(S(done), t)
                    for f in range(FCH):
                        if what == 0:
                            pe.wait_ge(S("w_split"), t * PIECES + (f + 1))
                        for k in range(M):
                            o = (what * M + k) * P
                            r = three(bank[:, b0 + f // 2, (f % 2) * SLOTS:(f % 2 + 1) * SLOTS],
                                      (w_hi[:, slot, f, o:o + P], w_lo[:, slot, f, o:o + P]),
                                      (x_hi[:, slot, k], x_lo[:, slot, k]), k == 0, k == M - 1)
                    r.then_inc(S("front" if what else "gate_mm"), 1)

            def back(t, slot, left):
                pe.wait_ge(S("f_lo"), t + 1)
                pe.wait_ge(S("w_split"), t * PIECES + PIECES)
                pe.wait_ge(S("y_out"), left)
                for g in range(2):
                    for f in range(FCH):
                        p, o = GU + f // 2, (f % 2) * D
                        r = three(bank[0:GR, 6 + slot, g * D:(g + 1) * D],
                                  (f_hi[:, slot, f, g * GR:(g + 1) * GR], f_lo[:, slot, f, g * GR:(g + 1) * GR]),
                                  (w_hi[:, slot, p, o:o + D], w_lo[:, slot, p, o:o + D]), f == 0, f == FCH - 1)
                r.then_inc(S("back"), 1)

            pe.wait_ge(S("tok_lo"), 2)
            gather(0, 0)
            front(0, 0)
            gather(1, 1)
            with pe.Fori(0, E // 2 - 1) as i:
                for slot in range(2):
                    t = i * 2 + slot
                    front(t + 1, 1 - slot)
                    gather(t + 2, slot)
                    back(t, slot, t + 1)
            front(E - 1, 1)
            back(E - 2, 0, E - 1)
            back(E - 1, 1, E)
            pe.wait_ge(S("e_tab"), 1)
            n_over = pe.value_load(e_tab[0:1, OV:OV + 1], min_val=0, max_val=OV)
            with pe.If(n_over > 0):
                with pe.Fori(0, n_over) as o:
                    gather(o + E, 0)
                    front(o + E, 0)
                    back(o + E, 0, o + E + 2)
            for r_ in range(NR):
                pe.wait_ge(S("y_sum"), r_ + 1)
                rows_ = min(P, B * T - r_ * P)
                for m in range(M):
                    b, o = m + M * (r_ // NRT0), (r_ % NRT0) * P
                    r = pe.transpose(bank[:, b, o:o + rows_],
                                     y_sum[0:rows_, r_, m * P:(m + 1) * P], ident[0:rows_, 0:rows_])
                r.then_inc(S("y_turned"), 1)
                if r_ < NR - 1:
                    keep_warm(5, WARM_RESULT)

            for c in range(HALF):
                pe.wait_ge(S("h2"), c + 1)
                ln_mean(3, c, h, 4 + c)
            keep_warm(0, WARM_NORM)
            for c in range(HALF):
                ln_var(3, c, 6 + c)
            keep_warm(0, WARM_NORM)
            for c in range(HALF):
                ln_spread(3, c, 6 + c)
            pe.wait_ge(S("hawk_w_in"), 16 * 3)
            for c in range(HALF):
                pe.wait_ge(S(f"ln_n{c}"), 4)
                project(wi, D, c, 4 * c).then_inc(S("hx_mm"), 1)
                project(wi, 0, c, 4 * c + 2).then_inc(S("hgate_mm"), 1)
            for c in range(HALF):
                pe.wait_ge(S("conv"), (CONV - 1) * M * (c + 1))
                for m in range(M):
                    r = linear(bank[:, 4 * c + m, 0:NT], lambda k: wg[:, k, m * P:(m + 1) * P],
                               lambda k: xc[:, c, k], M)
                r.then_inc(S("forget_mm"), 1)
                pe.wait_ge(S("gelu_g"), c + 1)
                for m in range(M):
                    r = linear(bank[:, 4 * c + 2 + m, 0:NT], lambda k: wg[:, k, D + m * P:D + (m + 1) * P],
                               lambda k: xc[:, c, k], M)
                r.then_inc(S("input_mm"), 1)
            pe.wait_ge(S("one_minus"), 2)
            keep_warm(0, WARM_HAWK)
            for c in range(HALF):
                pe.wait_ge(S("hawk_y"), c + 1)
                for m in range(M):
                    r = linear(bank[:, 4 * c + m, 0:NT], lambda k: wh[:, k, m * P:(m + 1) * P],
                               lambda k: hst[:, c, k], M)
                r.then_inc(S("hawk_mm"), 1)
            for c in range(HALF):
                pe.wait_ge(S("h3"), c + 1)
                ln_mean(4, c, h, 4 * c + 2)
            for c in range(HALF):
                ln_var(4, c, 4 * c + 3)
            keep_warm(0, 3)
            for c in range(HALF):
                ln_spread(4, c, 4 * c + 3)
            keep_warm(0, WARM_INT)
            pe.wait_ge(S("w8b"), 1)
            for c in range(HALF):
                pe.wait_ge(S("qx"), c + 1)
                for m in range(M):
                    r = linear(bank[:, 2 * c + m, 0:NT], lambda k: w8b[:, k, m * P:(m + 1) * P],
                               lambda k: qx[:, c, k], M)
                r.then_inc(S("int_mm"), 1)


def _tiles(a):
    k, n = a.shape
    return a.reshape(k // 128, 128, n).transpose(1, 0, 2)


def kernel(**inputs):
    import numpy as np
    import concourse.bacc as bacc
    from concourse.bass_utils import run_bass_kernel_spmd

    a = {k: np.asarray(v) for k, v in inputs.items()}
    g = IMG // PATCH
    x = a["x"].reshape(HALF, BH, CIN, g, PATCH, g, PATCH).transpose(0, 2, 4, 6, 1, 3, 5)
    x = x.reshape(HALF, KE, P, NP).transpose(0, 2, 1, 3)

    def cols(v):
        return v.reshape(-1, P).T

    pos = a["L0_tok_position_embeddings"][0].reshape(T, M, P).transpose(2, 1, 0).reshape(P, M * T)
    conv = a["L1_attn_w_conv"].reshape(M, P, CONV).transpose(1, 0, 2).reshape(P, M * CONV)
    def every(v):
        return np.broadcast_to(np.asarray(v, np.float32), (P, len(v)))

    rank = every(np.arange(E, 0, -1))
    valid = (np.arange(TP) < B * T).astype(np.float32).reshape(NR, P).T
    reset = every(np.arange(E * NR) % NR != 0)
    base = every(np.arange(E) * SLOTS)
    over = every((E - 1 - np.arange(E)) * SLOTS)
    iota = every(np.arange(SLOTS))
    vecs = np.concatenate([
        cols(a["L0_tok_b_lin"]), cols(a["L0_tok_class_token"].reshape(D)), pos,
        cols(a["L0_attn_ln_g"]), cols(a["L0_attn_ln_b"]), conv, cols(a["L1_attn_b_conv"]),
        cols(a["L1_attn_b_gates"]), cols(a["L1_attn_forget_base"]),
        cols(a["L1_ffn_weight_scale"].reshape(D)), cols(a["L1_ffn_bias"]), rank, valid,
        reset, base, over, iota], axis=1)

    def up(w):
        return w.reshape(E, M, P, FCH, P).transpose(0, 2, 3, 1, 4).reshape(E, P, FCH, M * P)

    dn = a["L0_ffn_kernel_down_EFD"].reshape(E, FCH, P, D).transpose(0, 2, 1, 3)
    experts = np.concatenate([
        np.concatenate([up(a["L0_ffn_kernel_gating_EDF"]), up(a["L0_ffn_kernel_up_EDF"])], axis=3),
        dn.reshape(E, P, PIECES - GU, PW)], axis=2)
    arrays = {
        "patches": x,
        "w_lin": _tiles(a["L0_tok_W_lin"].T),
        "vecs": vecs,
        "w_qkvg": _tiles(np.concatenate([a["L0_attn_Wq"], a["L0_attn_Wk"], a["L0_attn_Wv"],
                                         a["L0_attn_Wg"]], axis=1)),
        "w_beta": _tiles(a["L0_attn_Wbeta"]),
        "w_attn_out": _tiles(a["L0_attn_Wout"]),
        "w_router": _tiles(a["L0_ffn_router_kernel_DE"]),
        "w_experts": experts,
        "w_in": _tiles(a["L1_attn_w_in"].T),
        "w_gates": _tiles(a["L1_attn_w_gates"].T),
        "w_hawk_out": _tiles(a["L1_attn_w_out"].T),
        "w_int8": np.ascontiguousarray(_tiles(a["L1_ffn_weight_int8"].T)).view(np.int32),
    }
    nc = bacc.Bacc("TRN2", target_bir_lowering=False, num_devices=1)
    args = []
    for name in arrays:
        arrays[name] = np.ascontiguousarray(arrays[name])
        args.append(nc.dram_tensor(name, arrays[name].shape, mybir.dt.from_np(arrays[name].dtype),
                                   kind="ExternalInput").ap())
    args.append(nc.dram_tensor("out", (P, M, B * T), F32, kind="ExternalOutput").ap())
    vit_tower(nc, *args)
    r = run_bass_kernel_spmd(nc, [arrays], core_ids=[0])
    o = r.results[0]["out"]
    return o.transpose(2, 1, 0).reshape(B, T, D)
```
